# Optimizing a Trainium2 kernel written in Bass

```python
import numpy as np
import jax
import jax.numpy as jnp

def _softmax(x, axis=-1):
    return jax.nn.softmax(x, axis=axis)

def _gelu(x):
    return jax.nn.gelu(x, approximate=True)

def _silu(x):
    return jax.nn.silu(x)

def _sigmoid(x):
    return jax.nn.sigmoid(x)

def _layernorm(x, axis=-1, eps=1e-05):
    m = jnp.mean(x, axis=axis, keepdims=True)
    v = jnp.var(x, axis=axis, keepdims=True)
    return (x - m) / jnp.sqrt(v + eps)

def _scatter_add(tgt, idx, src, axis=0):
    return tgt.at[idx].add(src)

def _segment_sum(src, seg, n):
    return jax.ops.segment_sum(src, seg, n)
kernel_name = 'mk_macaron_d1_jaxref_r4_291074'

def setup_inputs(seed: int=0):
    np.random.seed(seed)
    _w = jnp.asarray

    def _L0_attn_setup():
        import jax, jax.numpy as jnp
        from jax import lax
        import numpy as np
        B, L, D_MODEL = (1, 256, 512)
        H, P, G, S = (32, 64, 8, 32)
        D_SSM = H * P
        CONV_DIM = D_SSM + 2 * G * S
        PROJ_DIM = 2 * D_SSM + 2 * G * S + H
        K = 4
        EPS = 1e-05

        def _forward(hidden_states, W_in, b_in, conv_w, conv_b, A_log, D_param, dt_bias, norm_w, W_out, b_out, mup_vector):
            Bb, Ll, _ = hidden_states.shape
            zxbcdt = (hidden_states @ W_in + b_in) * mup_vector
            z = zxbcdt[..., :D_SSM]
            xBC = zxbcdt[..., D_SSM:D_SSM + CONV_DIM]
            dt = zxbcdt[..., D_SSM + CONV_DIM:]
            xBC_t = jnp.transpose(xBC, (0, 2, 1))
            conv = lax.conv_general_dilated(xBC_t, conv_w[:, None, :], (1,), [(K - 1, 0)], dimension_numbers=('NCH', 'OIH', 'NCH'), feature_group_count=CONV_DIM)
            xBC = jnp.transpose(jax.nn.silu(conv + conv_b[None, :, None]), (0, 2, 1))
            x = xBC[..., :D_SSM].reshape(Bb, Ll, H, P)
            Bm = xBC[..., D_SSM:D_SSM + G * S].reshape(Bb, Ll, G, S)
            Cm = xBC[..., D_SSM + G * S:].reshape(Bb, Ll, G, S)
            rep = H // G
            Bh = jnp.repeat(Bm, rep, axis=2)
            Ch = jnp.repeat(Cm, rep, axis=2)
            dt = jax.nn.softplus(dt + dt_bias)
            a = jnp.exp(dt * -jnp.exp(A_log))
            db = dt[..., None, None] * x[..., None] * Bh[:, :, :, None, :]

            def combine(e1, e2):
                a1, s1 = e1
                a2, s2 = e2
                return (a1 * a2, a2[..., None, None] * s1 + s2)
            states = lax.associative_scan(combine, (a, db), axis=1)[1]
            y = jnp.einsum('blhps,blhs->blhp', states, Ch) + D_param[None, None, :, None] * x
            y = y.reshape(Bb, Ll, D_SSM) * jax.nn.silu(z)
            yg = y.reshape(Bb, Ll, G, D_SSM // G)
            var = jnp.mean(yg * yg, axis=-1, keepdims=True)
            y = (yg * lax.rsqrt(var + EPS)).reshape(Bb, Ll, D_SSM) * norm_w
            return y @ W_out + b_out
        key = jax.random.key(seed)
        ks = jax.random.split(key, 12)
        mults = np.array([0.9, 1.1, 0.8, 1.2, 1.0], dtype=np.float32)
        mv = np.ones(PROJ_DIM, dtype=np.float32)
        mv[:D_SSM] *= mults[0]
        mv[D_SSM:2 * D_SSM] *= mults[1]
        mv[2 * D_SSM:2 * D_SSM + G * S] *= mults[2]
        mv[2 * D_SSM + G * S:2 * D_SSM + 2 * G * S] *= mults[3]
        mv[2 * D_SSM + 2 * G * S:] *= mults[4]
        return {'hidden_states': jax.random.normal(ks[0], (B, L, D_MODEL), jnp.float32), 'W_in': jax.random.normal(ks[1], (D_MODEL, PROJ_DIM), jnp.float32) * 0.02, 'b_in': jax.random.normal(ks[2], (PROJ_DIM,), jnp.float32) * 0.01, 'conv_w': jax.random.normal(ks[3], (CONV_DIM, K), jnp.float32) * 0.2, 'conv_b': jax.random.normal(ks[4], (CONV_DIM,), jnp.float32) * 0.01, 'A_log': jnp.log(jax.random.uniform(ks[5], (H,), jnp.float32, 1.0, 16.0)), 'D_param': jax.random.normal(ks[6], (H,), jnp.float32) * 0.5 + 1.0, 'dt_bias': jax.random.normal(ks[7], (H,), jnp.float32) * 0.5, 'norm_w': jnp.ones((D_SSM,), jnp.float32) + 0.01 * jax.random.normal(ks[8], (D_SSM,), jnp.float32), 'W_out': jax.random.normal(ks[9], (D_SSM, D_MODEL), jnp.float32) * 0.02, 'b_out': jnp.zeros((D_MODEL,), jnp.float32), 'mup_vector': jnp.asarray(mv)}
    _L0_attn_in = _L0_attn_setup()

    def _L0_ffn_setup():
        import jax, jax.numpy as jnp
        import numpy as np
        B, S, D, E, TOPK = (4, 512, 512, 8, 2)
        key = jax.random.key(seed)
        k1, k2, k3 = jax.random.split(key, 3)
        x = jax.random.normal(k1, (B, S, D), dtype=jnp.float32)
        gate_w = jax.random.normal(k2, (E, D), dtype=jnp.float32) * 0.02
        expert_w = jax.random.normal(k3, (E, D, D), dtype=jnp.float32) / np.sqrt(D)
        expert_b = jnp.zeros((E, D), dtype=jnp.float32)
        return {'x': x, 'gate_w': gate_w, 'expert_w': expert_w, 'expert_b': expert_b}
    _L0_ffn_in = _L0_ffn_setup()
    _d = {'L0_attn_hidden_states': _L0_attn_in['hidden_states'], 'L0_attn_W_in': _L0_attn_in['W_in'], 'L0_attn_b_in': _L0_attn_in['b_in'], 'L0_attn_conv_w': _L0_attn_in['conv_w'], 'L0_attn_conv_b': _L0_attn_in['conv_b'], 'L0_attn_A_log': _L0_attn_in['A_log'], 'L0_attn_D_param': _L0_attn_in['D_param'], 'L0_attn_dt_bias': _L0_attn_in['dt_bias'], 'L0_attn_norm_w': _L0_attn_in['norm_w'], 'L0_attn_W_out': _L0_attn_in['W_out'], 'L0_attn_b_out': _L0_attn_in['b_out'], 'L0_attn_mup_vector': _L0_attn_in['mup_vector'], 'L0_ffn_gate_w': _L0_ffn_in['gate_w'], 'L0_ffn_expert_w': _L0_ffn_in['expert_w'], 'L0_ffn_expert_b': _L0_ffn_in['expert_b']}
    _x0 = _d['L0_attn_hidden_states']
    _d['L0_attn_hidden_states'] = jax.random.normal(jax.random.fold_in(jax.random.key(seed), 1), (2, 1024, 512), dtype=_x0.dtype)
    del _x0
    return _d

def reference(L0_attn_hidden_states, L0_attn_W_in, L0_attn_b_in, L0_attn_conv_w, L0_attn_conv_b, L0_attn_A_log, L0_attn_D_param, L0_attn_dt_bias, L0_attn_norm_w, L0_attn_W_out, L0_attn_b_out, L0_attn_mup_vector, L0_ffn_gate_w, L0_ffn_expert_w, L0_ffn_expert_b):

    def _L0_attn_ref(hidden_states, W_in, b_in, conv_w, conv_b, A_log, D_param, dt_bias, norm_w, W_out, b_out, mup_vector):
        import jax, jax.numpy as jnp
        from jax import lax
        import numpy as np
        B, L, D_MODEL = (1, 256, 512)
        H, P, G, S = (32, 64, 8, 32)
        D_SSM = H * P
        CONV_DIM = D_SSM + 2 * G * S
        PROJ_DIM = 2 * D_SSM + 2 * G * S + H
        K = 4
        EPS = 1e-05

        def _forward(hidden_states, W_in, b_in, conv_w, conv_b, A_log, D_param, dt_bias, norm_w, W_out, b_out, mup_vector):
            Bb, Ll, _ = hidden_states.shape
            zxbcdt = (hidden_states @ W_in + b_in) * mup_vector
            z = zxbcdt[..., :D_SSM]
            xBC = zxbcdt[..., D_SSM:D_SSM + CONV_DIM]
            dt = zxbcdt[..., D_SSM + CONV_DIM:]
            xBC_t = jnp.transpose(xBC, (0, 2, 1))
            conv = lax.conv_general_dilated(xBC_t, conv_w[:, None, :], (1,), [(K - 1, 0)], dimension_numbers=('NCH', 'OIH', 'NCH'), feature_group_count=CONV_DIM)
            xBC = jnp.transpose(jax.nn.silu(conv + conv_b[None, :, None]), (0, 2, 1))
            x = xBC[..., :D_SSM].reshape(Bb, Ll, H, P)
            Bm = xBC[..., D_SSM:D_SSM + G * S].reshape(Bb, Ll, G, S)
            Cm = xBC[..., D_SSM + G * S:].reshape(Bb, Ll, G, S)
            rep = H // G
            Bh = jnp.repeat(Bm, rep, axis=2)
            Ch = jnp.repeat(Cm, rep, axis=2)
            dt = jax.nn.softplus(dt + dt_bias)
            a = jnp.exp(dt * -jnp.exp(A_log))
            db = dt[..., None, None] * x[..., None] * Bh[:, :, :, None, :]

            def combine(e1, e2):
                a1, s1 = e1
                a2, s2 = e2
                return (a1 * a2, a2[..., None, None] * s1 + s2)
            states = lax.associative_scan(combine, (a, db), axis=1)[1]
            y = jnp.einsum('blhps,blhs->blhp', states, Ch) + D_param[None, None, :, None] * x
            y = y.reshape(Bb, Ll, D_SSM) * jax.nn.silu(z)
            yg = y.reshape(Bb, Ll, G, D_SSM // G)
            var = jnp.mean(yg * yg, axis=-1, keepdims=True)
            y = (yg * lax.rsqrt(var + EPS)).reshape(Bb, Ll, D_SSM) * norm_w
            return y @ W_out + b_out
        return _forward(hidden_states, W_in, b_in, conv_w, conv_b, A_log, D_param, dt_bias, norm_w, W_out, b_out, mup_vector)

    def _L0_ffn_ref(x, gate_w, expert_w, expert_b):
        import jax, jax.numpy as jnp
        import numpy as np
        B, S, D, E, TOPK = (4, 512, 512, 8, 2)
        batch_shape = x.shape[:-1]
        xf = x.reshape(-1, x.shape[-1])
        T = xf.shape[0]
        logits = jnp.einsum('td,ed->te', xf, gate_w)
        top_w, top_i = jax.lax.top_k(logits, TOPK)
        top_w = jax.nn.softmax(top_w.astype(jnp.float32), axis=-1).astype(x.dtype)
        gates = jnp.zeros((T, logits.shape[-1]), dtype=x.dtype)
        gates = gates.at[jnp.arange(T)[:, None], top_i].set(top_w)
        y = jnp.einsum('td,edo->eto', xf, expert_w) + expert_b[:, None, :]
        out = jnp.einsum('te,eto->to', gates, y)
        return out.reshape(*batch_shape, -1)
    x = L0_attn_hidden_states
    x = x + 0.5 * _L0_ffn_ref(_layernorm(x, axis=-1), L0_ffn_gate_w, L0_ffn_expert_w, L0_ffn_expert_b)
    x = x + _L0_attn_ref(_layernorm(x, axis=-1), L0_attn_W_in, L0_attn_b_in, L0_attn_conv_w, L0_attn_conv_b, L0_attn_A_log, L0_attn_D_param, L0_attn_dt_bias, L0_attn_norm_w, L0_attn_W_out, L0_attn_b_out, L0_attn_mup_vector)
    x = x + 0.5 * _L0_ffn_ref(_layernorm(x, axis=-1), L0_ffn_gate_w, L0_ffn_expert_w, L0_ffn_expert_b)
    return x

_drawn_inputs = setup_inputs


def setup_inputs(seed=0):
    import zlib

    import numpy as np

    out = dict(_drawn_inputs(seed))
    spreads = {'L0_attn_b_out': (0.0, 0.1), 'L0_ffn_expert_b': (0.0, 0.1)}
    factors = {'L0_attn_A_log': 7.899, 'L0_attn_dt_bias': 3.534, 'L0_attn_norm_w': 3.403}
    for name, (base, spread) in spreads.items():
        noise = np.random.default_rng([zlib.crc32(name.encode()), seed]).standard_normal(out[name].shape)
        drawn = base * np.exp(spread * noise) if base else spread * noise
        out[name] = jnp.asarray(drawn.astype(out[name].dtype))
    for name, factor in factors.items():
        out[name] = (out[name] * factor).astype(out[name].dtype)
    return out
```

```python
from contextlib import ExitStack

import concourse.bass as bass
from concourse import mybir

P = 128
F32 = mybir.dt.float32
I32 = mybir.dt.int32
U32 = mybir.dt.uint32
ALU = mybir.AluOpType
ACT = mybir.ActivationFunctionType
AX_X = mybir.AxisListType.X
ds = bass.ds

D = 512
KD = D // P
TOKENS = 2 * 1024
NT = TOKENS // P
QT = 4
NQ = NT // QT
BLK = QT * P
NE = 8
MAX_SLOT_TILES = 2 * NT + NE - 1
U = 3
SLOT_LOOPS = MAX_SLOT_TILES // U
assert SLOT_LOOPS * U == MAX_SLOT_TILES

NH, HD, NG, NS = 32, 64, 8, 32
GH = NH // NG
D_SSM = NH * HD
GC = D_SSM // NG
CT = GC // P
X0 = D_SSM
B0 = 2 * D_SSM
C0 = B0 + NG * NS
DT0 = C0 + NG * NS
TAPS = 4
PAD = TAPS - 1
EPS = 1e-5
WORK = 11840
KEPT = 3
IN_TILES = 5
BC, XA, XB, ZA, ZB = range(IN_TILES)
HALVES = 2
BLOCKS = NG * NQ
STEPS_PER_GROUP = 90

P_BX, P_MX, P_CB, P_D, P_NW, P_BZ, P_MZ, P_HBZ, P_HMZ, P_TAP = range(10)
NPAR = P_TAP + TAPS
Q_B, Q_M, Q_CB, Q_TAP = range(4)
NPARB = Q_TAP + TAPS


class Steps:

    def __init__(self, engine, sem):
        self.engine, self.sem, self.n, self.turn = engine, sem, 0, None

    def did(self, ins):
        ins.then_inc(self.sem, 1)
        self.n += 1
        return self.value()

    def value(self):
        return self.n if self.turn is None else self.turn + self.n

    def wait(self, value=None):
        self.engine.wait_ge(self.sem, self.value() if value is None else value)

    def then(self, ins):
        self.did(ins)
        self.wait()

    def enter(self, i, first, per):
        self.turn, self.start, self.per = (i - first) * per, self.n, per

    def leave(self, turns):
        assert self.n - self.start == self.per, (self.n - self.start, self.per)
        self.n, self.turn = self.start + turns * self.per, None


def build(nc, hidden, w_in, b_in, conv_w, conv_b, a_log, d_param, dt_bias, norm_w, w_out, b_out,
          mup, gate_w, expert_w, expert_b, out):
    ctx = ExitStack()
    with ctx:
        def sb(name, shape, dt=F32):
            return ctx.enter_context(nc.sbuf_tensor(name, shape, dt))

        def sem(name):
            return ctx.enter_context(nc.semaphore(name))

        x_rows = hidden.rearrange("b l d -> (b l) d").rearrange("(t p) d -> p t d", p=P)
        out_rows = out.rearrange("b l d -> (b l) d").rearrange("(t p) d -> p t d", p=P)
        slots_in = nc.dram_tensor("slots_in", [MAX_SLOT_TILES * P, D], F32)
        slots_out = nc.dram_tensor("slots_out", [MAX_SLOT_TILES * P, D], F32)
        w_in_rows = w_in.rearrange("(k p) n -> p k n", p=P)
        w_out_rows = w_out.rearrange("(g c p) n -> g p c n", c=CT, p=P)

        banks = [ctx.enter_context(nc.psum_tensor(f"bank{i}", [P, 512], F32)) for i in range(8)]
        xres = sb("xres", [P, NT, D])
        normed = sb("normed", [P, NT * D])
        xn_tok = normed[:, :].rearrange("p (t d) -> p t d", t=NT)
        xn_T = normed[:, :].rearrange("p (k t) -> p k t", k=KD)
        ew = sb("ew", [P, NE * KD * D])
        eb = sb("eb", [P, NE * D])
        arena_at = [KEPT * KD * D]

        def over(*shape):
            n = 1
            for s in shape:
                n *= s
            at = arena_at[0]
            arena_at[0] += n
            assert arena_at[0] <= NE * KD * D, "the mixer's buffers do not fit over the experts"
            names = "abcdef"[:len(shape)]
            pattern = f"p ({' '.join(names)}) -> p {' '.join(names)}"
            return ew[:, at:at + n].rearrange(pattern, **dict(zip(names, shape)))

        ident = sb("ident", [P, P])
        ones = sb("ones", [P, P])
        le = sb("le", [P, P])
        gt = sb("gt", [P, P])
        lt = sb("lt", [P, P])
        le4 = sb("le4", [P, P])
        heads_own = sb("heads_own", [P, GC])
        minus_half = sb("minus_half", [P, QT])
        zeros = sb("zeros", [P, D])
        gw_T = sb("gw_T", [P, KD, NE])
        iota_e = sb("iota_e", [P, NE])
        tile_start = sb("tile_start", [P, MAX_SLOT_TILES])
        par = sb("par", [P, NPAR, NG * CT])
        parb = sb("parb", [2 * NS, NPARB, NG])
        dt_all = sb("dt_all", [P, NG * NT * GH])
        da_all = sb("da_all", [P, NG * NT * GH])

        stats = sb("stats", [P, QT, 6])
        mean_var = sb("mean_var", [P, QT, 2])
        var_eps = sb("var_eps", [P, QT])
        rstd = sb("rstd", [P, QT])
        logits = sb("logits", [P, NT, NE])
        best = sb("best", [P, NT, 8])
        best_at = sb("best_at", [P, NT, 8], U32)
        pick = sb("pick", [P, 2, NT])
        one_hot = sb("one_hot", [P, 2, NT, NE])
        sent = sb("sent", [P, NT, NE])
        rank = sb("rank", [P, NT, NE])
        counts = sb("counts", [P, NE, NT])
        offsets = sb("offsets", [P, NE, NT])
        total = sb("total", [P, 4, NE])
        total_i = sb("total_i", [P, 2, NE], I32)
        bounds = sb("bounds", [P, 1 + NE])
        slot_f = sb("slot_f", [P, 2, NT])
        slot_i = sb("slot_i", [P, 2, NT], U32)
        emap = sb("emap", [P, MAX_SLOT_TILES])
        emap_i = sb("emap_i", [P, MAX_SLOT_TILES], I32)
        gates = sb("gates", [P, 2, NT])
        gate_e = sb("gate_e", [P, 3, NT])

        work = sb("work", [P, WORK])
        at = [0]

        def cut(*shape):
            n = 1
            for s in shape:
                n *= s
            a = at[0]
            at[0] += n
            assert at[0] <= WORK, at[0]
            names = "abcdef"[:len(shape)]
            pattern = f"p ({' '.join(names)}) -> p {' '.join(names)}"
            return work[:, a:a + n].rearrange(pattern, **dict(zip(names, shape)))

        xn_now = cut(QT, D)
        xt = cut(2, KD, P)
        xg = xn_now
        xg_T = cut(U, KD, P)
        y_sb = cut(U, D)
        y_pick = cut(QT, 2, D)
        rows_a = y_pick[:, 0, 0, :P]
        rows_w = y_pick[:, 0, 1, :]
        rows_bc = y_pick[:, 1, 0, :3 * 2 * NS].rearrange("p (v n) -> p v n", v=3)
        rows_bcw = y_pick[:, 1, 1, :2 * NS * TAPS]
        rows_gate = y_pick[:, 2, 0, :]
        d_rows = y_pick[:, 2, 1, :2]
        w_dt = cut(KD, NH)
        dt_vec = cut(4, NH)
        b_out_all = cut(D)

        at[0] = 0
        w_grp = over(KD, 5 * P)
        w_cols = [w_grp[:, :, i * P:(i + 1) * P] if i else w_grp[:, :, 0:2 * NS] for i in range(IN_TILES)]
        wo_raw = cut(CT, D)
        wo = cut(CT, D)
        x_raw = over(2, CT, PAD + BLK)
        bc_raw = cut(2, PAD + BLK)
        x_c = cut(2, CT, BLK)
        bc_c = over(2, BLK)
        th_x = over(BLK)
        th_z = over(CT, BLK)
        z_c = cut(2, CT, BLK)
        c_rep = over(2, BLK)
        r_seg = cut(2, GH, P)
        decay = cut(GH, P)
        wts = cut(GH, P)
        g_m = cut(P)
        x_tok = cut(GC + NS)
        e_cum = over(2, P)
        c_dec = over(P)
        b_dec = cut(GH, NS)
        w_dec = over(GH)
        state = over(GC)
        state_in = over(GC)
        y_c = cut(CT, BLK)
        y_sq = over(CT, BLK)
        da_rep = cut(2, QT * GH, NS)
        dt_blk = over(2, QT * GH)
        v_grp = over(QT)
        rs_grp = over(QT)

        sp_a, sp_b, sp_c, sp_d = (work[:, i * 512:(i + 1) * 512] for i in range(4))

        s_dve, s_pool, a_exp = sem("dve_step"), sem("pool_step"), sem("a_exp")
        waited = sem("waited")
        s_mix, s_last = sem("dve_mixer_step"), sem("dve_last_step")
        x_in = [sem(f"x_in{q}") for q in range(NQ)]
        gate_in, experts_in, bias_in, zeros_out = sem("gate_in"), sem("experts_in"), sem("bias_in"), sem("zeros_out")
        rows_in, dtw_in = sem("rows_in"), sem("dtw_in")
        masks_made, zeros_made = sem("masks_made"), sem("zeros_made")
        d_wide, params_T, params_made, gate_T, gate_ready = (
            sem("d_wide"), sem("params_T"), sem("params_made"), sem("gate_T"), sem("gate_ready"))

        class Norm:

            def __init__(self, n):
                self.var_ready = sem(f"{n}_var_ready")
                self.rstd_ready = sem(f"{n}_rstd_ready")
                self.xn_ready = sem(f"{n}_xn_ready")
                self.kept = sem(f"{n}_xn_kept")
                self.turned = sem(f"{n}_xn_turned")
                self.xt_ready = sem(f"{n}_xt_ready")
                self.xt_used = sem(f"{n}_xt_used")

        class Mix:

            def __init__(self, n):
                self.norm = Norm(n)
                self.logits_done = sem(f"{n}_logits_done")
                self.best_ready = sem(f"{n}_best_ready")
                self.gate_exp = sem(f"{n}_gate_exp")
                self.sent_ready = sem(f"{n}_sent_ready")
                self.ranks_done = sem(f"{n}_ranks_done")
                self.slots_ready = sem(f"{n}_slots_ready")
                self.map_ready = sem(f"{n}_map_ready")
                self.scattered = sem(f"{n}_scattered")
                self.turned = sem(f"{n}_turned")
                self.xg_ready = sem(f"{n}_xg_ready")
                self.product_done = sem(f"{n}_product_done")
                self.y_ready = sem(f"{n}_y_ready")
                self.picked = sem(f"{n}_picked")
                self.stored = sem(f"{n}_stored")
                self.xg_in = [sem(f"{n}_xg_in{u}") for u in range(U)]
                self.y_out = [sem(f"{n}_y_out{u}") for u in range(U)]
                self.y_in = [sem(f"{n}_y_in{i}") for i in range(QT)]

        mixes = [Mix("mix1"), Mix("mix2")]
        mid = Norm("mid")
        dt_done, dt_kept, soft_in, soft_exp, soft_ln, dt_ready = (
            sem("dt_done"), sem("dt_kept"), sem("soft_in"), sem("soft_exp"), sem("soft_ln"), sem("dt_ready"))
        experts_again = sem("experts_again")

        w_loaded = [sem(f"w_loaded{i}") for i in range(IN_TILES)]
        wo_loaded, wo_scaled = sem("wo_loaded"), sem("wo_scaled")
        in_done, in_taken = sem("in_done"), sem("in_taken")
        conv_done, tanh_done, silu_done = sem("conv_done"), sem("tanh_done"), sem("silu_done")
        c_rep_made = sem("c_rep_made")
        r_made, da_rep_made = sem("r_made"), sem("da_rep_made")
        seg_done, turn_done, g_done = sem("seg_done"), sem("turn_done"), sem("g_done")
        decay_ready, tok_ready = sem("decay_ready"), sem("tok_ready")
        weights_ready = sem("weights_ready")
        chunk_done, state_ready = sem("chunk_done"), sem("state_ready")
        z_done, y_ready, sq_ready = sem("z_done"), sem("y_ready"), sem("sq_ready")
        v_ready, rs_ready = sem("v_ready"), sem("rs_ready")
        out_done, out_added = sem("out_done"), sem("out_added")

        def norm_vector(dve, st, nm, q, tile_ready):
            for i in range(QT):
                tile_ready(i)
                dve.sem_inc(waited, 1)
                st.did(nc.vector.bn_stats(stats[:, i, :], xres[:, ds(q * QT + i, 1), :].rearrange("p a d -> p (a d)")))
            st.wait()
            dve.sem_inc(waited, 1)
            for i in range(QT):
                st.did(nc.vector.bn_aggr(mean_var[:, i, :], stats[:, i, :]))
            st.wait()
            nc.vector.tensor_scalar(var_eps[:], mean_var[:, :, 1], EPS, None, ALU.add).then_inc(nm.var_ready, 1)
            dve.wait_ge(nm.rstd_ready, q + 1)
            for i in range(QT):
                dve.wait_ge(nm.turned, q * QT + i + 1)
                dve.wait_ge(nm.kept, q * QT + i + 1)
                nc.vector.tensor_scalar(xn_now[:, i, :], xres[:, ds(q * QT + i, 1), :].rearrange("p a d -> p (a d)"),
                                        mean_var[:, i, 0:1], rstd[:, i:i + 1], ALU.subtract, ALU.mult
                                        ).then_inc(nm.xn_ready, 1)

        def norm_pool_rstd(pool, nm, q):
            pool.wait_ge(nm.var_ready, q + 1)
            nc.gpsimd.tensor_tensor(rstd[:], var_eps[:], minus_half[:], ALU.pow).then_inc(nm.rstd_ready, 1)

        def norm_turn(pe, nm, q, i):
            pe.wait_ge(nm.xn_ready, q * QT + i + 1)
            pe.wait_ge(nm.xt_ready, q * QT + i + 1)
            for k in range(KD):
                last = nc.tensor.transpose(banks[i % 2][:, k * P:(k + 1) * P], xn_now[:, i, k * P:(k + 1) * P], ident[:])
            last.then_inc(nm.turned, 1)

        def norm_copy(act, nm, q, i):
            act.wait_ge(nm.turned, QT + q * QT + i + 1)
            act.wait_ge(nm.xt_used, q * QT + i + 1)
            return nc.scalar.copy(xt[:, i % 2, :, :].rearrange("p k t -> p (k t)"), banks[i % 2][:])

        def mix_sync(sp, m, last):
            def load(i, u):
                sp.wait_ge(m.turned, i * U + u + 1)
                sp.dma_start(xg[:, u, :], slots_in[ds((i * U + u) * P, P), :]).then_inc(m.xg_in[u], 16)

            def store(i, u):
                sp.wait_ge(m.y_ready, U + i * U + u + 1)
                sp.dma_start(slots_out[ds((i * U + u) * P, P), :], y_sb[:, u, :]).then_inc(m.y_out[u], 16)

            sp.wait_ge(m.scattered, 2 * NT * 16)
            load(0, 0)
            load(0, 1)
            with sp.Fori(0, SLOT_LOOPS - 1) as i:
                for u in range(U):
                    load(i + (u + 2) // U, (u + 2) % U)
                    store(i, u)
            n = SLOT_LOOPS - 1
            load(n, 2)
            for u in range(U):
                store(n, u)
            if last:
                for q in range(NQ):
                    sp.wait_ge(m.picked, QT * (q + 1))
                    sp.dma_start(out_rows[:, q * QT:(q + 1) * QT, :], xres[:, q * QT:(q + 1) * QT, :]).then_inc(m.stored, 16)
                sp.wait_ge(m.stored, 16 * NQ)

        def mix_tensor(pe, m):
            nm = m.norm

            def turn(q, i):
                norm_turn(pe, nm, q, i)

            def gate(q, i):
                pe.wait_ge(nm.xt_ready, 2 + q * QT + i + 1)
                for k in range(KD):
                    last = nc.tensor.matmul(banks[2][:, i * NE:(i + 1) * NE], xt[:, i % 2, k, :], gw_T[:, k, :],
                                            start=(k == 0), stop=(k == KD - 1))
                last.then_inc(nm.xt_used, 1)

            pe.sem_inc(nm.turned, QT)
            pe.sem_inc(nm.xt_used, 2)
            pe.wait_ge(masks_made, 1)
            pe.wait_ge(gate_ready, 1)
            with pe.Fori(0, NQ) as q:
                pe.wait_ge(m.logits_done, q + 1)
                turn(q, 0)
                for i in range(1, QT):
                    turn(q, i)
                    gate(q, i - 1)
                gate(q, QT - 1)
            pe.wait_ge(m.sent_ready, 1)
            flat = sent[:, :, :].rearrange("p t e -> p (t e)")
            nc.tensor.matmul(banks[3][:, 0:P], lt[:], flat, start=True, stop=True)
            nc.tensor.matmul(banks[3][:, P:2 * P], ones[:], flat, start=True, stop=True).then_inc(m.ranks_done, 1)

            turn_bank, out_bank = [banks[0], banks[1], banks[7]], [banks[4], banks[5], banks[6]]

            def turn_slots(i, u):
                pe.wait_ge(m.xg_in[u], i * 16 + 16)
                pe.wait_ge(m.xg_ready, i * U + u + 1)
                for k in range(KD):
                    last = nc.tensor.transpose(turn_bank[u][:, k * P:(k + 1) * P], xg[:, u, k * P:(k + 1) * P], ident[:])
                last.then_inc(m.turned, 1)

            def expert(i, u):
                pe.wait_ge(m.xg_ready, U + i * U + u + 1)
                pe.wait_ge(m.y_ready, i * U + u + 1)
                e = pe.value_load(emap_i[0:1, ds(i * U + u, 1)], min_val=0, max_val=(NE - 1) * D)
                for k in range(KD):
                    last = nc.tensor.matmul(out_bank[u][:], xg_T[:, u, k, :], ew[:, ds(e * KD + k * D, D)],
                                            start=(k == 0), stop=(k == KD - 1))
                last.then_inc(m.product_done, 1)

            pe.sem_inc(m.turned, U)
            pe.sem_inc(m.product_done, U)
            turn_slots(0, 0)
            pe.wait_ge(m.map_ready, 1)
            if m is mixes[0]:
                pe.wait_ge(experts_in, 16 * NE)
            else:
                pe.wait_ge(experts_again, 16 * (NE - KEPT))
            with pe.Fori(0, SLOT_LOOPS - 1) as i:
                for u in range(U):
                    turn_slots(i + (u + 1) // U, (u + 1) % U)
                    expert(i, u)
            n = SLOT_LOOPS - 1
            for u in range(U):
                if u < U - 1:
                    turn_slots(n, u + 1)
                expert(n, u)

        def mix_scalar(act, m):
            nm = m.norm
            act.sem_inc(nm.xt_ready, 2)
            with act.Fori(0, NQ) as q:
                for i in range(QT):
                    norm_copy(act, nm, q, i).then_inc(nm.xt_ready, 1)
            act.wait_ge(m.best_ready, 1)
            nc.scalar.activation(gate_e[:, 1, :], gate_e[:, 0, :], ACT.Exp).then_inc(m.gate_exp, 1)
            act.sem_inc(m.xg_ready, U)
            with act.Fori(0, SLOT_LOOPS) as i:
                for u in range(U):
                    act.wait_ge(m.turned, U + i * U + u + 1)
                    act.wait_ge(m.product_done, i * U + u + 1)
                    nc.scalar.copy(xg_T[:, u, :, :].rearrange("p k t -> p (k t)"), [banks[0], banks[1], banks[7]][u][:]
                                   ).then_inc(m.xg_ready, 1)

        def mix_pool(pool, m, first):
            nm = m.norm
            pool.sem_inc(nm.kept, QT)
            with pool.Fori(0, NQ) as q:
                norm_pool_rstd(pool, nm, q)
                for i in range(QT):
                    pool.wait_ge(nm.xn_ready, q * QT + i + 1)
                    nc.gpsimd.tensor_copy(xn_tok[:, ds(q * QT + i, 1), :].rearrange("p a d -> p (a d)"), xn_now[:, i, :]
                                          ).then_inc(nm.kept, 1)
            pool.wait_ge(nm.kept, QT + NT)
            pool.wait_ge(m.slots_ready, 1)
            if first:
                pool.wait_ge(zeros_out, 16 * SLOT_LOOPS)
            for t in range(NT):
                for j in range(2):
                    nc.gpsimd.indirect_dma_start(slots_in[:, :], bass.IndirectOffsetOnAxis(slot_i[:, j, t:t + 1], 0),
                                                 xn_tok[:, t, :], None).then_inc(m.scattered, 16)

        def mix_vector(dve, st, m, tile_ready):
            nm = m.norm
            dve.sem_inc(m.logits_done, 1)
            with dve.Fori(0, NQ) as q:
                st.enter(q, 0, 2 * QT)
                norm_vector(dve, st, nm, q, lambda i: tile_ready(q, i))
                st.leave(NQ)
                dve.wait_ge(nm.xt_used, 2 + q * QT + QT)
                nc.vector.tensor_copy(logits[:, ds(q * QT, QT), :].rearrange("p t e -> p (t e)"), banks[2][:, 0:QT * NE]
                                      ).then_inc(m.logits_done, 1)
            dve.wait_ge(m.logits_done, 1 + NQ)
            for t in range(NT):
                st.did(nc.vector.max(best[:, t, :], logits[:, t, :]))
            st.wait()
            for t in range(NT):
                st.did(nc.vector.max_index(best_at[:, t, :], best[:, t, :], logits[:, t, :]))
            nc.vector.tensor_tensor(gate_e[:, 0, :], best[:, :, 1], best[:, :, 0], ALU.subtract).then_inc(m.best_ready, 1)
            st.wait()
            st.then(nc.vector.tensor_copy(pick[:, :, :].rearrange("p j t -> p t j"), best_at[:, :, 0:2]))
            for j in range(2):
                st.did(nc.vector.tensor_tensor(one_hot[:, j, :, :], iota_e[:, None, :].to_broadcast([P, NT, NE]),
                                               pick[:, j, :, None].to_broadcast([P, NT, NE]), ALU.is_equal))
            st.wait()
            nc.vector.tensor_tensor(sent[:], one_hot[:, 0, :, :], one_hot[:, 1, :, :], ALU.add).then_inc(m.sent_ready, 1)
            dve.wait_ge(m.gate_exp, 1)
            st.then(nc.vector.tensor_scalar(gate_e[:, 2, :], gate_e[:, 1, :], 1.0, None, ALU.add))
            st.then(nc.vector.reciprocal(gate_e[:, 0, :], gate_e[:, 2, :]))
            st.did(nc.vector.tensor_scalar(gates[:, 0, :], gate_e[:, 0, :], 0.5, None, ALU.mult))
            st.did(nc.vector.scalar_tensor_tensor(gates[:, 1, :], gate_e[:, 0, :], 0.5, gate_e[:, 1, :], ALU.mult, ALU.mult))
            dve.wait_ge(m.ranks_done, 1)
            st.did(nc.vector.tensor_copy(rank[:, :, :].rearrange("p t e -> p (t e)"), banks[3][:, 0:P]))
            st.then(nc.vector.tensor_copy(counts[:], banks[3][:, P:2 * P].rearrange("p (t e) -> p e t", e=NE)))
            st.then(nc.vector.tensor_reduce(total[:, 0, :], counts[:], AX_X, ALU.add))
            st.then(nc.vector.tensor_scalar(total_i[:, 0, :], total[:, 0, :], float(P - 1), None, ALU.add))
            st.then(nc.vector.tensor_scalar(total_i[:, 1, :], total_i[:, 0, :], 7, 7, ALU.logical_shift_right, ALU.logical_shift_left))
            st.then(nc.vector.tensor_copy(total[:, 1, :], total_i[:, 1, :]))
            st.did(nc.vector.memset(bounds[:, 0:1], 0.0))
            st.then(nc.vector.memset(total[:, 2, :], 0.0))
            st.then(nc.vector.tensor_tensor_scan(bounds[:, 1:1 + NE], total[:, 1, :], total[:, 2, :], 0.0, ALU.add, ALU.add))
            for e in range(NE):
                st.did(nc.vector.tensor_tensor_scan(offsets[:, e, :], counts[:, e, :], zeros[:, 0:NT], bounds[:, e:e + 1],
                                                    ALU.add, ALU.add))
            st.wait()
            st.then(nc.vector.tensor_tensor(offsets[:], offsets[:], counts[:], ALU.subtract))
            st.then(nc.vector.tensor_tensor(rank[:], rank[:], offsets[:, :, :].rearrange("p e t -> p t e"), ALU.add))
            for j in range(2):
                st.did(nc.vector.tensor_tensor(one_hot[:, j, :, :], one_hot[:, j, :, :], rank[:], ALU.mult))
            st.wait()
            for j in range(2):
                st.did(nc.vector.tensor_reduce(slot_f[:, j, :], one_hot[:, j, :, :], AX_X, ALU.add))
            st.wait()
            nc.vector.tensor_copy(slot_i[:], slot_f[:]).then_inc(m.slots_ready, 1)
            st.then(nc.vector.tensor_scalar(emap[:], tile_start[:], bounds[:, 1:2], None, ALU.is_ge))
            for e in range(1, NE):
                st.then(nc.vector.scalar_tensor_tensor(emap[:], tile_start[:], bounds[:, 1 + e:2 + e], emap[:], ALU.is_ge, ALU.add))
            nc.vector.tensor_scalar(emap_i[:], emap[:], float(NE - 1), float(D), ALU.min, ALU.mult).then_inc(m.map_ready, 1)
            dve.sem_inc(m.y_ready, U)
            dve.wait_ge(m.map_ready, 1)
            dve.wait_ge(bias_in, 16)
            with dve.Fori(0, SLOT_LOOPS) as i:
                for u in range(U):
                    dve.wait_ge(m.product_done, U + i * U + u + 1)
                    dve.wait_ge(m.y_out[u], i * 16)
                    e = dve.value_load(emap_i[0:1, ds(i * U + u, 1)], min_val=0, max_val=(NE - 1) * D)
                    nc.vector.tensor_tensor(y_sb[:, u, :], [banks[4], banks[5], banks[6]][u][:], eb[:, ds(e, D)], ALU.add
                                            ).then_inc(m.y_ready, 1)

        def pick_pool(pool, m, t):
            i, q = t % QT, t // QT
            if t == 0:
                for u in range(U):
                    pool.wait_ge(m.y_out[u], 16 * SLOT_LOOPS)
            if q:
                pool.wait_ge(m.picked, t - QT + 1)
            for j in range(2):
                nc.gpsimd.indirect_dma_start(y_pick[:, i, j, :], None, slots_out[:, :],
                                             bass.IndirectOffsetOnAxis(slot_i[:, j, t:t + 1], 0)).then_inc(m.y_in[i], 16)

        def pick_vector(dve, st, m, q, i):
            row = xres[:, ds(q * QT + i, 1), :].rearrange("p a d -> p (a d)")
            dve.wait_ge(m.y_in[i], q * 32 + 32)
            st.then(nc.vector.scalar_tensor_tensor(row, y_pick[:, i, 0, :], gates[:, 0, ds(q * QT + i, 1)], row, ALU.mult, ALU.add))
            nc.vector.scalar_tensor_tensor(row, y_pick[:, i, 1, :], gates[:, 1, ds(q * QT + i, 1)], row, ALU.mult, ALU.add
                                           ).then_inc(m.picked, 1)

        block1 = nc.Block()
        block1.__enter__()

        @block1.sync
        def _(sp):
            for q in range(NQ):
                sp.dma_start(xres[:, q * QT:(q + 1) * QT, :], x_rows[:, q * QT:(q + 1) * QT, :]).then_inc(x_in[q], 16)
                if q == 0:
                    sp.dma_start(rows_gate[0:NE, :], gate_w).then_inc(gate_in, 16)
            sp.wait_ge(zeros_made, 1)
            for n in range(SLOT_LOOPS):
                sp.dma_start(slots_in[n * U * P:(n + 1) * U * P, :].rearrange("(u p) d -> p u d", p=P),
                             zeros[:, None, :].to_broadcast([P, U, D])).then_inc(zeros_out, 16)
            for e in range(NE):
                sp.dma_start(ew[:, e * KD * D:(e + 1) * KD * D].rearrange("p (k o) -> p k o", k=KD),
                             expert_w[e].rearrange("(k p) o -> p k o", p=P)).then_inc(experts_in, 16)
            mix_sync(sp, mixes[0], False)

        @block1.scalar
        def _(act):
            def rows(dst, src):
                act.dma_start(dst, src).then_inc(rows_in, 16)

            r = NG * CT
            for n, v in enumerate((b_in[X0:B0], b_in[0:X0], mup[X0:B0], mup[0:X0], conv_b[0:D_SSM], norm_w)):
                rows(rows_a[n * r:(n + 1) * r, :], v.rearrange("(r p) -> r p", p=P))
            rows(d_rows[96:96 + r, :], d_param.rearrange("(r h) -> r h", h=2))
            rows(rows_w[0:r, :], conv_w[0:D_SSM, :].rearrange("(r p) k -> r (p k)", p=P))
            for n, (v, o) in enumerate(((b_in, B0), (mup, B0), (conv_b, D_SSM))):
                rows(rows_bc[0:NG, n, :].rearrange("g (s n) -> g s n", s=2),
                     v[o:o + 2 * NG * NS].rearrange("(s g n) -> g s n", s=2, g=NG))
            rows(rows_bcw[0:NG, :].rearrange("g (s n) -> g s n", s=2),
                 conv_w[D_SSM:D_SSM + 2 * NG * NS, :].rearrange("(s g n) k -> g s (n k)", s=2, g=NG))
            act.dma_start(eb[:], expert_b.rearrange("e d -> (e d)").partition_broadcast(P)).then_inc(bias_in, 16)
            act.dma_start(w_dt, w_in_rows[:, :, DT0:DT0 + NH]).then_inc(dtw_in, 16)
            for n, v in enumerate((b_in[DT0:DT0 + NH], mup[DT0:DT0 + NH], dt_bias, a_log)):
                act.dma_start(dt_vec[:, n, :], v.partition_broadcast(P)).then_inc(dtw_in, 16)
            act.dma_start(b_out_all, b_out.partition_broadcast(P)).then_inc(dtw_in, 16)

            mix_scalar(act, mixes[0])
            act.sem_inc(mid.xt_ready, 2)
            with act.Fori(0, NQ) as q:
                for i in range(QT):
                    act.wait_ge(mid.turned, QT + q * QT + i + 1)
                    nc.scalar.copy(xn_T[:, :, ds((q * QT + i) * P, P)], banks[i % 2][:].rearrange("p (k t) -> p k t", k=KD))
                    norm_copy(act, mid, q, i).then_inc(mid.xt_ready, 1)
            act.wait_ge(soft_in, 1)
            nc.scalar.activation(dt_vec[:, 0, :], dt_vec[:, 3, :], ACT.Exp).then_inc(a_exp, 1)
            nc.scalar.activation(sp_c, sp_b, ACT.Exp, scale=-1.0).then_inc(soft_exp, 1)
            act.wait_ge(soft_exp, 1)
            nc.scalar.activation(sp_b, sp_c, ACT.Ln, bias=1.0).then_inc(soft_ln, 1)

        @block1.gpsimd
        def _(pool):
            nc.gpsimd.memset(ones[:], 1.0).then_inc(s_pool, 1)
            nc.gpsimd.memset(le4[:], 0.25).then_inc(s_pool, 1)
            pool.wait_ge(s_pool, 2)

            def mask(dst, src, op, row, col):
                nc.gpsimd.affine_select(out=dst[:], in_=src[:], pattern=[[col, P]], compare_op=op, fill=0.0, base=0,
                                        channel_multiplier=row).then_inc(s_pool, 1)

            mask(ident, ones, ALU.is_equal, 1, -1)
            mask(le, ones, ALU.is_ge, -1, 1)
            mask(gt, ones, ALU.is_gt, 1, -1)
            mask(lt, ones, ALU.is_gt, -1, 1)
            mask(le4, le4, ALU.is_ge, -1, 1)
            nc.gpsimd.iota(iota_e[:], pattern=[[1, NE]], base=0, channel_multiplier=0, allow_small_or_imprecise_dtypes=True
                           ).then_inc(s_pool, 1)
            nc.gpsimd.iota(tile_start[:], pattern=[[P, MAX_SLOT_TILES]], base=0, channel_multiplier=0,
                           allow_small_or_imprecise_dtypes=True).then_inc(s_pool, 1)
            nc.gpsimd.memset(minus_half[:], -0.5).then_inc(s_pool, 1)
            pool.wait_ge(s_pool, 10)
            pool.sem_inc(masks_made, 1)
            mix_pool(pool, mixes[0], True)
            for t in range(QT):
                pick_pool(pool, mixes[0], t)
            pool.sem_inc(mid.kept, QT)
            pool.wait_ge(dtw_in, 16 * 6)
            for q in range(NQ):
                norm_pool_rstd(pool, mid, q)
                if q < NQ - 1:
                    for t in range((q + 1) * QT, (q + 2) * QT):
                        pick_pool(pool, mixes[0], t)
                for i in range(QT):
                    pool.wait_ge(mid.xn_ready, q * QT + i + 1)
                    row = xres[:, q * QT + i, :]
                    nc.gpsimd.tensor_tensor(row, row, b_out_all, ALU.add).then_inc(mid.kept, 1)

        @block1.vector
        def _(dve):
            st = Steps(dve, s_dve)
            nc.vector.memset(zeros[:], 0.0).then_inc(zeros_made, 1)
            st.did(nc.vector.memset(heads_own[:], 0.0))
            st.did(nc.vector.memset(dt_all[:], 0.0))
            st.wait()
            for h in range(GH):
                st.did(nc.vector.memset(heads_own[h * NS:(h + 1) * NS, h * HD:(h + 1) * HD], 1.0))
            dve.wait_ge(rows_in, 16 * 12)
            nc.vector.tensor_copy(rows_a[96:96 + NG * CT, :].rearrange("r (h c) -> r h c", h=2),
                                  d_rows[96:96 + NG * CT, :, None].to_broadcast([NG * CT, 2, HD])).then_inc(d_wide, 1)
            dve.wait_ge(gate_T, 1)
            nc.vector.tensor_copy(gw_T[:], banks[0][:, 0:KD * NE].rearrange("p (k e) -> p k e", k=KD)).then_inc(gate_ready, 1)
            dve.wait_ge(params_T, 1)
            r = NG * CT

            def col(n):
                return banks[1][:, n * r:(n + 1) * r]

            st.did(nc.vector.tensor_copy(par[:, P_MX, :], col(2)))
            st.did(nc.vector.tensor_copy(par[:, P_MZ, :], col(3)))
            st.did(nc.vector.tensor_copy(par[:, P_CB, :], col(4)))
            st.did(nc.vector.tensor_scalar(par[:, P_NW, :], col(5), 0.5, None, ALU.mult))
            st.did(nc.vector.tensor_scalar(par[:, P_D, :], col(6), 0.5, None, ALU.mult))
            st.did(nc.vector.tensor_scalar(par[:, P_HMZ, :], col(3), 0.5, None, ALU.mult))
            for k in range(TAPS):
                st.did(nc.vector.tensor_copy(par[:, P_TAP + k, :], col(7 + k)))
            o = 11 * r
            st.did(nc.vector.tensor_copy(parb[:, :, :].rearrange("p v g -> p (v g)"), banks[1][0:2 * NS, o:o + NPARB * NG]))
            st.wait()
            st.did(nc.vector.tensor_tensor(par[:, P_BX, :], col(0), par[:, P_MX, :], ALU.mult))
            st.did(nc.vector.tensor_tensor(par[:, P_BZ, :], col(1), par[:, P_MZ, :], ALU.mult))
            st.did(nc.vector.tensor_tensor(parb[:, Q_B, :], parb[:, Q_B, :], parb[:, Q_M, :], ALU.mult))
            st.wait()
            nc.vector.tensor_scalar(par[:, P_HBZ, :], par[:, P_BZ, :], 0.5, None, ALU.mult).then_inc(params_made, 1)

            for q in range(NQ):
                dve.wait_ge(x_in[q], 16)
            mix_vector(dve, st, mixes[0], lambda q, i: None)

            with dve.Fori(0, NQ) as q:
                st.enter(q, 0, 3 * QT)
                for i in range(QT):
                    pick_vector(dve, st, mixes[0], q, i)
                norm_vector(dve, st, mid, q, lambda i: dve.wait_ge(mixes[0].picked, q * QT + i + 1))
                dve.wait_ge(mid.xt_used, 2 + q * QT + QT)
                nc.vector.tensor_copy(
                    dt_all[:, :].rearrange("p (g t h) -> p t g h", g=NG, h=GH)[:, ds(q * QT, QT), :, :],
                    banks[2][:, 0:QT * NH].rearrange("p (t g h) -> p t g h", t=QT, g=NG)).then_inc(dt_kept, 1)
                st.leave(NQ)
            dve.wait_ge(dt_kept, 1 + NQ)
            dve.wait_ge(mid.kept, QT + NT)
            dve.wait_ge(dtw_in, 16 * 6)

            def by_head(v):
                return v.rearrange("p (g h) -> p g h", g=NG)[:, :, None, :].to_broadcast([P, NG, NT, GH])

            def wide(v):
                return v.rearrange("p (g t h) -> p g t h", g=NG, h=GH)

            st.then(nc.vector.tensor_tensor(wide(sp_a), wide(dt_all[:, :]), by_head(dt_vec[:, 0, :]), ALU.add))
            st.then(nc.vector.tensor_tensor(wide(sp_a), wide(sp_a), by_head(dt_vec[:, 1, :]), ALU.mult))
            st.then(nc.vector.tensor_tensor(wide(sp_a), wide(sp_a), by_head(dt_vec[:, 2, :]), ALU.add))
            nc.vector.scalar_tensor_tensor(sp_b, sp_a, -1.0, sp_a, ALU.mult, ALU.max).then_inc(soft_in, 1)
            dve.wait_ge(soft_exp, 1)
            st.then(nc.vector.tensor_scalar(sp_d, sp_c, -0.25, 1.0 / 3.0, ALU.mult, ALU.add))
            st.then(nc.vector.tensor_tensor(sp_d, sp_d, sp_c, ALU.mult))
            st.then(nc.vector.scalar_tensor_tensor(sp_d, sp_d, -0.5, sp_c, ALU.add, ALU.mult))
            st.then(nc.vector.scalar_tensor_tensor(sp_d, sp_d, 1.0, sp_c, ALU.add, ALU.mult))
            dve.wait_ge(soft_ln, 1)
            st.then(nc.vector.tensor_tensor(sp_d, sp_d, sp_b, ALU.subtract))
            st.then(nc.vector.scalar_tensor_tensor(sp_d, sp_c, 2.0 ** -5, sp_d, ALU.is_lt, ALU.mult))
            st.then(nc.vector.tensor_tensor(sp_d, sp_d, sp_b, ALU.add))
            st.then(nc.vector.scalar_tensor_tensor(dt_all[:], sp_a, 0.0, sp_d, ALU.max, ALU.add))
            dve.wait_ge(a_exp, 1)
            st.then(nc.vector.tensor_tensor(wide(da_all[:, :]), wide(dt_all[:, :]), by_head(dt_vec[:, 0, :]), ALU.mult))
            nc.vector.tensor_scalar(da_all[:], da_all[:], -1.0, None, ALU.mult).then_inc(dt_ready, 1)

        @block1.tensor
        def _(pe):
            pe.wait_ge(masks_made, 1)
            pe.wait_ge(gate_in, 16)
            for k in range(KD):
                last = nc.tensor.transpose(banks[0][:, k * NE:(k + 1) * NE], rows_gate[0:NE, k * P:(k + 1) * P], ident[0:NE, 0:NE])
            last.then_inc(gate_T, 1)
            pe.wait_ge(d_wide, 1)
            r = NG * CT
            nc.tensor.transpose(banks[1][:, 0:7 * r], rows_a[0:7 * r, :], ident[0:7 * r, 0:7 * r])
            for k in range(TAPS):
                nc.tensor.transpose(banks[1][:, (7 + k) * r:(8 + k) * r],
                                    rows_w[0:r, :].rearrange("r (p k) -> r p k", k=TAPS)[:, :, k], ident[0:r, 0:r])
            o = 11 * r
            for n in range(3):
                nc.tensor.transpose(banks[1][0:2 * NS, o + n * NG:o + (n + 1) * NG], rows_bc[0:NG, n, :], ident[0:NG, 0:NG])
            o += 3 * NG
            for k in range(TAPS):
                last = nc.tensor.transpose(banks[1][0:2 * NS, o + k * NG:o + (k + 1) * NG],
                                           rows_bcw[0:NG, :].rearrange("g (n k) -> g n k", k=TAPS)[:, :, k], ident[0:NG, 0:NG])
            last.then_inc(params_T, 1)
            pe.wait_ge(params_made, 1)
            mix_tensor(pe, mixes[0])

            pe.sem_inc(mid.turned, QT)
            pe.sem_inc(mid.xt_used, 2)
            pe.sem_inc(dt_kept, 1)
            pe.wait_ge(dtw_in, 16 * 6)

            def dt_product(q, i):
                pe.wait_ge(mid.xt_ready, 2 + q * QT + i + 1)
                for k in range(KD):
                    last = nc.tensor.matmul(banks[2][:, i * NH:(i + 1) * NH], xt[:, i % 2, k, :], w_dt[:, k, :],
                                            start=(k == 0), stop=(k == KD - 1))
                last.then_inc(mid.xt_used, 1)

            with pe.Fori(0, NQ) as q:
                pe.wait_ge(dt_kept, q + 1)
                norm_turn(pe, mid, q, 0)
                for i in range(1, QT):
                    norm_turn(pe, mid, q, i)
                    dt_product(q, i - 1)
                dt_product(q, QT - 1)

        block1.__exit__(None, None, None)

        class At:
            def __init__(self, g, k):
                self.g, self.k = g, k
                self.grp = g + k // NQ
                self.tb = k % NQ
                self.half = self.tb % HALVES
                self.par = self.tb % 2
                self.n = g * NQ + k if isinstance(g, int) else None
                self.first, self.last = self.n == 0, self.n == BLOCKS - 1

            def before(self, n):
                return self.n is not None and self.n < n

            def plus(self, d):
                return At(self.g, self.k + d)

            def count(self, per, extra=0):
                return self.g * (per * NQ) + (self.k * per + extra)

        def in_slot(c):
            return [(BC, XA), (XB,), (ZA,), (ZB,)][c]

        def in_tile(pe, b, i):
            if b.tb == 0:
                per = 32 if i == BC else 16
                pe.wait_ge(w_loaded[i], b.grp * per + per)
            if not (b.first and i < 2):
                pe.wait_ge(in_taken, b.count(IN_TILES, i - 1))
            rows = 2 * NS if i == BC else P
            dst = banks[(b.k * IN_TILES + i) % 2][0:rows, :]
            for k in range(KD):
                last = nc.tensor.matmul(dst, w_cols[i][:, k, :], xn_T[:, k, b.tb * BLK:(b.tb + 1) * BLK],
                                        start=(k == 0), stop=(k == KD - 1))
            last.then_inc(in_done, 1)

        def chunk_start(pe, b, c):
            if c == 0:
                pe.wait_ge(silu_done, b.count(3, 3))
                pe.wait_ge(c_rep_made, b.count(1, 1))
                pe.wait_ge(da_rep_made, b.count(1, 1))
            t = slice(c * P, (c + 1) * P)
            pe.wait_ge(r_made, b.count(QT, c + 1))
            if not (b.first and c == 0):
                pe.wait_ge(decay_ready, b.count(QT, c))
            nc.tensor.matmul(banks[2][:], gt[:], r_seg[:, c % 2, :, :].rearrange("p h t -> p (h t)"),
                             start=True, stop=True).then_inc(seg_done, 1)
            if not (b.first and c == 0):
                pe.wait_ge(tok_ready, b.count(QT, c))
            nc.tensor.matmul(banks[3][:, 0:P], da_rep[:, b.par, c * GH:(c + 1) * GH, :].rearrange("p h n -> p (h n)"), le[:],
                             start=True, stop=True)
            for j in range(CT):
                nc.tensor.transpose(banks[3][:, P + j * P:P + (j + 1) * P], x_c[:, b.par, j, t], ident[:])
            nc.tensor.transpose(banks[3][:, P + GC:P + GC + NS], bc_c[0:NS, b.par, t], ident[0:NS, 0:NS]).then_inc(turn_done, 1)
            if not (b.first and c == 0):
                pe.wait_ge(state_ready, b.count(QT, c))
            nc.tensor.matmul(banks[4][:, 0:P], bc_c[0:NS, b.par, t], c_rep[0:NS, b.par, t],
                             start=True, stop=True).then_inc(g_done, 1)

        def chunk_end(pe, b, c):
            t = slice(c * P, (c + 1) * P)
            fresh = b.half == 0 and c == 0
            if c == 0 and not b.first:
                pe.wait_ge(y_ready, b.count(1))
            pe.wait_ge(weights_ready, b.count(QT, c + 1))
            for j in range(CT):
                if not fresh:
                    nc.tensor.matmul(banks[5 + j][:, t], state[:, j * P:(j + 1) * P], c_dec, start=True, stop=True,
                                     skip_group_check=True)
                for h in range(2):
                    hh = 2 * j + h
                    nc.tensor.matmul(banks[5 + j][h * HD:(h + 1) * HD, t], x_tok[:, hh * HD:(hh + 1) * HD], wts[:, hh, :],
                                     start=fresh, stop=True, skip_group_check=True)
            last = nc.tensor.matmul(banks[4][:, P:P + GC], b_dec.rearrange("p h n -> p (h n)"), x_tok[:, 0:GC], start=True, stop=True)
            if c == 0 and not b.first:
                pe.wait_ge(sq_ready, b.count(1))
                for i in range(QT):
                    for j in range(CT):
                        last = nc.tensor.matmul(banks[4][:, P + GC + i:P + GC + i + 1], y_sq[:, j, i * P:(i + 1) * P], ones[:, 0:1],
                                                start=(j == 0), stop=(j == CT - 1))
            last.then_inc(chunk_done, 1)

        def out_tile(pe, b, i):
            if i == 0:
                pe.wait_ge(wo_scaled, b.grp + 1)
                pe.wait_ge(y_ready, b.count(1, 1))
            if not (b.first and i == 0):
                pe.wait_ge(out_added, b.count(QT, i))
            for j in range(CT):
                last = nc.tensor.matmul(banks[7][:], y_c[:, j, i * P:(i + 1) * P], wo[:, j, :], start=(j == 0), stop=(j == CT - 1))
            last.then_inc(out_done, 1)

        def tensor_block(pe, b):
            for c in range(QT):
                chunk_start(pe, b, c)
                if not b.last:
                    for i in in_slot(c):
                        in_tile(pe, b.plus(1), i)
                chunk_end(pe, b, c)
                if not b.first:
                    out_tile(pe, b.plus(-1), c)

        def column(v, n, b, j=0):
            return v[:, n, ds(b.grp * CT + j, 1)] if v is par else v[:, n, ds(b.grp, 1)]

        def take_in(act, b, i):
            act.wait_ge(in_done, b.count(IN_TILES, i + 1))
            src = banks[(b.k * IN_TILES + i) % 2]
            if i in (ZA, ZB):
                j = i - ZA
                if not b.first:
                    act.wait_ge(z_done, b.count(1))
                if not b.before(2):
                    act.wait_ge(y_ready, b.plus(-1).count(1))
                act.sem_inc(waited, 1)
                nc.scalar.activation(th_z[:, j, :], src[:], ACT.Tanh, bias=column(par, P_HBZ, b, j), scale=column(par, P_HMZ, b, j))
                nc.scalar.activation(z_c[:, b.par, j, :], src[:], ACT.Identity, bias=column(par, P_BZ, b, j),
                                     scale=column(par, P_MZ, b, j)).then_inc(in_taken, 1)
                return
            if i == BC:
                n, s, o = 2 * NS, column(parb, Q_M, b), column(parb, Q_B, b)
                raw = bc_raw
            else:
                n, s, o = P, column(par, P_MX, b, i - XA), column(par, P_BX, b, i - XA)
                raw = x_raw[:, :, i - XA, :]
            if b.half == 0:
                if not b.first:
                    act.wait_ge(conv_done, b.plus(-1).count(3, i + 1))
                act.sem_inc(waited, 1)
                nc.scalar.activation(raw[0:n, 1, 0:PAD], src[0:n, BLK - PAD:BLK], ACT.Identity, bias=o, scale=s)
            elif not b.before(2):
                act.wait_ge(conv_done, b.plus(-2).count(3, i + 1))
            act.sem_inc(waited, 1)
            nc.scalar.activation(raw[0:n, b.half, PAD:], src[0:n, :], ACT.Identity, bias=o, scale=s).then_inc(in_taken, 1)

        def tanh_conv(act, b, i):
            act.wait_ge(conv_done, b.count(3, i + 1))
            if not (b.first and i == 0):
                act.wait_ge(silu_done, b.count(3, i))
            src = bc_c[0:2 * NS, b.par, :] if i == BC else x_c[:, b.par, i - XA, :]
            nc.scalar.activation(th_x[0:2 * NS, :] if i == BC else th_x, src, ACT.Tanh, scale=0.5).then_inc(tanh_done, 1)

        def repeat_c(act, b):
            act.wait_ge(silu_done, b.count(3, 1))
            for h in range(GH):
                last = nc.scalar.copy(c_rep[h * NS:(h + 1) * NS, b.par, :], bc_c[NS:2 * NS, b.par, :])
            last.then_inc(c_rep_made, 1)

        def chunk_scalar(act, b, c):
            act.wait_ge(seg_done, b.count(QT, c + 1))
            if not (b.first and c == 0):
                act.wait_ge(weights_ready, b.count(QT, c))
            nc.scalar.activation(decay.rearrange("p h t -> p (h t)"), banks[2][:], ACT.Exp).then_inc(decay_ready, 1)
            act.wait_ge(turn_done, b.count(QT, c + 1))
            if c >= 2 or not b.first:
                act.wait_ge(state_ready, b.count(QT, c - 1))
            nc.scalar.activation(e_cum[:, c % 2, :], banks[3][:, 0:P], ACT.Exp)
            nc.scalar.mul(x_tok, banks[3][:, P:P + GC + NS], 0.5).then_inc(tok_ready, 1)

        def squares(act, b):
            act.wait_ge(y_ready, b.count(1, 1))
            if not b.first:
                act.wait_ge(v_ready, b.count(1))
            nc.scalar.activation(y_sq, y_c, ACT.Square).then_inc(sq_ready, 1)

        def scalar_block(act, b):
            nx = b.plus(1)
            for c in range(QT):
                chunk_scalar(act, b, c)
                if c == 0 and not b.first:
                    squares(act, b.plus(-1))
                if b.last:
                    continue
                if c == 0:
                    take_in(act, nx, BC)
                    take_in(act, nx, XA)
                elif c == 1:
                    take_in(act, nx, XB)
                    tanh_conv(act, nx, BC)
                elif c == 2:
                    repeat_c(act, nx)
                    tanh_conv(act, nx, XA)
                    take_in(act, nx, ZA)
                else:
                    tanh_conv(act, nx, XB)
                    take_in(act, nx, ZB)

        def convolve(dve, st, b, i):
            dve.wait_ge(in_taken, b.count(IN_TILES, i + 1))
            if i == BC:
                src, dst = bc_raw[0:2 * NS, b.half, :], bc_c[0:2 * NS, b.par, :]
                w = [column(parb, Q_TAP + k, b) for k in range(TAPS)]
                bias = column(parb, Q_CB, b)
            else:
                j = i - XA
                src, dst = x_raw[:, b.half, j, :], x_c[:, b.par, j, :]
                w = [column(par, P_TAP + k, b, j) for k in range(TAPS)]
                bias = column(par, P_CB, b, j)
            st.then(nc.vector.tensor_scalar(dst, src[:, 0:BLK], w[0], bias, ALU.mult, ALU.add))
            for k in range(1, TAPS):
                ins = nc.vector.scalar_tensor_tensor(dst, src[:, k:k + BLK], w[k], dst, ALU.mult, ALU.add)
                if k < TAPS - 1:
                    st.then(ins)
            ins.then_inc(conv_done, 1)

        def silu(dve, b, i):
            dve.wait_ge(tanh_done, b.count(3, i + 1))
            v = bc_c[0:2 * NS, b.par, :] if i == BC else x_c[:, b.par, i - XA, :]
            th = th_x[0:2 * NS, :] if i == BC else th_x
            nc.vector.scalar_tensor_tensor(v, th, 1.0, v, ALU.add, ALU.mult).then_inc(silu_done, 1)

        def gate_z(dve, b):
            dve.wait_ge(in_taken, b.count(IN_TILES, IN_TILES))
            nc.vector.scalar_tensor_tensor(z_c[:, b.par, :, :].rearrange("p j t -> p (j t)"), th_z.rearrange("p j t -> p (j t)"),
                                           1.0, z_c[:, b.par, :, :].rearrange("p j t -> p (j t)"), ALU.add, ALU.mult).then_inc(z_done, 1)

        def chunk_weights(dve, st, b, c):
            fresh = b.half == 0 and c == 0
            t = slice(c * P, (c + 1) * P)
            dt_c = dt_blk[:, b.par, c * GH:(c + 1) * GH]
            if c == 0:
                dve.wait_ge(da_rep_made, b.count(1, 1))
            dve.wait_ge(decay_ready, b.count(QT, c + 1))
            st.did(nc.vector.tensor_tensor(w_dec, decay[:, :, P - 1], dt_c, ALU.mult))
            dve.wait_ge(g_done, b.count(QT, c + 1))
            st.did(nc.vector.tensor_tensor(g_m, banks[4][:, 0:P], le4[:], ALU.mult))
            dve.wait_ge(tok_ready, b.count(QT, c + 1))
            st.wait()
            nc.vector.tensor_tensor(b_dec, x_tok[:, None, GC:GC + NS].to_broadcast([P, GH, NS]),
                                    w_dec[:, :, None].to_broadcast([P, GH, NS]), ALU.mult)
            if not fresh:
                nc.vector.scalar_tensor_tensor(c_dec, c_rep[:, b.par, t], 0.5, e_cum[:, c % 2, :], ALU.mult, ALU.mult)
            for h in range(GH):
                last = nc.vector.scalar_tensor_tensor(wts[:, h, :], decay[:, h, :], dt_c[:, h:h + 1], g_m, ALU.mult, ALU.mult)
            last.then_inc(weights_ready, 1)

        def chunk_state(dve, st, b, c):
            fresh = b.half == 0 and c == 0
            dve.wait_ge(chunk_done, b.count(QT, c + 1))
            if c == 0 and not b.first:
                nc.vector.tensor_scalar(v_grp, banks[4][:, P + GC:P + GC + QT], 0.25 / GC, EPS, ALU.mult, ALU.add).then_inc(v_ready, 1)
            if fresh:
                ins = nc.vector.tensor_tensor(state, banks[4][:, P:P + GC], heads_own[:], ALU.mult)
            else:
                st.then(nc.vector.tensor_tensor(state_in, banks[4][:, P:P + GC], heads_own[:], ALU.mult))
                ins = nc.vector.scalar_tensor_tensor(state, state, e_cum[:, c % 2, P - 1:P], state_in, ALU.mult, ALU.add)
            ins.then_inc(state_ready, 1)

        def add_out(dve, b, i):
            dve.wait_ge(out_done, b.count(QT, i + 1))
            if i == 0:
                dve.wait_ge(rs_ready, b.count(1, 1))
            row = xres[:, b.tb * QT + i, :]
            nc.vector.scalar_tensor_tensor(row, banks[7][:], rs_grp[:, i:i + 1], row, ALU.mult, ALU.add).then_inc(out_added, 1)

        def finish_y(dve, st, b):
            for j in range(CT):
                st.did(nc.vector.scalar_tensor_tensor(y_c[:, j, :], x_c[:, b.par, j, :], column(par, P_D, b, j), banks[5 + j][:],
                                                      ALU.mult, ALU.add))
            st.wait()
            dve.wait_ge(z_done, b.count(1, 1))
            nc.vector.tensor_tensor(y_c.rearrange("p j t -> p (j t)"), y_c.rearrange("p j t -> p (j t)"),
                                    z_c[:, b.par, :, :].rearrange("p j t -> p (j t)"), ALU.mult).then_inc(y_ready, 1)
            if b.tb == 0:
                dve.wait_ge(wo_loaded, b.grp * 16 + 16)
                for j in range(CT):
                    last = nc.vector.tensor_scalar(wo[:, j, :], wo_raw[:, j, :], column(par, P_NW, b, j), None, ALU.mult)
                last.then_inc(wo_scaled, 1)

        def vector_block(dve, st, b):
            nx = b.plus(1)
            for c in range(QT):
                chunk_weights(dve, st, b, c)
                if c == 0:
                    gate_z(dve, b)
                elif not b.last:
                    convolve(dve, st, nx, (BC, XA, XB)[c - 1])
                chunk_state(dve, st, b, c)
                if c and not b.last:
                    silu(dve, nx, (BC, XA, XB)[c - 1])
                if not b.first:
                    add_out(dve, b.plus(-1), c)
            finish_y(dve, st, b)

        def pool_head(pool, b):
            n = QT * GH
            if not b.before(2):
                pool.wait_ge(turn_done, b.plus(-1).count(QT))
                pool.wait_ge(weights_ready, b.plus(-1).count(QT))
            where = ds(b.grp * (NT * GH) + b.tb * n, n)
            nc.gpsimd.tensor_copy(dt_blk[:, b.par, :], dt_all[:, where])
            nc.gpsimd.tensor_copy(da_rep[:, b.par, :, :], da_all[:, where][:, :, None].to_broadcast([P, n, NS])
                                  ).then_inc(da_rep_made, 1)

        def pool_block(pool, b):
            for c in range(QT):
                if not (b.first and c < 2):
                    pool.wait_ge(seg_done, b.count(QT, c - 1))
                pool.sem_inc(waited, 1)
                where = ds(b.grp * (NT * GH) + (b.tb * QT + c) * GH, GH)
                nc.gpsimd.tensor_tensor(r_seg[:, c % 2, :, :], da_all[:, where][:, :, None].to_broadcast([P, GH, P]),
                                        le[:, None, :].to_broadcast([P, GH, P]), ALU.mult).then_inc(r_made, 1)
                if c == 1 and not b.first:
                    pool.wait_ge(v_ready, b.count(1))
                    nc.gpsimd.tensor_tensor(rs_grp, v_grp, minus_half[:], ALU.pow).then_inc(rs_ready, 1)
                if c == 2 and not b.last:
                    pool_head(pool, b.plus(1))

        def load_group(sp, g):
            for i in range(IN_TILES):
                if not isinstance(g, int):
                    sp.wait_ge(in_done, g * (IN_TILES * NQ) - (IN_TILES - 1 - i))
                    sp.sem_inc(waited, 1)
                if i == BC:
                    sp.dma_start(w_cols[i][:, :, 0:NS], w_in_rows[:, :, ds(g * NS + B0, NS)]).then_inc(w_loaded[i], 16)
                    sp.dma_start(w_cols[i][:, :, NS:2 * NS], w_in_rows[:, :, ds(g * NS + C0, NS)]).then_inc(w_loaded[i], 16)
                else:
                    base = X0 + (i - XA) * P if i in (XA, XB) else (i - ZA) * P
                    sp.dma_start(w_cols[i], w_in_rows[:, :, ds(g * GC + base, P)]).then_inc(w_loaded[i], 16)
            if not isinstance(g, int):
                sp.wait_ge(wo_scaled, g)
            sp.dma_start(wo_raw, w_out_rows[ds(g, 1), :, :, :].rearrange("a p c n -> p (a c) n")).then_inc(wo_loaded, 16)

        block2 = nc.Block()
        block2.__enter__()

        @block2.sync
        def _(sp):
            load_group(sp, 0)
            with sp.Fori(1, NG) as g:
                load_group(sp, g)

        @block2.scalar
        def _(act):
            b = At(0, 0)
            take_in(act, b, BC)
            take_in(act, b, XA)
            tanh_conv(act, b, BC)
            take_in(act, b, XB)
            repeat_c(act, b)
            tanh_conv(act, b, XA)
            take_in(act, b, ZA)
            tanh_conv(act, b, XB)
            take_in(act, b, ZB)
            scalar_block(act, b)
            with act.Fori(0, NG - 1) as g:
                for k in range(1, NQ + 1):
                    scalar_block(act, At(g, k))
            for k in range(1, NQ):
                scalar_block(act, At(NG - 1, k))
            squares(act, At(NG - 1, NQ - 1))

        @block2.vector
        def _(dve):
            st = Steps(dve, s_mix)
            st.did(nc.vector.memset(x_raw[:, 0, :, 0:PAD], 0.0))
            st.then(nc.vector.memset(bc_raw[:, 0, 0:PAD], 0.0))
            b = At(0, 0)
            for i in (BC, XA, XB):
                convolve(dve, st, b, i)
                silu(dve, b, i)
            vector_block(dve, st, b)
            with dve.Fori(0, NG - 1) as g:
                st.enter(g, 0, STEPS_PER_GROUP)
                for k in range(1, NQ + 1):
                    vector_block(dve, st, At(g, k))
                st.leave(NG - 1)
            for k in range(1, NQ):
                vector_block(dve, st, At(NG - 1, k))
            b = At(NG - 1, NQ - 1)
            nxt = b.plus(1)
            dve.wait_ge(chunk_done, nxt.count(QT, 1))
            nc.vector.tensor_scalar(v_grp, banks[4][:, P + GC:P + GC + QT], 0.25 / GC, EPS, ALU.mult, ALU.add).then_inc(v_ready, 1)
            for i in range(QT):
                add_out(dve, b, i)

        @block2.gpsimd
        def _(pool):
            b = At(0, 0)
            pool_head(pool, b)
            pool_block(pool, b)
            with pool.Fori(0, NG - 1) as g:
                for k in range(1, NQ + 1):
                    pool_block(pool, At(g, k))
            for k in range(1, NQ):
                pool_block(pool, At(NG - 1, k))
            pool.wait_ge(v_ready, BLOCKS)
            nc.gpsimd.tensor_tensor(rs_grp, v_grp, minus_half[:], ALU.pow).then_inc(rs_ready, 1)

        @block2.tensor
        def _(pe):
            b = At(0, 0)
            for i in range(IN_TILES):
                in_tile(pe, b, i)
            tensor_block(pe, b)
            with pe.Fori(0, NG - 1) as g:
                for k in range(1, NQ + 1):
                    tensor_block(pe, At(g, k))
            for k in range(1, NQ):
                tensor_block(pe, At(NG - 1, k))
            b = At(NG - 1, NQ - 1)
            pe.wait_ge(state_ready, BLOCKS * QT)
            pe.wait_ge(sq_ready, BLOCKS)
            for i in range(QT):
                for j in range(CT):
                    last = nc.tensor.matmul(banks[4][:, P + GC + i:P + GC + i + 1], y_sq[:, j, i * P:(i + 1) * P], ones[:, 0:1],
                                            start=(j == 0), stop=(j == CT - 1))
            last.then_inc(chunk_done, 1)
            for i in range(QT):
                out_tile(pe, b, i)

        block2.__exit__(None, None, None)

        block3 = nc.Block()
        block3.__enter__()

        @block3.sync
        def _(sp):
            for e in range(KEPT, NE):
                sp.dma_start(ew[:, e * KD * D:(e + 1) * KD * D].rearrange("p (k o) -> p k o", k=KD),
                             expert_w[e].rearrange("(k p) o -> p k o", p=P)).then_inc(experts_again, 16)
            mix_sync(sp, mixes[1], True)

        @block3.scalar
        def _(act):
            mix_scalar(act, mixes[1])

        @block3.gpsimd
        def _(pool):
            mix_pool(pool, mixes[1], False)
            for t in range(NT):
                pick_pool(pool, mixes[1], t)

        @block3.vector
        def _(dve):
            st = Steps(dve, s_last)
            mix_vector(dve, st, mixes[1], lambda q, i: None)
            with dve.Fori(0, NQ) as q:
                st.enter(q, 0, QT)
                for i in range(QT):
                    pick_vector(dve, st, mixes[1], q, i)
                st.leave(NQ)

        @block3.tensor
        def _(pe):
            mix_tensor(pe, mixes[1])

        block3.__exit__(None, None, None)


_INS = ["L0_attn_hidden_states", "L0_attn_W_in", "L0_attn_b_in", "L0_attn_conv_w", "L0_attn_conv_b", "L0_attn_A_log",
        "L0_attn_D_param", "L0_attn_dt_bias", "L0_attn_norm_w", "L0_attn_W_out", "L0_attn_b_out", "L0_attn_mup_vector",
        "L0_ffn_gate_w", "L0_ffn_expert_w", "L0_ffn_expert_b"]


def kernel(**inputs):
    import numpy as _np
    import concourse.bacc as _bacc
    from concourse import mybir as _mybir
    from concourse.bass_utils import run_bass_kernel_spmd as _run

    nc = _bacc.Bacc("TRN2", target_bir_lowering=False, num_devices=1)
    arrays, args = {}, []
    for name in _INS:
        a = _np.ascontiguousarray(inputs[name])
        arrays[f"in_{name}_dram"] = a
        args.append(nc.dram_tensor(f"in_{name}_dram", a.shape, _mybir.dt.from_np(a.dtype), kind="ExternalInput").ap())
    out = nc.dram_tensor("out_0_dram", inputs["L0_attn_hidden_states"].shape, _mybir.dt.float32, kind="ExternalOutput").ap()
    build(nc, *args, out)
    r = _run(nc, [arrays], core_ids=[0])
    return r.results[0]["out_0_dram"]
```

```python
from contextlib import ExitStack

import concourse.bass as bass
from concourse import mybir

P = 128
F32 = mybir.dt.float32
F32R = mybir.dt.float32r
F16 = mybir.dt.float16
I32 = mybir.dt.int32
U32 = mybir.dt.uint32
ALU = mybir.AluOpType
ACT = mybir.ActivationFunctionType
AX_X = mybir.AxisListType.X
ds = bass.ds

D = 512
KD = D // P
TOKENS = 2 * 1024
NT = TOKENS // P
QT = 4
NQ = NT // QT
BLK = QT * P
NE = 8
MAX_SLOT_TILES = 2 * NT + NE - 1
HOT = 8
U = 3
SLOT_LOOPS = MAX_SLOT_TILES // U
assert SLOT_LOOPS * U == MAX_SLOT_TILES

NH, HD, NG, NS = 32, 64, 8, 32
GH = NH // NG
D_SSM = NH * HD
GC = D_SSM // NG
CT = GC // P
X0 = D_SSM
B0 = 2 * D_SSM
C0 = B0 + NG * NS
DT0 = C0 + NG * NS
TAPS = 4
PAD = TAPS - 1
EPS = 1e-5
IN_TILES = 5
BC, XA, XB, ZA, ZB = range(IN_TILES)
HALVES = 2
BLOCKS = NG * NQ
STEPS_PER_GROUP = 62
POOL_STEPS_PER_GROUP = NQ * QT

P_BX, P_MX, P_CB, P_D, P_NW, P_BZ, P_MZ, P_HBZ, P_HMZ, P_LM, P_LB, P_TAP = range(12)
NPAR = P_TAP + TAPS
Q_B, Q_M, Q_CB, Q_TAP = range(4)
Q_LM = Q_TAP + TAPS
Q_LB = Q_LM + 1
NPARB = Q_LB + 1


class Steps:

    def __init__(self, engine, sem):
        self.engine, self.sem, self.n, self.turn = engine, sem, 0, None

    def did(self, ins):
        ins.then_inc(self.sem, 1)
        self.n += 1
        return self.value()

    def value(self):
        return self.n if self.turn is None else self.turn + self.n

    def wait(self, value=None):
        self.engine.wait_ge(self.sem, self.value() if value is None else value)

    def then(self, ins):
        self.did(ins)
        self.wait()

    def enter(self, i, first, per):
        self.turn, self.start, self.per = (i - first) * per, self.n, per

    def leave(self, turns):
        assert self.n - self.start == self.per, (self.n - self.start, self.per)
        self.n, self.turn = self.start + turns * self.per, None


def build(nc, hidden, w_in, b_in, conv_w, conv_b, a_log, d_param, dt_bias, norm_w, w_out, b_out,
          mup, gate_w, expert_w, expert_b, out):
    ctx = ExitStack()
    with ctx:
        def sb(name, shape, dt=F32):
            return ctx.enter_context(nc.sbuf_tensor(name, shape, dt))

        def sem(name):
            return ctx.enter_context(nc.semaphore(name))

        x_rows = hidden.rearrange("b l d -> (b l) d").rearrange("(t p) d -> p t d", p=P)
        out_rows = out.rearrange("b l d -> (b l) d").rearrange("(t p) d -> p t d", p=P)
        xn_rows = nc.dram_tensor("xn_rows", [TOKENS, D], F32)
        slots_out = nc.dram_tensor("slots_out", [MAX_SLOT_TILES * P, D], F32)
        w_in_rows = w_in.rearrange("(k p) n -> p k n", p=P)
        w_out_rows = w_out.rearrange("(g c p) n -> g p c n", c=CT, p=P)

        banks = [ctx.enter_context(nc.psum_tensor(f"bank{i}", [P, 512], F32)) for i in range(8)]
        xres = sb("xres", [P, NT, D])
        ident = sb("ident", [P, P])
        ones = sb("ones", [P, P])
        le = sb("le", [P, P])
        le_half = sb("le_half", [P, P])
        heads_own = sb("heads_own", [P, GH])
        minus_half = sb("minus_half", [P, NT])
        gw_T = sb("gw_T", [P, KD, NE])
        iota_e = sb("iota_e", [P, NE])
        tile_start = sb("tile_start", [P, MAX_SLOT_TILES])
        par = sb("par", [P, NPAR, NG * CT])
        parb = sb("parb", [P, NPARB, NG])
        iota_p = sb("iota_p", [P, P])
        token_id = sb("token_id", [P, NT])
        stats = sb("stats", [P, QT, 6])
        mean_var = sb("mean_var", [P, QT, 2])
        mean = sb("mean", [P, NT])
        var_eps = sb("var_eps", [P, NT])
        rstd = sb("rstd", [P, NT])

        s_dve, s_pool, a_exp = sem("dve_step"), sem("pool_step"), sem("a_exp")
        waited = sem("waited")
        s_mix, s_last = sem("dve_mixer_step"), sem("dve_last_step")
        x_in = [sem(f"x_in{q}") for q in range(NQ)]
        gate_in, experts_in, bias_in = sem("gate_in"), sem("experts_in"), sem("bias_in")
        rows_in, dtw_in = sem("rows_in"), sem("dtw_in")
        masks_made = sem("masks_made")
        d_wide, params_T, params_made, gate_T, gate_ready = (
            sem("d_wide"), sem("params_T"), sem("params_made"), sem("gate_T"), sem("gate_ready"))

        class Norm:

            def __init__(self, n):
                self.var_ready = sem(f"{n}_var_ready")
                self.rstd_ready = sem(f"{n}_rstd_ready")
                self.xn_ready = sem(f"{n}_xn_ready")
                self.turned = sem(f"{n}_xn_turned")
                self.xt_ready = sem(f"{n}_xt_ready")
                self.xt_used = sem(f"{n}_xt_used")
                self.stored = [sem(f"{n}_xn_stored{h}") for h in range(2)]

        class Mix:

            def __init__(self, n):
                self.name, self.norm = n, Norm(n)
                self.gate_taken = sem(f"{n}_gate_taken")
                self.logits_done = sem(f"{n}_logits_done")
                self.best_ready = sem(f"{n}_best_ready")
                self.gate_exp = sem(f"{n}_gate_exp")
                self.sent_ready = sem(f"{n}_sent_ready")
                self.ranks_done = sem(f"{n}_ranks_done")
                self.map_ready = sem(f"{n}_map_ready")
                self.parts_ready = sem(f"{n}_parts_ready")
                self.tile_ready = sem(f"{n}_tile_ready")
                self.low_ready = sem(f"{n}_low_ready")
                self.high_ready = sem(f"{n}_high_ready")
                self.table_done = sem(f"{n}_table_done")
                self.table_ready = sem(f"{n}_table_ready")
                self.turned = sem(f"{n}_turned")
                self.xg_ready = sem(f"{n}_xg_ready")
                self.product_done = sem(f"{n}_product_done")
                self.y_ready = sem(f"{n}_y_ready")
                self.picked = sem(f"{n}_picked")
                self.stored = sem(f"{n}_stored")
                self.xg_in = [sem(f"{n}_xg_in{u}") for u in range(U)]
                self.y_out = [sem(f"{n}_y_out{u}") for u in range(U)]
                self.y_in = [sem(f"{n}_y_in{i}") for i in range(QT)]

            def allocate(self, stack):
                def sb(name, shape, dt=F32):
                    return stack.enter_context(nc.sbuf_tensor(f"{self.name}_{name}", shape, dt))

                self.ew = sb("ew", [P, NE * KD * D])
                self.eb = sb("eb", [P, NE * D])
                self.xn = sb("xn", [P, 2, QT, D])
                self.norm.slots = [self.xn[:, n // QT, n % QT, :] for n in range(2 * QT)]
                self.xt = sb("xt", [P, 2, KD, BLK])
                self.xg = sb("xg", [P, U, D])
                self.hot_low = sb("hot_low", [P, 2 * NT, P], F16)
                self.hot_high = sb("hot_high", [P, 2 * NT, MAX_SLOT_TILES], F16)
                self.slot_part_i = sb("slot_part_i", [P, 2, 2, NT], U32)
                self.slot_part = sb("slot_part", [P, 2, 2, NT])
                self.table = sb("table", [P, MAX_SLOT_TILES], U32)
                self.xg_T = sb("xg_T", [P, U, KD, P])
                self.y_sb = sb("y_sb", [P, U, D])
                self.logits_T = [self.y_sb[0:NE, q, :] for q in range(U)] + [self.xg[0:NE, 0, :]]
                self.hot_tile = self.xg_T[:, :, :, :].rearrange("p u k n -> p (u k n)")[:, 0:2 * NT * MAX_SLOT_TILES].rearrange(
                    "p (t n) -> p t n", t=2 * NT)
                self.y_pick = sb("y_pick", [P, QT, 2, D])
                self.zeros = sb("zeros", [P, NT])
                self.lt = sb("lt", [P, P])
                self.logits = sb("logits", [P, NT, NE])
                self.best = sb("best", [P, NT, 8])
                self.best_at = sb("best_at", [P, NT, 8], U32)
                self.pick = sb("pick", [P, 2, NT])
                self.one_hot = sb("one_hot", [P, 2, NT, NE])
                self.sent = sb("sent", [P, NT, NE])
                self.rank = sb("rank", [P, NT, NE])
                self.counts = sb("counts", [P, NE, NT])
                self.offsets = sb("offsets", [P, NE, NT])
                self.total = sb("total", [P, 4, NE])
                self.total_i = sb("total_i", [P, 2, NE], I32)
                self.bounds = sb("bounds", [P, 1 + NE])
                self.slot_f = sb("slot_f", [P, 2, NT])
                self.slot_i = sb("slot_i", [P, 2, NT], U32)
                self.emap = sb("emap", [P, MAX_SLOT_TILES])
                self.emap_i = sb("emap_i", [P, MAX_SLOT_TILES], I32)
                self.gates = sb("gates", [P, 2, NT])
                self.gate_e = sb("gate_e", [P, 3, NT])

        mixes = [Mix("mix1"), Mix("mix2")]
        mid = Norm("mid")
        dt_done, dt_taken, dt_turned, w_dt_cleared, soft_in, soft_exp, soft_ln, dt_ready = (
            sem("dt_done"), sem("dt_taken"), sem("dt_turned"), sem("w_dt_cleared"), sem("soft_in"), sem("soft_exp"), sem("soft_ln"), sem("dt_ready"))
        experts_again = sem("experts_again")

        w_loaded = [sem(f"w_loaded{i}") for i in range(IN_TILES)]
        w_hi_made, w_split = sem("w_hi_made"), sem("w_split")
        wo_loaded, wo_hi_made, wo_split = sem("wo_loaded"), sem("wo_hi_made"), sem("wo_split")
        w_dt_hi, w_dt_split, b_out_added = sem("w_dt_hi"), sem("w_dt_split"), sem("b_out_added")
        last_kept = sem("last_kept")
        y_hi_made, y_split = sem("y_hi_made"), sem("y_split")
        dt_blk_made, dec_ready, pool_step = sem("dt_blk_made"), sem("dec_ready"), sem("pool_mixer_step")
        in_done, in_taken = sem("in_done"), sem("in_taken")
        conv_done, tanh_done, silu_done = sem("conv_done"), sem("tanh_done"), sem("silu_done")
        c_rep_made = sem("c_rep_made")
        r_made, da_rep_made = sem("r_made"), sem("da_rep_made")
        seg_done, turn_done, g_done = sem("seg_done"), sem("turn_done"), sem("g_done")
        decay_ready, tok_ready = sem("decay_ready"), sem("tok_ready")
        weights_ready = sem("weights_ready")
        chunk_done, state_ready = sem("chunk_done"), sem("state_ready")
        z_done, y_ready, sq_ready = sem("z_done"), sem("y_ready"), sem("sq_ready")
        v_ready, rs_ready = sem("v_ready"), sem("rs_ready")
        out_done, out_added = sem("out_done"), sem("out_added")

        def norm_stats(dve, st, nm, q):
            for i in range(QT):
                st.did(nc.vector.bn_stats(stats[:, i, :], xres[:, ds(q * QT + i, 1), :].rearrange("p a d -> p (a d)")))
            st.wait()
            dve.sem_inc(waited, 1)
            for i in range(QT):
                st.did(nc.vector.bn_aggr(mean_var[:, i, :], stats[:, i, :]))
            st.wait()
            dve.sem_inc(waited, 1)
            st.then(nc.vector.tensor_copy(mean[:, ds(q * QT, QT)], mean_var[:, :, 0]))
            dve.sem_inc(waited, 1)
            nc.vector.tensor_scalar(var_eps[:, ds(q * QT, QT)], mean_var[:, :, 1], EPS, None, ALU.add
                                    ).then_inc(nm.var_ready, 1)

        def norm_apply(dve, nm, q):
            dve.wait_ge(nm.rstd_ready, q + 1)
            for i in range(QT):
                t = q * QT + i
                if t >= 2 * QT:
                    dve.wait_ge(nm.turned, t - 2 * QT + 1)
                    if nm is not mid:
                        dve.wait_ge(nm.stored[q % 2], 16)
                nc.vector.tensor_scalar(nm.slots[t % (2 * QT)], xres[:, t, :], mean[:, t:t + 1], rstd[:, t:t + 1],
                                        ALU.subtract, ALU.mult).then_inc(nm.xn_ready, 1)

        def norm_rstd(pool, nm, q):
            pool.wait_ge(nm.var_ready, q + 1)
            nc.gpsimd.tensor_tensor(rstd[:, q * QT:(q + 1) * QT], var_eps[:, q * QT:(q + 1) * QT], minus_half[:, 0:QT], ALU.pow
                                    ).then_inc(nm.rstd_ready, 1)

        def norm_turn(pe, nm, t):
            pe.wait_ge(nm.xn_ready, t + 1)
            if t >= QT:
                if nm is mid:
                    pe.wait_ge(nm.xt_used, t - QT + 1)
                else:
                    pe.wait_ge(nm.xt_ready, t - QT + 1)
            for k in range(KD):
                last = nc.tensor.transpose(banks[t % QT][:, k * P:(k + 1) * P], nm.slots[t % (2 * QT)][:, k * P:(k + 1) * P], ident[:])
            last.then_inc(nm.turned, 1)

        def load_expert(sp, m, e, loaded):
            sp.dma_start(m.ew[:, e * KD * D:(e + 1) * KD * D].rearrange("p (k o) -> p k o", k=KD),
                         expert_w[e].rearrange("(k p) o -> p k o", p=P)).then_inc(loaded, 16)

        def mix_sync(sp, m, last, loaded):
            nm = m.norm
            for q in range(NQ):
                for e in {0: (0,), 2: (1, 2, 3)}.get(q, ()):
                    load_expert(sp, m, e, loaded)
                sp.wait_ge(nm.xn_ready, (q + 1) * QT)
                sp.dma_start(xn_rows[q * BLK:(q + 1) * BLK, :].rearrange("(t p) d -> p t d", p=P), m.xn[:, q % 2, :, :]
                             ).then_inc(nm.stored[q % 2], 16)

            def store(i, u):
                sp.wait_ge(m.y_ready, U + i * U + u + 1)
                sp.dma_start(slots_out[ds((i * U + u) * P, P), :], m.y_sb[:, u, :]).then_inc(m.y_out[u], 16)

            for e in range(4, NE):
                load_expert(sp, m, e, loaded)
            sp.dma_start(m.eb[:], expert_b.rearrange("e d -> (e d)").partition_broadcast(P)).then_inc(bias_in, 16)
            with sp.Fori(0, SLOT_LOOPS) as i:
                for u in range(U):
                    store(i, u)
            if last:
                for q in range(NQ):
                    sp.wait_ge(m.picked, QT * (q + 1))
                    sp.dma_start(out_rows[:, q * QT:(q + 1) * QT, :], xres[:, q * QT:(q + 1) * QT, :]).then_inc(m.stored, 16)
                sp.wait_ge(m.stored, 16 * NQ)

        def mix_tensor(pe, m, after_table=None):
            nm = m.norm

            def gate(q):
                pe.wait_ge(nm.xt_ready, (q + 1) * QT)
                if q >= 2:
                    pe.wait_ge(m.gate_taken, q - 1)
                for k in range(KD):
                    last = nc.tensor.matmul(banks[4 + q % 2][0:NE, :], gw_T[:, k, :], m.xt[:, q % 2, k, :],
                                            start=(k == 0), stop=(k == KD - 1))
                last.then_inc(nm.xt_used, 1)

            def gate_turn(q):
                pe.wait_ge(m.gate_taken, q + 1)
                for t in range(q * QT, (q + 1) * QT):
                    last = nc.tensor.transpose(banks[6][:, t * NE:(t + 1) * NE], m.logits_T[q][:, (t % QT) * P:(t % QT + 1) * P],
                                               ident[0:NE, 0:NE])
                return last

            pe.wait_ge(masks_made, 1)
            pe.wait_ge(gate_ready, 1)
            for q in range(NQ):
                for i in range(QT):
                    norm_turn(pe, nm, q * QT + i)
                if q:
                    gate(q - 1)
                if q >= 2:
                    gate_turn(q - 2)
            gate_turn(NQ - 2)
            gate(NQ - 1)
            gate_turn(NQ - 1).then_inc(m.logits_done, 1)
            pe.wait_ge(m.sent_ready, 1)
            flat = m.sent[:, :, :].rearrange("p t e -> p (t e)")
            nc.tensor.matmul(banks[3][:, 0:P], m.lt[:], flat, start=True, stop=True)
            nc.tensor.matmul(banks[3][:, P:2 * P], ones[:], flat, start=True, stop=True).then_inc(m.ranks_done, 1)
            for n in range(2 * NT):
                pe.wait_ge(m.low_ready, n // HOT + 1)
                pe.wait_ge(m.high_ready, n // NT + 1)
                last = nc.tensor.matmul(banks[2][:, 0:MAX_SLOT_TILES], m.hot_low[:, n, :], m.hot_high[:, n, :],
                                        start=(n == 0), stop=(n == 2 * NT - 1))
            last.then_inc(m.table_done, 1)
            if after_table:
                after_table()

            turn_bank, out_bank = [banks[0], banks[1], banks[7]], [banks[4], banks[5], banks[6]]

            def turn_slots(i, u):
                pe.wait_ge(m.xg_in[u], i * 16 + 16)
                pe.wait_ge(m.xg_ready, i * U + u + 1)
                for k in range(KD):
                    last = nc.tensor.transpose(turn_bank[u][:, k * P:(k + 1) * P], m.xg[:, u, k * P:(k + 1) * P], ident[:])
                last.then_inc(m.turned, 1)

            def expert(i, u):
                pe.wait_ge(m.xg_ready, U + i * U + u + 1)
                pe.wait_ge(m.y_ready, i * U + u + 1)
                e = pe.value_load(m.emap_i[0:1, ds(i * U + u, 1)], min_val=0, max_val=(NE - 1) * D)
                for k in range(KD):
                    last = nc.tensor.matmul(out_bank[u][:], m.xg_T[:, u, k, :], m.ew[:, ds(e * KD + k * D, D)],
                                            start=(k == 0), stop=(k == KD - 1))
                last.then_inc(m.product_done, 1)

            pe.sem_inc(m.turned, U)
            pe.sem_inc(m.product_done, U)
            turn_slots(0, 0)
            pe.wait_ge(m.map_ready, 1)
            if m is mixes[0]:
                pe.wait_ge(params_made, 1)
                pe.wait_ge(experts_in, 16 * NE)
            else:
                pe.wait_ge(experts_again, 16 * NE)
            with pe.Fori(0, SLOT_LOOPS - 1) as i:
                for u in range(U):
                    turn_slots(i + (u + 1) // U, (u + 1) % U)
                    expert(i, u)
            n = SLOT_LOOPS - 1
            for u in range(U):
                if u < U - 1:
                    turn_slots(n, u + 1)
                expert(n, u)

        def mix_scalar(act, m):
            nm = m.norm
            def take_gate(q):
                act.wait_ge(nm.xt_used, q + 1)
                nc.scalar.copy(m.logits_T[q], banks[4 + q % 2][0:NE, :]).then_inc(m.gate_taken, 1)

            for q in range(NQ):
                for i in range(QT):
                    t = q * QT + i
                    act.wait_ge(nm.turned, t + 1)
                    if q >= 2:
                        act.wait_ge(nm.xt_used, q - 1)
                    nc.scalar.copy(m.xt[:, q % 2, :, i * P:(i + 1) * P], banks[i][:].rearrange("p (k t) -> p k t", k=KD)
                                   ).then_inc(nm.xt_ready, 1)
                if q:
                    take_gate(q - 1)
            take_gate(NQ - 1)
            act.wait_ge(m.best_ready, 1)
            nc.scalar.activation(m.gate_e[:, 1, :], m.gate_e[:, 0, :], ACT.Exp).then_inc(m.gate_exp, 1)
            act.sem_inc(m.xg_ready, U)
            with act.Fori(0, SLOT_LOOPS) as i:
                for u in range(U):
                    act.wait_ge(m.turned, U + i * U + u + 1)
                    act.wait_ge(m.product_done, i * U + u + 1)
                    nc.scalar.copy(m.xg_T[:, u, :, :].rearrange("p k t -> p (k t)"), [banks[0], banks[1], banks[7]][u][:]
                                   ).then_inc(m.xg_ready, 1)

        def mix_pool(pool, m):
            for q in range(NQ):
                norm_rstd(pool, m.norm, q)
            for j in range(2):
                hot = m.hot_high[:, j * NT:(j + 1) * NT, :]
                pool.wait_ge(m.tile_ready, 1)
                nc.gpsimd.tensor_tensor(hot, m.hot_tile[:, j * NT:(j + 1) * NT, :], token_id[:, :, None].to_broadcast([P, NT, MAX_SLOT_TILES]), ALU.mult
                                        ).then_inc(m.high_ready, 1)
            for h in range(2):
                pool.wait_ge(m.norm.stored[h], 16 * NQ // 2)
            pool.wait_ge(m.table_ready, 1)
            for n in range(MAX_SLOT_TILES):
                pool.wait_ge(m.turned, n + 1)
                nc.gpsimd.indirect_dma_start(m.xg[:, n % U, :], None, xn_rows[:, :],
                                             bass.IndirectOffsetOnAxis(m.table[:, n:n + 1], 0)).then_inc(m.xg_in[n % U], 16)

        def mix_vector(dve, st, m, block_ready, after_norm=None, after_table=None):
            nm = m.norm
            dve.wait_ge(masks_made, 1)
            st.did(nc.vector.tensor_tensor(m.lt[:], le[:], ident[:], ALU.subtract))
            st.did(nc.vector.memset(m.zeros[:], 0.0))
            block_ready(0)
            norm_stats(dve, st, nm, 0)
            for q in range(NQ):
                if q < NQ - 1:
                    block_ready(q + 1)
                    norm_stats(dve, st, nm, q + 1)
                norm_apply(dve, nm, q)
            if after_norm:
                after_norm()
            dve.wait_ge(m.logits_done, 1)
            st.then(nc.vector.tensor_copy(m.logits[:, :, :].rearrange("p t e -> p (t e)"), banks[6][:, 0:NT * NE]))
            for t in range(NT):
                st.did(nc.vector.max(m.best[:, t, :], m.logits[:, t, :]))
            st.wait()
            for t in range(NT):
                st.did(nc.vector.max_index(m.best_at[:, t, :], m.best[:, t, :], m.logits[:, t, :]))
            nc.vector.tensor_tensor(m.gate_e[:, 0, :], m.best[:, :, 1], m.best[:, :, 0], ALU.subtract).then_inc(m.best_ready, 1)
            st.wait()
            st.then(nc.vector.tensor_copy(m.pick[:, :, :].rearrange("p j t -> p t j"), m.best_at[:, :, 0:2]))
            for j in range(2):
                st.did(nc.vector.tensor_tensor(m.one_hot[:, j, :, :], iota_e[:, None, :].to_broadcast([P, NT, NE]),
                                               m.pick[:, j, :, None].to_broadcast([P, NT, NE]), ALU.is_equal))
            st.wait()
            nc.vector.tensor_tensor(m.sent[:], m.one_hot[:, 0, :, :], m.one_hot[:, 1, :, :], ALU.add).then_inc(m.sent_ready, 1)
            dve.wait_ge(m.gate_exp, 1)
            st.then(nc.vector.tensor_scalar(m.gate_e[:, 2, :], m.gate_e[:, 1, :], 1.0, None, ALU.add))
            st.then(nc.vector.reciprocal(m.gate_e[:, 0, :], m.gate_e[:, 2, :]))
            st.did(nc.vector.tensor_scalar(m.gates[:, 0, :], m.gate_e[:, 0, :], 0.5, None, ALU.mult))
            st.did(nc.vector.scalar_tensor_tensor(m.gates[:, 1, :], m.gate_e[:, 0, :], 0.5, m.gate_e[:, 1, :], ALU.mult, ALU.mult))
            dve.wait_ge(m.ranks_done, 1)
            st.did(nc.vector.tensor_copy(m.rank[:, :, :].rearrange("p t e -> p (t e)"), banks[3][:, 0:P]))
            st.then(nc.vector.tensor_copy(m.counts[:], banks[3][:, P:2 * P].rearrange("p (t e) -> p e t", e=NE)))
            st.then(nc.vector.tensor_reduce(m.total[:, 0, :], m.counts[:], AX_X, ALU.add))
            st.then(nc.vector.tensor_scalar(m.total_i[:, 0, :], m.total[:, 0, :], float(P - 1), None, ALU.add))
            st.then(nc.vector.tensor_scalar(m.total_i[:, 1, :], m.total_i[:, 0, :], 7, 7, ALU.logical_shift_right, ALU.logical_shift_left))
            st.then(nc.vector.tensor_copy(m.total[:, 1, :], m.total_i[:, 1, :]))
            st.did(nc.vector.memset(m.bounds[:, 0:1], 0.0))
            st.then(nc.vector.memset(m.total[:, 2, :], 0.0))
            st.then(nc.vector.tensor_tensor_scan(m.bounds[:, 1:1 + NE], m.total[:, 1, :], m.total[:, 2, :], 0.0, ALU.add, ALU.add))
            for e in range(NE):
                st.did(nc.vector.tensor_tensor_scan(m.offsets[:, e, :], m.counts[:, e, :], m.zeros[:, 0:NT], m.bounds[:, e:e + 1],
                                                    ALU.add, ALU.add))
            st.wait()
            st.then(nc.vector.tensor_tensor(m.offsets[:], m.offsets[:], m.counts[:], ALU.subtract))
            st.then(nc.vector.tensor_tensor(m.rank[:], m.rank[:], m.offsets[:, :, :].rearrange("p e t -> p t e"), ALU.add))
            for j in range(2):
                st.did(nc.vector.tensor_tensor(m.one_hot[:, j, :, :], m.one_hot[:, j, :, :], m.rank[:], ALU.mult))
            st.wait()
            for j in range(2):
                st.did(nc.vector.tensor_reduce(m.slot_f[:, j, :], m.one_hot[:, j, :, :], AX_X, ALU.add))
            st.wait()
            st.then(nc.vector.tensor_copy(m.slot_i[:], m.slot_f[:]))
            st.did(nc.vector.tensor_scalar(m.slot_part_i[:, 0, :, :], m.slot_i[:], P - 1, None, ALU.bitwise_and))
            st.did(nc.vector.tensor_scalar(m.slot_part_i[:, 1, :, :], m.slot_i[:], 7, None, ALU.logical_shift_right))
            st.wait()
            nc.vector.tensor_copy(m.slot_part[:], m.slot_part_i[:]).then_inc(m.parts_ready, 1)
            dve.wait_ge(m.parts_ready, 1)
            tile = m.slot_part[:, 1, :, :].rearrange("p j t -> p (j t)")
            nc.vector.tensor_tensor(m.hot_tile, iota_p[:, None, 0:MAX_SLOT_TILES].to_broadcast([P, 2 * NT, MAX_SLOT_TILES]),
                                    tile[:, :, None].to_broadcast([P, 2 * NT, MAX_SLOT_TILES]), ALU.is_equal).then_inc(m.tile_ready, 1)
            low = m.slot_part[:, 0, :, :].rearrange("p j t -> p (j t)")
            for n in range(0, 2 * NT, HOT):
                nc.vector.tensor_tensor(m.hot_low[:, n:n + HOT, :], iota_p[:, None, :].to_broadcast([P, HOT, P]),
                                        low[:, n:n + HOT, None].to_broadcast([P, HOT, P]), ALU.is_equal).then_inc(m.low_ready, 1)
            st.then(nc.vector.tensor_scalar(m.emap[:], tile_start[:], m.bounds[:, 1:2], None, ALU.is_ge))
            for e in range(1, NE):
                st.then(nc.vector.scalar_tensor_tensor(m.emap[:], tile_start[:], m.bounds[:, 1 + e:2 + e], m.emap[:], ALU.is_ge, ALU.add))
            nc.vector.tensor_scalar(m.emap_i[:], m.emap[:], float(NE - 1), float(D), ALU.min, ALU.mult).then_inc(m.map_ready, 1)
            dve.wait_ge(m.table_done, 1)
            nc.vector.tensor_copy(m.table[:], banks[2][:, 0:MAX_SLOT_TILES]).then_inc(m.table_ready, 1)
            if after_table:
                after_table()
            dve.sem_inc(m.y_ready, U)
            for u in range(U):
                dve.sem_inc(m.y_out[u], 16)
            dve.wait_ge(m.map_ready, 1)
            dve.wait_ge(bias_in, 16 if m is mixes[0] else 32)
            with dve.Fori(0, SLOT_LOOPS) as i:
                for u in range(U):
                    dve.wait_ge(m.product_done, U + i * U + u + 1)
                    dve.wait_ge(m.y_out[u], i * 16 + 16)
                    e = dve.value_load(m.emap_i[0:1, ds(i * U + u, 1)], min_val=0, max_val=(NE - 1) * D)
                    nc.vector.tensor_tensor(m.y_sb[:, u, :], [banks[4], banks[5], banks[6]][u][:], m.eb[:, ds(e, D)], ALU.add
                                            ).then_inc(m.y_ready, 1)

        def pick_pool(pool, m, t):
            i, q = t % QT, t // QT
            if t == 0:
                for u in range(U):
                    pool.wait_ge(m.y_out[u], 16 * SLOT_LOOPS + 16)
            if q:
                pool.wait_ge(m.picked, t - QT + 1)
            for j in range(2):
                nc.gpsimd.indirect_dma_start(m.y_pick[:, i, j, :], None, slots_out[:, :],
                                             bass.IndirectOffsetOnAxis(m.slot_i[:, j, t:t + 1], 0)).then_inc(m.y_in[i], 16)

        def pick_vector(dve, st, m, q, i):
            row = xres[:, ds(q * QT + i, 1), :].rearrange("p a d -> p (a d)")
            dve.wait_ge(m.y_in[i], q * 32 + 32)
            st.then(nc.vector.scalar_tensor_tensor(row, m.y_pick[:, i, 0, :], m.gates[:, 0, ds(q * QT + i, 1)], row, ALU.mult, ALU.add))
            nc.vector.scalar_tensor_tensor(row, m.y_pick[:, i, 1, :], m.gates[:, 1, ds(q * QT + i, 1)], row, ALU.mult, ALU.add
                                           ).then_inc(m.picked, 1)

        phase = ExitStack()
        m = mixes[0]
        m.allocate(phase)
        rows_a = m.y_pick[:, 0, 0, :P]
        rows_w = m.y_pick[:, 0, 1, :]
        rows_bc = m.y_pick[:, 1, 0, :3 * P].rearrange("p (v n) -> p v n", v=3)
        rows_bcw = m.y_pick[:, 1, 1, :]
        rows_gate = m.y_pick[:, 2, 0, :]
        d_rows = m.y_pick[:, 2, 1, :2]
        block1 = nc.Block()
        block1.__enter__()

        @block1.sync
        def _(sp):
            for q in range(NQ):
                sp.dma_start(xres[:, q * QT:(q + 1) * QT, :], x_rows[:, q * QT:(q + 1) * QT, :]).then_inc(x_in[q], 16)
                if q == 0:
                    sp.dma_start(rows_gate[0:NE, :], gate_w).then_inc(gate_in, 16)
            mix_sync(sp, mixes[0], False, experts_in)

        @block1.scalar
        def _(act):
            def rows(dst, src):
                act.dma_start(dst, src).then_inc(rows_in, 16)

            r = NG * CT
            for n, v in enumerate((b_in[X0:B0], b_in[0:X0], mup[X0:B0], mup[0:X0], conv_b[0:D_SSM], norm_w)):
                rows(rows_a[n * r:(n + 1) * r, :], v.rearrange("(r p) -> r p", p=P))
            rows(d_rows[96:96 + r, :], d_param.rearrange("(r h) -> r h", h=2))
            rows(rows_w[0:r, :], conv_w[0:D_SSM, :].rearrange("(r p) k -> r (p k)", p=P))
            for n, (v, o) in enumerate(((b_in, B0), (mup, B0), (conv_b, D_SSM))):
                rows(rows_bc[0:NG, n, 0:2 * NS].rearrange("g (s n) -> g s n", s=2),
                     v[o:o + 2 * NG * NS].rearrange("(s g n) -> g s n", s=2, g=NG))
                for c in (2, 3):
                    rows(rows_bc[0:NG, n, c * NS:(c + 1) * NS], v[o + NG * NS:o + 2 * NG * NS].rearrange("(g n) -> g n", g=NG))
            taps = conv_w[D_SSM:D_SSM + 2 * NG * NS, :]
            rows(rows_bcw[0:NG, 0:2 * NS * TAPS].rearrange("g (s n) -> g s n", s=2), taps.rearrange("(s g n) k -> g s (n k)", s=2, g=NG))
            for c in (2, 3):
                rows(rows_bcw[0:NG, c * NS * TAPS:(c + 1) * NS * TAPS], taps[NG * NS:, :].rearrange("(g n) k -> g (n k)", g=NG))

            mix_scalar(act, mixes[0])

        @block1.gpsimd
        def _(pool):
            nc.gpsimd.memset(ones[:], 1.0).then_inc(s_pool, 1)
            nc.gpsimd.memset(le_half[:], 0.5).then_inc(s_pool, 1)
            pool.wait_ge(s_pool, 2)

            def mask(dst, src, op, row, col):
                nc.gpsimd.affine_select(out=dst[:], in_=src[:], pattern=[[col, P]], compare_op=op, fill=0.0, base=0,
                                        channel_multiplier=row).then_inc(s_pool, 1)

            mask(ident, ones, ALU.is_equal, 1, -1)
            mask(le, ones, ALU.is_ge, -1, 1)
            mask(le_half, le_half, ALU.is_ge, -1, 1)
            nc.gpsimd.iota(iota_e[:], pattern=[[1, NE]], base=0, channel_multiplier=0, allow_small_or_imprecise_dtypes=True
                           ).then_inc(s_pool, 1)
            nc.gpsimd.iota(tile_start[:], pattern=[[P, MAX_SLOT_TILES]], base=0, channel_multiplier=0,
                           allow_small_or_imprecise_dtypes=True).then_inc(s_pool, 1)
            nc.gpsimd.memset(minus_half[:], -0.5).then_inc(s_pool, 1)
            nc.gpsimd.iota(iota_p[:], pattern=[[1, P]], base=0, channel_multiplier=0, allow_small_or_imprecise_dtypes=True
                           ).then_inc(s_pool, 1)
            nc.gpsimd.iota(token_id[:], pattern=[[P, NT]], base=0, channel_multiplier=1, allow_small_or_imprecise_dtypes=True
                           ).then_inc(s_pool, 1)
            pool.wait_ge(s_pool, 10)
            pool.sem_inc(masks_made, 1)
            mix_pool(pool, mixes[0])
            for t in range(NT):
                pick_pool(pool, mixes[0], t)
            for q in range(NQ):
                norm_rstd(pool, mid, q)

        @block1.vector
        def _(dve):
            st = Steps(dve, s_dve)
            st.did(nc.vector.memset(heads_own[:], 0.0))
            st.wait()
            for h in range(GH):
                st.did(nc.vector.memset(heads_own[h * NS:(h + 1) * NS, h:h + 1], 1.0))
            dve.wait_ge(gate_T, 1)
            nc.vector.tensor_copy(gw_T[:], banks[0][:, 0:KD * NE].rearrange("p (k e) -> p k e", k=KD)).then_inc(gate_ready, 1)
            def widen_d():
                dve.wait_ge(rows_in, 16 * 20)
                nc.vector.tensor_copy(rows_a[96:96 + NG * CT, :].rearrange("r (h c) -> r h c", h=2),
                                      d_rows[96:96 + NG * CT, :, None].to_broadcast([NG * CT, 2, HD])).then_inc(d_wide, 1)

            def parameters():
                dve.wait_ge(params_T, 1)
                r = NG * CT

                def col(n):
                    return banks[5][:, n * r:(n + 1) * r]

                st.did(nc.vector.tensor_copy(par[:, P_MX, :], col(2)))
                st.did(nc.vector.tensor_copy(par[:, P_MZ, :], col(3)))
                st.did(nc.vector.tensor_copy(par[:, P_CB, :], col(4)))
                st.did(nc.vector.tensor_scalar(par[:, P_NW, :], col(5), 0.5, None, ALU.mult))
                st.did(nc.vector.tensor_scalar(par[:, P_D, :], col(6), 0.5, None, ALU.mult))
                st.did(nc.vector.tensor_scalar(par[:, P_HMZ, :], col(3), 0.5, None, ALU.mult))
                for k in range(TAPS):
                    st.did(nc.vector.tensor_copy(par[:, P_TAP + k, :], col(7 + k)))
                o = 11 * r
                st.did(nc.vector.tensor_copy(parb[:, 0:Q_LM, :].rearrange("p v g -> p (v g)"), banks[5][:, o:o + Q_LM * NG]))
                st.wait()
                st.did(nc.vector.tensor_tensor(par[:, P_BX, :], col(0), par[:, P_MX, :], ALU.mult))
                st.did(nc.vector.tensor_tensor(par[:, P_BZ, :], col(1), par[:, P_MZ, :], ALU.mult))
                st.did(nc.vector.tensor_tensor(parb[:, Q_B, :], parb[:, Q_B, :], parb[:, Q_M, :], ALU.mult))
                last = TAPS - 1
                st.did(nc.vector.tensor_tensor(par[:, P_LM, :], par[:, P_TAP + last, :], par[:, P_MX, :], ALU.mult))
                st.did(nc.vector.tensor_tensor(parb[:, Q_LM, :], parb[:, Q_TAP + last, :], parb[:, Q_M, :], ALU.mult))
                st.wait()
                st.did(nc.vector.tensor_tensor(par[:, P_LB, :], par[:, P_TAP + last, :], par[:, P_BX, :], ALU.mult))
                st.then(nc.vector.tensor_tensor(parb[:, Q_LB, :], parb[:, Q_TAP + last, :], parb[:, Q_B, :], ALU.mult))
                st.did(nc.vector.tensor_tensor(par[:, P_LB, :], par[:, P_LB, :], par[:, P_CB, :], ALU.add))
                st.did(nc.vector.tensor_tensor(parb[:, Q_LB, :], parb[:, Q_LB, :], parb[:, Q_CB, :], ALU.add))
                st.wait()
                nc.vector.tensor_scalar(par[:, P_HBZ, :], par[:, P_BZ, :], 0.5, None, ALU.mult).then_inc(params_made, 1)

            mix_vector(dve, st, mixes[0], lambda q: dve.wait_ge(x_in[q], 16), widen_d, parameters)

            with dve.Fori(0, NQ) as q:
                st.enter(q, 0, 3 * QT + 1)
                for i in range(QT):
                    pick_vector(dve, st, mixes[0], q, i)
                dve.wait_ge(mixes[0].picked, q * QT + QT)
                dve.sem_inc(waited, 1)
                norm_stats(dve, st, mid, q)
                st.leave(NQ)

        @block1.tensor
        def _(pe):
            pe.wait_ge(masks_made, 1)
            pe.wait_ge(gate_in, 16)
            for k in range(KD):
                last = nc.tensor.transpose(banks[0][:, k * NE:(k + 1) * NE], rows_gate[0:NE, k * P:(k + 1) * P], ident[0:NE, 0:NE])
            last.then_inc(gate_T, 1)
            def parameters():
                pe.wait_ge(d_wide, 1)
                r = NG * CT
                nc.tensor.transpose(banks[5][:, 0:7 * r], rows_a[0:7 * r, :], ident[0:7 * r, 0:7 * r])
                for k in range(TAPS):
                    nc.tensor.transpose(banks[5][:, (7 + k) * r:(8 + k) * r],
                                        rows_w[0:r, :].rearrange("r (p k) -> r p k", k=TAPS)[:, :, k], ident[0:r, 0:r])
                o = 11 * r
                for n in range(3):
                    nc.tensor.transpose(banks[5][:, o + n * NG:o + (n + 1) * NG], rows_bc[0:NG, n, :], ident[0:NG, 0:NG])
                o += 3 * NG
                for k in range(TAPS):
                    last = nc.tensor.transpose(banks[5][:, o + k * NG:o + (k + 1) * NG],
                                               rows_bcw[0:NG, :].rearrange("g (n k) -> g n k", k=TAPS)[:, :, k], ident[0:NG, 0:NG])
                last.then_inc(params_T, 1)

            mix_tensor(pe, mixes[0], parameters)

        block1.__exit__(None, None, None)
        phase.close()

        phase = ExitStack()

        def sb(name, shape, dt=F32):
            return phase.enter_context(nc.sbuf_tensor(name, shape, dt))

        HI, LO = range(2)
        xn = [sb(f"xn_{p}", [P, KD, TOKENS], F32R) for p in ("hi", "lo")]
        w_raw = sb("w_raw", [P, 2, KD, P])
        w_grp = [sb(f"w_{p}", [P, IN_TILES, KD, P], F32R) for p in ("hi", "lo")]
        wo_raw = w_raw[:, :, :, :].rearrange("p a k n -> p (a k n)").rearrange("p (c d) -> p c d", c=CT)
        wo = [sb(f"wo_{p}", [P, CT, D], F32R) for p in ("hi", "lo")]
        y_part = [sb(f"y_{p}", [P, CT, BLK], F32R) for p in ("hi", "lo")]
        gt_r = sb("gt_r", [P, P], F32R)
        le_r = sb("le_r", [P, P], F32R)
        dt_all = sb("dt_all", [P, NG * NT * GH])
        da = sb("da", [P, 2, NG * NT * GH], F32R)
        da_rep = sb("da_rep", [P, 2, 2, GH, NS], F32R)
        r_seg = sb("r_seg", [P, 2, 2, GH, P], F32R)
        x_raw = sb("x_raw", [P, CT, PAD + BLK])
        bc_raw = sb("bc_raw", [P, PAD + BLK])
        no_steps = sb("no_steps", [P, PAD])
        x_c = sb("x_c", [P, 2, CT, BLK])
        bc_c = sb("bc_c", [P, 2, BLK])
        th_x = sb("th_x", [P, BLK])
        th_z = sb("th_z", [P, CT, BLK])
        z_c = sb("z_c", [P, 2, CT, BLK])
        c_rep = sb("c_rep", [P, 2, BLK])
        decay = sb("decay", [P, GH, P])
        wts = sb("wts", [P, GH, P])
        g_m = sb("g_m", [P, P])
        x_tok = sb("x_tok", [P, GC + NS])
        e_cum = sb("e_cum", [P, 2, P])
        c_dec = sb("c_dec", [P, P])
        w_dec = sb("w_dec", [P, GH])
        b_dec = sb("b_dec", [P, GH, NS])
        state = sb("state", [P, GC])
        state_in = sb("state_in", [P, GC])
        dt_blk = sb("dt_blk", [P, 2, QT * GH])
        v_grp = sb("v_grp", [P, QT])
        rs_grp = sb("rs_grp", [P, QT])
        mid.slots = [buf[:, n // CT, n % CT, :] for buf in (z_c, x_c) for n in range(2 * CT)]
        b_out_all = th_x
        w_dt_raw = wts[:, :, 0:NH]
        w_dt = [w[:, ZB, :, :] for w in w_grp]
        dt_T = [th_z[0:NH, 0, :], th_z[0:NH, 1, :], x_raw[0:NH, 0, 0:BLK], x_raw[0:NH, 1, 0:BLK]]
        dt_vec = decay[:, :, 0:NH]
        sp_a, sp_d = z_c[:, 0, 0, :], z_c[:, 0, 1, :]
        sp_b, sp_c = th_z[:, 0, :], th_z[:, 1, :]

        class At:
            def __init__(self, g, k):
                self.g, self.k = g, k
                self.grp = g + k // NQ
                self.tb = k % NQ
                self.half = self.tb % HALVES
                self.par = self.tb % 2
                self.n = g * NQ + k if isinstance(g, int) else None
                self.first, self.last = self.n == 0, self.n == BLOCKS - 1

            def before(self, n):
                return self.n is not None and self.n < n

            def plus(self, d):
                return At(self.g, self.k + d)

            def count(self, per, extra=0):
                assert isinstance(self.g, int) or self.k * per + extra > 0, "a wait for zero at the first group"
                return self.g * (per * NQ) + (self.k * per + extra)

            def in_group(self, per, extra):
                assert isinstance(self.g, int) or self.k // NQ * per + extra > 0, "a wait for zero at the first group"
                return self.g * per + (self.k // NQ * per + extra)

        def in_slot(c):
            return [(BC, XA), (XB,), (ZA,), (ZB,)][c]

        def split_slot(b, c):
            if b.n is not None and b.n // NQ == NG - 1:
                return ()
            if b.tb == NQ - 2:
                return [(), (BC, XA), (XB,), (ZA,)][c]
            return (ZB,) if b.tb == NQ - 1 and c == 0 else ()

        def in_tile(pe, b, i):
            if b.tb == 0:
                pe.wait_ge(w_split, b.in_group(IN_TILES, i + 1))
            if not (b.first and i < 2):
                pe.wait_ge(in_taken, b.count(IN_TILES, i - 1))
            dst = banks[(b.k * IN_TILES + i) % 2]
            for k in range(KD):
                for n, (pw, px) in enumerate(((HI, HI), (HI, LO), (LO, HI))):
                    last = nc.tensor.matmul(dst[:], w_grp[pw][:, i, k, :], xn[px][:, k, b.tb * BLK:(b.tb + 1) * BLK],
                                            start=(k == 0 and n == 0), stop=(k == KD - 1 and n == 2))
            last.then_inc(in_done, 1)

        def chunk_start(pe, b, c):
            if c == 0:
                pe.wait_ge(silu_done, b.count(3, 3))
                pe.wait_ge(c_rep_made, b.count(1, 1))
            t = slice(c * P, (c + 1) * P)
            pe.wait_ge(r_made, b.count(QT, c + 1))
            if not (b.first and c == 0):
                pe.wait_ge(decay_ready, b.count(QT, c))
            for p in (HI, LO):
                last = nc.tensor.matmul(banks[2][:], gt_r[:], r_seg[:, c % 2, p, :, :].rearrange("p h t -> p (h t)"),
                                        start=(p == HI), stop=(p == LO))
            last.then_inc(seg_done, 1)
            if not (b.first and c == 0):
                pe.wait_ge(tok_ready, b.count(QT, c))
            pe.wait_ge(da_rep_made, b.count(QT, c + 1))
            for p in (HI, LO):
                nc.tensor.matmul(banks[3][:, 0:P], da_rep[:, c % 2, p, :, :].rearrange("p h n -> p (h n)"),
                                 le_r[:], start=(p == HI), stop=(p == LO))
            for j in range(CT):
                nc.tensor.transpose(banks[3][:, P + j * P:P + (j + 1) * P], x_c[:, b.par, j, t], ident[:])
            nc.tensor.transpose(banks[3][:, P + GC:P + GC + NS], bc_c[0:NS, b.par, t], ident[0:NS, 0:NS]).then_inc(turn_done, 1)
            if not (b.first and c == 0):
                pe.wait_ge(state_ready, b.count(QT, c))
            nc.tensor.matmul(banks[4][:, 0:P], bc_c[0:NS, b.par, t], c_rep[0:NS, b.par, t],
                             start=True, stop=True).then_inc(g_done, 1)

        def chunk_end(pe, b, c):
            t = slice(c * P, (c + 1) * P)
            fresh = b.half == 0 and c == 0
            if c == 0 and not b.first:
                pe.wait_ge(y_ready, b.count(1))
            pe.wait_ge(dec_ready, b.count(QT, c + 1))
            pe.wait_ge(weights_ready, b.count(QT, c + 1))
            for j in range(CT):
                if not fresh:
                    nc.tensor.matmul(banks[5 + j][:, t], state[:, j * P:(j + 1) * P], c_dec[:], start=True, stop=True,
                                     skip_group_check=True)
                for h in range(2):
                    hh = 2 * j + h
                    nc.tensor.matmul(banks[5 + j][h * HD:(h + 1) * HD, t], x_tok[:, hh * HD:(hh + 1) * HD], wts[:, hh, :],
                                     start=fresh, stop=True, skip_group_check=True)
            last = nc.tensor.matmul(banks[4][:, P:P + GC], b_dec[:, :, :].rearrange("p h n -> p (h n)"), x_tok[:, 0:GC],
                                    start=True, stop=True)
            if c == 0 and not b.first:
                last = sum_squares(pe, b.plus(-1))
            last.then_inc(chunk_done, 1)

        def sum_squares(pe, b):
            pe.wait_ge(sq_ready, b.count(1, 1))
            for i in range(QT):
                for j in range(CT):
                    last = nc.tensor.matmul(banks[4][:, P + GC + i:P + GC + i + 1], z_c[:, b.par, j, i * P:(i + 1) * P], ones[:, 0:1],
                                            start=(j == 0), stop=(j == CT - 1))
            return last

        def out_tile(pe, b, i):
            if i == 0:
                if b.tb == 0:
                    pe.wait_ge(wo_split, b.in_group(1, 1))
                pe.wait_ge(y_split, b.count(1, 1))
            pe.wait_ge(out_added, b.count(QT, 1 + i))
            for j in range(CT):
                for n, (py, pw) in enumerate(((HI, HI), (HI, LO), (LO, HI))):
                    last = nc.tensor.matmul(banks[7][:], y_part[py][:, j, i * P:(i + 1) * P], wo[pw][:, j, :],
                                            start=(j == 0 and n == 0), stop=(j == CT - 1 and n == 2))
            last.then_inc(out_done, 1)

        def tensor_block(pe, b):
            for c in range(QT):
                chunk_start(pe, b, c)
                if not b.last:
                    for i in in_slot(c):
                        in_tile(pe, b.plus(1), i)
                chunk_end(pe, b, c)
                if not b.first:
                    out_tile(pe, b.plus(-1), c)

        def column(v, n, b, j=0):
            return v[:, n, ds(b.grp * CT + j, 1)] if v is par else v[:, n, ds(b.grp, 1)]

        def parts_of(v, i):
            if i != BC:
                return [(slice(0, P), v[:, i % 2, :, :])]
            return [(slice(0, 2 * NS), v[:, 0, :, 0:2 * NS]), (slice(2 * NS, 3 * NS), v[:, 0, :, NS:2 * NS]),
                    (slice(3 * NS, P), v[:, 0, :, NS:2 * NS])]

        def split_w_hi(act, b, i):
            per = 32 if i == BC else 16
            act.wait_ge(w_loaded[i], b.in_group(per, per))
            if not b.first:
                act.wait_ge(in_done, At(b.g, b.k // NQ * NQ).count(IN_TILES, i + 1 - IN_TILES))
            for where, src in parts_of(w_raw, i):
                last = nc.scalar.copy(w_grp[HI][:, i, :, where], src)
            last.then_inc(w_hi_made, 1)

        def take_in(act, b, i):
            act.wait_ge(in_done, b.count(IN_TILES, i + 1))
            src = banks[(b.k * IN_TILES + i) % 2]
            if i in (ZA, ZB):
                j = i - ZA
                if not b.first:
                    act.wait_ge(z_done, b.count(1))
                if not b.before(2):
                    act.wait_ge(v_ready, b.plus(-1).count(1))
                act.sem_inc(waited, 1)
                nc.scalar.activation(th_z[:, j, :], src[:], ACT.Tanh, bias=column(par, P_HBZ, b, j), scale=column(par, P_HMZ, b, j))
                nc.scalar.activation(z_c[:, b.par, j, :], src[:], ACT.Identity, bias=column(par, P_BZ, b, j),
                                     scale=column(par, P_MZ, b, j)).then_inc(in_taken, 1)
                return
            if i == BC:
                s, o = column(parb, Q_M, b), column(parb, Q_B, b)
                sl, ol = column(parb, Q_LM, b), column(parb, Q_LB, b)
                raw, conv = bc_raw, bc_c[:, b.par, :]
            else:
                s, o = column(par, P_MX, b, i - XA), column(par, P_BX, b, i - XA)
                sl, ol = column(par, P_LM, b, i - XA), column(par, P_LB, b, i - XA)
                raw, conv = x_raw[:, i - XA, :], x_c[:, b.par, i - XA, :]
            if not b.before(2):
                act.wait_ge(y_split, b.plus(-1).count(1))
            if not b.first:
                act.wait_ge(conv_done, b.plus(-1).count(3, i + 1))
                act.wait_ge(in_taken, b.plus(-1).count(IN_TILES, i + 1))
            act.sem_inc(waited, 1)
            nc.scalar.copy(raw[:, 0:PAD], raw[:, BLK:BLK + PAD] if b.half else no_steps[:]).then_inc(last_kept, 1)
            nc.scalar.activation(conv, src[:], ACT.Identity, bias=ol, scale=sl)
            act.wait_ge(last_kept, b.count(3, i + 1))
            act.sem_inc(waited, 1)
            nc.scalar.activation(raw[:, PAD:], src[:], ACT.Identity, bias=o, scale=s).then_inc(in_taken, 1)

        def tanh_conv(act, b, i):
            act.wait_ge(conv_done, b.count(3, i + 1))
            if not (b.first and i == 0):
                act.wait_ge(silu_done, b.count(3, i))
            src = bc_c[:, b.par, :] if i == BC else x_c[:, b.par, i - XA, :]
            nc.scalar.activation(th_x[:], src, ACT.Tanh, scale=0.5).then_inc(tanh_done, 1)

        def repeat_c(act, b):
            act.wait_ge(silu_done, b.count(3, 1))
            for h in range(2):
                last = nc.scalar.mul(c_rep[h * 2 * NS:(h + 1) * 2 * NS, b.par, :], bc_c[2 * NS:4 * NS, b.par, :], 0.5)
            last.then_inc(c_rep_made, 1)

        def repeat_da(act, b, c):
            if not (b.first and c < 2):
                act.wait_ge(turn_done, b.count(QT, c - 1))
            act.sem_inc(waited, 1)
            where = ds(b.grp * (NT * GH) + (b.tb * QT + c) * GH, GH)
            nc.scalar.copy(da_rep[:, c % 2, :, :, :], da[:, :, where].bitcast(F32)[:, :, :, None].to_broadcast([P, 2, GH, NS])
                           ).then_inc(da_rep_made, 1)

        def chunk_scalar(act, b, c):
            act.wait_ge(seg_done, b.count(QT, c + 1))
            if not (b.first and c == 0):
                act.wait_ge(weights_ready, b.count(QT, c))
                act.wait_ge(dec_ready, b.count(QT, c))
            nc.scalar.activation(decay[:, :, :].rearrange("p h t -> p (h t)"), banks[2][:], ACT.Exp).then_inc(decay_ready, 1)
            act.wait_ge(turn_done, b.count(QT, c + 1))
            if c >= 2 or not b.first:
                act.wait_ge(state_ready, b.count(QT, c - 1))
            nc.scalar.activation(e_cum[:, c % 2, :], banks[3][:, 0:P], ACT.Exp)
            nc.scalar.mul(x_tok[:], banks[3][:, P:P + GC + NS], 0.5).then_inc(tok_ready, 1)
            if not (b.last and c >= 2):
                repeat_da(act, b.plus((c + 2) // QT), (c + 2) % QT)

        def take_y(act, b):
            act.wait_ge(y_ready, b.count(1, 1))
            if not b.first:
                act.wait_ge(out_done, b.count(QT, 1))
            nc.scalar.copy(y_part[HI][:], x_c[:, b.par, :, :]).then_inc(y_hi_made, 1)
            nc.scalar.activation(z_c[:, b.par, :, :], x_c[:, b.par, :, :], ACT.Square).then_inc(sq_ready, 1)

        def split_wo_hi(act, b):
            act.wait_ge(wo_loaded, b.in_group(16, 16))
            if not b.first:
                act.wait_ge(out_done, b.count(QT, 1))
            act.sem_inc(waited, 1)
            for j in range(CT):
                last = nc.scalar.activation(wo[HI][:, j, :], wo_raw[:, j, :], ACT.Identity, scale=column(par, P_NW, b, j))
            last.then_inc(wo_hi_made, 1)

        def scalar_block(act, b):
            nx = b.plus(1)
            for c in range(QT):
                chunk_scalar(act, b, c)
                if c == 0 and not b.first:
                    take_y(act, b.plus(-1))
                if not b.last:
                    if c == 0:
                        take_in(act, nx, BC)
                        take_in(act, nx, XA)
                    elif c == 1:
                        tanh_conv(act, nx, BC)
                        take_in(act, nx, XB)
                    elif c == 2:
                        tanh_conv(act, nx, XA)
                        take_in(act, nx, ZA)
                        repeat_c(act, nx)
                    else:
                        tanh_conv(act, nx, XB)
                        take_in(act, nx, ZB)
                for i in split_slot(b, c):
                    split_w_hi(act, At(b.g, b.k // NQ * NQ + NQ), i)
            if b.tb == 0:
                split_wo_hi(act, b)

        def split_w_lo(dve, b, i):
            dve.wait_ge(w_hi_made, b.in_group(IN_TILES, i + 1))
            for where, src in parts_of(w_raw, i):
                last = nc.vector.tensor_tensor(w_grp[LO][:, i, :, where], src, w_grp[HI][:, i, :, where].bitcast(F32), ALU.subtract)
            last.then_inc(w_split, 1)

        def split_wo_lo(dve, b):
            dve.wait_ge(wo_hi_made, b.in_group(1, 1))
            dve.sem_inc(waited, 1)
            for j in range(CT):
                last = nc.vector.scalar_tensor_tensor(wo[LO][:, j, :], wo_raw[:, j, :], column(par, P_NW, b, j),
                                                      wo[HI][:, j, :].bitcast(F32), ALU.mult, ALU.subtract)
            last.then_inc(wo_split, 1)

        def split_y_lo(dve, b):
            dve.wait_ge(y_hi_made, b.count(1, 1))
            nc.vector.tensor_tensor(y_part[LO][:], x_c[:, b.par, :, :], y_part[HI][:].bitcast(F32), ALU.subtract).then_inc(y_split, 1)

        def convolve(dve, st, b, i):
            dve.wait_ge(in_taken, b.count(IN_TILES, i + 1))
            if i == BC:
                src, dst = bc_raw, bc_c[:, b.par, :]
                w = [column(parb, Q_TAP + k, b) for k in range(PAD)]
            else:
                j = i - XA
                src, dst = x_raw[:, j, :], x_c[:, b.par, j, :]
                w = [column(par, P_TAP + k, b, j) for k in range(PAD)]
            for k in range(PAD):
                ins = nc.vector.scalar_tensor_tensor(dst, src[:, k:k + BLK], w[k], dst, ALU.mult, ALU.add)
                if k < PAD - 1:
                    st.then(ins)
            ins.then_inc(conv_done, 1)

        def silu(dve, b, i):
            dve.wait_ge(tanh_done, b.count(3, i + 1))
            v = bc_c[:, b.par, :] if i == BC else x_c[:, b.par, i - XA, :]
            nc.vector.scalar_tensor_tensor(v, th_x[:], 1.0, v, ALU.add, ALU.mult).then_inc(silu_done, 1)

        def gate_z(dve, b):
            dve.wait_ge(in_taken, b.count(IN_TILES, IN_TILES))
            nc.vector.scalar_tensor_tensor(z_c[:, b.par, :, :], th_z[:], 1.0, z_c[:, b.par, :, :], ALU.add, ALU.mult).then_inc(z_done, 1)

        def chunk_weights(dve, st, b, c):
            dt_c = dt_blk[:, b.par, c * GH:(c + 1) * GH]
            dve.wait_ge(g_done, b.count(QT, c + 1))
            st.then(nc.vector.tensor_tensor(g_m[:], banks[4][:, 0:P], le_half[:], ALU.mult))
            if c == 0:
                dve.wait_ge(dt_blk_made, b.count(1, 1))
            dve.wait_ge(decay_ready, b.count(QT, c + 1))
            for h in range(GH):
                last = nc.vector.scalar_tensor_tensor(wts[:, h, :], decay[:, h, :], dt_c[:, h:h + 1], g_m[:], ALU.mult, ALU.mult)
            last.then_inc(weights_ready, 1)

        def mean_square(dve):
            nc.vector.tensor_scalar(v_grp[:], banks[4][:, P + GC:P + GC + QT], 0.25 / GC, EPS, ALU.mult, ALU.add).then_inc(v_ready, 1)

        def chunk_state(dve, st, b, c):
            fresh = b.half == 0 and c == 0
            dve.wait_ge(chunk_done, b.count(QT, c + 1))
            if c == 0 and not b.first:
                mean_square(dve)
            if fresh:
                ins = nc.vector.tensor_tensor(state[:, :].rearrange("p (h c) -> p h c", h=GH), banks[4][:, P:P + GC].rearrange("p (h c) -> p h c", h=GH),
                     heads_own[:, :, None].to_broadcast([P, GH, HD]), ALU.mult)
            else:
                st.then(nc.vector.tensor_tensor(state_in[:, :].rearrange("p (h c) -> p h c", h=GH), banks[4][:, P:P + GC].rearrange("p (h c) -> p h c", h=GH),
                     heads_own[:, :, None].to_broadcast([P, GH, HD]), ALU.mult))
                ins = nc.vector.scalar_tensor_tensor(state[:], state[:], e_cum[:, c % 2, P - 1:P], state_in[:], ALU.mult, ALU.add)
            ins.then_inc(state_ready, 1)

        def add_out(dve, b, i):
            dve.wait_ge(out_done, b.count(QT, 1 + i + 1))
            if i == 0:
                dve.wait_ge(rs_ready, b.count(1, 1))
            row = xres[:, b.tb * QT + i, :]
            nc.vector.scalar_tensor_tensor(row, banks[7][:], rs_grp[:, i:i + 1], row, ALU.mult, ALU.add).then_inc(out_added, 1)

        def finish_y(dve, st, b):
            for j in range(CT):
                st.did(nc.vector.scalar_tensor_tensor(x_c[:, b.par, j, :], x_c[:, b.par, j, :], column(par, P_D, b, j), banks[5 + j][:],
                                                      ALU.mult, ALU.add))
            st.wait()
            dve.wait_ge(z_done, b.count(1, 1))
            nc.vector.tensor_tensor(x_c[:, b.par, :, :], x_c[:, b.par, :, :], z_c[:, b.par, :, :], ALU.mult).then_inc(y_ready, 1)

        def vector_block(dve, st, b):
            nx = b.plus(1)
            for c in range(QT):
                chunk_weights(dve, st, b, c)
                if c == 0 and not b.first:
                    split_y_lo(dve, b.plus(-1))
                if c == 1:
                    gate_z(dve, b)
                if c < 3 and not b.last:
                    convolve(dve, st, nx, (BC, XA, XB)[c])
                chunk_state(dve, st, b, c)
                if c and not b.last:
                    silu(dve, nx, (BC, XA, XB)[c - 1])
                if not b.first:
                    add_out(dve, b.plus(-1), c)
                for i in split_slot(b, c):
                    split_w_lo(dve, At(b.g, b.k // NQ * NQ + NQ), i)
            finish_y(dve, st, b)
            if b.tb == 0:
                split_wo_lo(dve, b)

        def pool_dt(pool, b):
            if not b.before(2):
                pool.wait_ge(weights_ready, b.plus(-1).count(QT))
            pool.sem_inc(waited, 1)
            nc.gpsimd.tensor_copy(dt_blk[:, b.par, :], dt_all[:, ds(b.grp * (NT * GH) + b.tb * QT * GH, QT * GH)]
                                  ).then_inc(dt_blk_made, 1)

        def pool_segments(pool, b, c):
            if not (b.first and c < 2):
                pool.wait_ge(seg_done, b.count(QT, c - 1))
            pool.sem_inc(waited, 1)
            where = ds(b.grp * (NT * GH) + (b.tb * QT + c) * GH, GH)
            nc.gpsimd.tensor_tensor(r_seg[:, c % 2, :, :, :], da[:, :, where].bitcast(F32)[:, :, :, None].to_broadcast([P, 2, GH, P]),
                                    le[:, None, None, :].to_broadcast([P, 2, GH, P]), ALU.mult).then_inc(r_made, 1)

        def pool_decays(pool, st, b, c):
            if c == 0:
                pool.wait_ge(dt_blk_made, b.count(1, 1))
                pool.wait_ge(c_rep_made, b.count(1, 1))
            pool.wait_ge(decay_ready, b.count(QT, c + 1))
            st.did(nc.gpsimd.tensor_tensor(w_dec[:], decay[:, :, P - 1], dt_blk[:, b.par, c * GH:(c + 1) * GH], ALU.mult))
            if not (b.first and c == 0):
                pool.wait_ge(chunk_done, b.count(QT, c))
            pool.wait_ge(tok_ready, b.count(QT, c + 1))
            st.wait()
            last = nc.gpsimd.tensor_tensor(b_dec[:], x_tok[:, None, GC:GC + NS].to_broadcast([P, GH, NS]),
                                           w_dec[:, :, None].to_broadcast([P, GH, NS]), ALU.mult)
            if not (b.half == 0 and c == 0):
                last = nc.gpsimd.tensor_tensor(c_dec[:], c_rep[:, b.par, c * P:(c + 1) * P], e_cum[:, c % 2, :], ALU.mult)
            last.then_inc(dec_ready, 1)

        def pool_block(pool, st, b):
            for c in range(QT):
                pool_decays(pool, st, b, c)
                nx = b.plus((c + 2) // QT)
                if not (b.last and c >= 2):
                    pool_segments(pool, nx, (c + 2) % QT)
                if c == 0 and not b.first:
                    pool.wait_ge(v_ready, b.count(1))
                    nc.gpsimd.tensor_tensor(rs_grp[:], v_grp[:], minus_half[:, 0:QT], ALU.pow).then_inc(rs_ready, 1)
                if c == 2 and not b.last:
                    pool_dt(pool, nx)

        def load_group(sp, g):
            for i in range(IN_TILES):
                if i >= 2:
                    sp.wait_ge(w_split, g * IN_TILES + (i - 1))
                elif not isinstance(g, int):
                    sp.wait_ge(wo_split, g)
                if not isinstance(g, int):
                    sp.sem_inc(waited, 1)
                if i == BC:
                    sp.dma_start(w_raw[:, 0, :, 0:NS], w_in_rows[:, :, ds(g * NS + B0, NS)]).then_inc(w_loaded[i], 16)
                    sp.dma_start(w_raw[:, 0, :, NS:2 * NS], w_in_rows[:, :, ds(g * NS + C0, NS)]).then_inc(w_loaded[i], 16)
                else:
                    base = X0 + (i - XA) * P if i in (XA, XB) else (i - ZA) * P
                    sp.dma_start(w_raw[:, i % 2, :, :], w_in_rows[:, :, ds(g * GC + base, P)]).then_inc(w_loaded[i], 16)
            sp.wait_ge(w_split, g * IN_TILES + IN_TILES)
            if not isinstance(g, int):
                sp.sem_inc(waited, 1)
            sp.dma_start(wo_raw, w_out_rows[ds(g, 1), :, :, :].rearrange("a p c n -> p (a c) n")).then_inc(wo_loaded, 16)

        block2 = nc.Block()
        block2.__enter__()

        @block2.sync
        def _(sp):
            sp.dma_start(w_dt_raw, w_in_rows[:, :, DT0:DT0 + NH]).then_inc(dtw_in, 16)
            sp.dma_start(b_out_all[:], b_out.partition_broadcast(P)).then_inc(dtw_in, 16)
            for n, v in enumerate((b_in[DT0:DT0 + NH], mup[DT0:DT0 + NH], dt_bias, a_log)):
                sp.dma_start(dt_vec[:, n, :], v.partition_broadcast(P)).then_inc(dtw_in, 16)
            load_group(sp, 0)
            with sp.Fori(1, NG) as g:
                load_group(sp, g)

        @block2.scalar
        def _(act):
            def take_dt(q):
                act.wait_ge(dt_done, q + 1)
                nc.scalar.copy(dt_T[q], banks[4 + q][0:NH, :]).then_inc(dt_taken, 1)

            for t in range(NT):
                act.wait_ge(mid.turned, t + 1)
                nc.scalar.copy(xn[HI][:, :, t * P:(t + 1) * P], banks[t % QT][:].rearrange("p (k t) -> p k t", k=KD)
                               ).then_inc(mid.xt_ready, 1)
                if t == QT - 1:
                    act.wait_ge(dtw_in, 16 * 6)
                    act.wait_ge(w_dt_cleared, 2)
                    nc.scalar.copy(w_dt[HI][:, :, 0:NH], w_dt_raw).then_inc(w_dt_hi, 1)
                elif t % QT == QT - 1:
                    take_dt(t // QT - 1)
            take_dt(NQ - 1)
            b = At(0, 0)
            for i in (BC, XA):
                split_w_hi(act, b, i)
            act.wait_ge(soft_in, 1)
            nc.scalar.activation(dt_vec[:, 0, :], dt_vec[:, 3, :], ACT.Exp).then_inc(a_exp, 1)
            nc.scalar.activation(sp_c, sp_b, ACT.Exp, scale=-1.0).then_inc(soft_exp, 1)
            act.wait_ge(soft_exp, 1)
            nc.scalar.activation(sp_b, sp_c, ACT.Ln, bias=1.0).then_inc(soft_ln, 1)
            for i in (XB, ZA, ZB):
                split_w_hi(act, b, i)
            act.wait_ge(b_out_added, NT)
            take_in(act, b, BC)
            take_in(act, b, XA)
            tanh_conv(act, b, BC)
            take_in(act, b, XB)
            repeat_c(act, b)
            tanh_conv(act, b, XA)
            act.wait_ge(dt_ready, 1)
            take_in(act, b, ZA)
            tanh_conv(act, b, XB)
            take_in(act, b, ZB)
            repeat_da(act, b, 0)
            repeat_da(act, b, 1)
            scalar_block(act, b)
            with act.Fori(0, NG - 1) as g:
                for k in range(1, NQ + 1):
                    scalar_block(act, At(g, k))
            for k in range(1, NQ):
                scalar_block(act, At(NG - 1, k))
            take_y(act, At(NG - 1, NQ - 1))

        @block2.vector
        def _(dve):
            st = Steps(dve, s_mix)
            dve.sem_inc(out_added, 1)
            st.did(nc.vector.memset(no_steps[:], 0.0))
            st.did(nc.vector.tensor_scalar(gt_r[:], le[:], -1.0, 1.0, ALU.mult, ALU.add))
            st.did(nc.vector.tensor_copy(le_r[:], le[:]))

            def norm_lo(q):
                for t in range(q * QT, (q + 1) * QT):
                    dve.wait_ge(mid.xt_ready, t + 1)
                    where = slice(t * P, (t + 1) * P)
                    nc.vector.tensor_tensor(xn[LO][:, :, where], banks[t % QT][:].rearrange("p (k t) -> p k t", k=KD),
                                            xn[HI][:, :, where].bitcast(F32), ALU.subtract).then_inc(mid.xt_used, 1)

            for q in range(NQ):
                norm_apply(dve, mid, q)
                if q:
                    norm_lo(q - 1)
                    if q == 1:
                        dve.wait_ge(w_dt_hi, 1)
                        nc.vector.tensor_tensor(w_dt[LO][:, :, 0:NH], w_dt_raw, w_dt[HI][:, :, 0:NH].bitcast(F32), ALU.subtract
                                                ).then_inc(w_dt_split, 1)
            norm_lo(NQ - 1)
            b = At(0, 0)
            for i in (BC, XA):
                split_w_lo(dve, b, i)

            def by_head(v):
                return v.rearrange("p (g h) -> p g h", g=NG)[:, :, None, :].to_broadcast([P, NG, NT, GH])

            def wide(v):
                return v.rearrange("p (g t h) -> p g t h", g=NG, h=GH)

            dve.wait_ge(dtw_in, 16 * 6)
            dve.wait_ge(dt_turned, 1)
            st.then(nc.vector.tensor_tensor(wide(sp_a), banks[4][:].rearrange("p (t g h) -> p g t h", t=NT, g=NG),
                                            by_head(dt_vec[:, 0, :]), ALU.add))
            st.then(nc.vector.tensor_tensor(wide(sp_a), wide(sp_a), by_head(dt_vec[:, 1, :]), ALU.mult))
            st.then(nc.vector.tensor_tensor(wide(sp_a), wide(sp_a), by_head(dt_vec[:, 2, :]), ALU.add))
            nc.vector.scalar_tensor_tensor(sp_b, sp_a, -1.0, sp_a, ALU.mult, ALU.max).then_inc(soft_in, 1)
            dve.wait_ge(soft_exp, 1)
            st.then(nc.vector.tensor_scalar(sp_d, sp_c, -0.25, 1.0 / 3.0, ALU.mult, ALU.add))
            st.then(nc.vector.tensor_tensor(sp_d, sp_d, sp_c, ALU.mult))
            st.then(nc.vector.scalar_tensor_tensor(sp_d, sp_d, -0.5, sp_c, ALU.add, ALU.mult))
            st.then(nc.vector.scalar_tensor_tensor(sp_d, sp_d, 1.0, sp_c, ALU.add, ALU.mult))
            dve.wait_ge(soft_ln, 1)
            st.then(nc.vector.tensor_tensor(sp_d, sp_d, sp_b, ALU.subtract))
            st.then(nc.vector.scalar_tensor_tensor(sp_d, sp_c, 2.0 ** -5, sp_d, ALU.is_lt, ALU.mult))
            st.then(nc.vector.tensor_tensor(sp_d, sp_d, sp_b, ALU.add))
            st.then(nc.vector.scalar_tensor_tensor(dt_all[:], sp_a, 0.0, sp_d, ALU.max, ALU.add))
            dve.wait_ge(a_exp, 1)
            st.then(nc.vector.tensor_tensor(wide(sp_b), wide(dt_all[:, :]), by_head(dt_vec[:, 0, :]), ALU.mult))
            st.then(nc.vector.tensor_scalar(sp_b, sp_b, -1.0, None, ALU.mult))
            st.then(nc.vector.tensor_copy(da[:, HI, :], sp_b))
            nc.vector.tensor_tensor(da[:, LO, :], sp_b, da[:, HI, :].bitcast(F32), ALU.subtract).then_inc(dt_ready, 1)
            for i in (XB, ZA, ZB):
                split_w_lo(dve, b, i)

            for i in (BC, XA, XB):
                convolve(dve, st, b, i)
                silu(dve, b, i)
            vector_block(dve, st, b)
            with dve.Fori(0, NG - 1) as g:
                st.enter(g, 0, STEPS_PER_GROUP)
                for k in range(1, NQ + 1):
                    vector_block(dve, st, At(g, k))
                st.leave(NG - 1)
            for k in range(1, NQ):
                vector_block(dve, st, At(NG - 1, k))
            b = At(NG - 1, NQ - 1)
            split_y_lo(dve, b)
            dve.wait_ge(chunk_done, BLOCKS * QT + 1)
            mean_square(dve)
            for i in range(QT):
                add_out(dve, b, i)

        @block2.gpsimd
        def _(pool):
            for p in (HI, LO):
                nc.gpsimd.memset(w_grp[p][:, ZB, :, :].bitcast(F32), 0.0).then_inc(w_dt_cleared, 1)
            pool.wait_ge(dtw_in, 16 * 6)
            for t in range(NT):
                pool.wait_ge(mid.xn_ready, t + 1)
                nc.gpsimd.tensor_tensor(xres[:, t, :], xres[:, t, :], b_out_all[:], ALU.add).then_inc(b_out_added, 1)
            st = Steps(pool, pool_step)
            pool.wait_ge(dt_ready, 1)
            b = At(0, 0)
            pool_dt(pool, b)
            pool_segments(pool, b, 0)
            pool_segments(pool, b, 1)
            pool_block(pool, st, b)
            with pool.Fori(0, NG - 1) as g:
                st.enter(g, 0, POOL_STEPS_PER_GROUP)
                for k in range(1, NQ + 1):
                    pool_block(pool, st, At(g, k))
                st.leave(NG - 1)
            for k in range(1, NQ):
                pool_block(pool, st, At(NG - 1, k))
            pool.wait_ge(v_ready, BLOCKS)
            nc.gpsimd.tensor_tensor(rs_grp[:], v_grp[:], minus_half[:, 0:QT], ALU.pow).then_inc(rs_ready, 1)

        @block2.tensor
        def _(pe):
            pe.sem_inc(out_done, 1)

            def dt_products(q):
                pe.wait_ge(w_dt_split, 1)
                pe.wait_ge(mid.xt_used, (q + 1) * QT)
                for k in range(KD):
                    for n, (pw, px) in enumerate(((HI, HI), (HI, LO), (LO, HI))):
                        last = nc.tensor.matmul(banks[4 + q][:], w_dt[pw][:, k, :], xn[px][:, k, q * BLK:(q + 1) * BLK],
                                                start=(k == 0 and n == 0), stop=(k == KD - 1 and n == 2))
                last.then_inc(dt_done, 1)

            for q in range(NQ):
                for t in range(q * QT, (q + 1) * QT):
                    norm_turn(pe, mid, t)
                if q:
                    dt_products(q - 1)
            dt_products(NQ - 1)
            for t in range(NT):
                pe.wait_ge(dt_taken, t // QT + 1)
                last = nc.tensor.transpose(banks[4][:, t * NH:(t + 1) * NH], dt_T[t // QT][:, (t % QT) * P:(t % QT + 1) * P],
                                           ident[0:NH, 0:NH])
            last.then_inc(dt_turned, 1)
            b = At(0, 0)
            for i in range(IN_TILES):
                in_tile(pe, b, i)
            tensor_block(pe, b)
            with pe.Fori(0, NG - 1) as g:
                for k in range(1, NQ + 1):
                    tensor_block(pe, At(g, k))
            for k in range(1, NQ):
                tensor_block(pe, At(NG - 1, k))
            b = At(NG - 1, NQ - 1)
            pe.wait_ge(state_ready, BLOCKS * QT)
            sum_squares(pe, b).then_inc(chunk_done, 1)
            for i in range(QT):
                out_tile(pe, b, i)

        block2.__exit__(None, None, None)
        phase.close()

        phase = ExitStack()
        mixes[1].allocate(phase)
        block3 = nc.Block()
        block3.__enter__()

        @block3.sync
        def _(sp):
            mix_sync(sp, mixes[1], True, experts_again)

        @block3.scalar
        def _(act):
            mix_scalar(act, mixes[1])

        @block3.gpsimd
        def _(pool):
            mix_pool(pool, mixes[1])
            for t in range(NT):
                pick_pool(pool, mixes[1], t)

        @block3.vector
        def _(dve):
            st = Steps(dve, s_last)
            mix_vector(dve, st, mixes[1], lambda q: None)
            with dve.Fori(0, NQ) as q:
                st.enter(q, 0, QT)
                for i in range(QT):
                    pick_vector(dve, st, mixes[1], q, i)
                st.leave(NQ)

        @block3.tensor
        def _(pe):
            mix_tensor(pe, mixes[1])

        block3.__exit__(None, None, None)
        phase.close()


_INS = ["L0_attn_hidden_states", "L0_attn_W_in", "L0_attn_b_in", "L0_attn_conv_w", "L0_attn_conv_b", "L0_attn_A_log",
        "L0_attn_D_param", "L0_attn_dt_bias", "L0_attn_norm_w", "L0_attn_W_out", "L0_attn_b_out", "L0_attn_mup_vector",
        "L0_ffn_gate_w", "L0_ffn_expert_w", "L0_ffn_expert_b"]


def kernel(**inputs):
    import numpy as _np
    import concourse.bacc as _bacc
    from concourse import mybir as _mybir
    from concourse.bass_utils import run_bass_kernel_spmd as _run

    nc = _bacc.Bacc("TRN2", target_bir_lowering=False, num_devices=1)
    arrays, args = {}, []
    for name in _INS:
        a = _np.ascontiguousarray(inputs[name])
        arrays[f"in_{name}_dram"] = a
        args.append(nc.dram_tensor(f"in_{name}_dram", a.shape, _mybir.dt.from_np(a.dtype), kind="ExternalInput").ap())
    out = nc.dram_tensor("out_0_dram", inputs["L0_attn_hidden_states"].shape, _mybir.dt.float32, kind="ExternalOutput").ap()
    build(nc, *args, out)
    r = _run(nc, [arrays], core_ids=[0])
    return r.results[0]["out_0_dram"]
```

```python
from contextlib import ExitStack

import concourse.bass as bass
from concourse import mybir

P = 128
F32 = mybir.dt.float32
F32R = mybir.dt.float32r
F16 = mybir.dt.float16
I32 = mybir.dt.int32
U32 = mybir.dt.uint32
ALU = mybir.AluOpType
ACT = mybir.ActivationFunctionType
AX_X = mybir.AxisListType.X
ds = bass.ds

D = 512
KD = D // P
TOKENS = 2 * 1024
NT = TOKENS // P
QT = 4
NQ = NT // QT
BLK = QT * P
NE = 8
MAX_SLOT_TILES = 2 * NT + NE - 1
PAIR = 2
HOT = 8
U = 3
SLOT_LOOPS = MAX_SLOT_TILES // U
assert SLOT_LOOPS * U == MAX_SLOT_TILES

NH, HD, NG, NS = 32, 64, 8, 32
GH = NH // NG
D_SSM = NH * HD
GC = D_SSM // NG
CT = GC // P
X0 = D_SSM
B0 = 2 * D_SSM
C0 = B0 + NG * NS
DT0 = C0 + NG * NS
TAPS = 4
PAD = TAPS - 1
EPS = 1e-5
IN_TILES = 5
BC, XA, XB, ZA, ZB = range(IN_TILES)
HALVES = 2
BLOCKS = NG * NQ
STEPS_PER_GROUP = 48
POOL_STEPS_PER_GROUP = NQ * QT

P_BX, P_MX, P_CB, P_D, P_NW, P_BZ, P_MZ, P_HBZ, P_HMZ, P_LM, P_LB, P_TAP = range(12)
NPAR = P_TAP + TAPS
Q_B, Q_M, Q_CB, Q_TAP = range(4)
Q_LM = Q_TAP + TAPS
Q_LB = Q_LM + 1
NPARB = Q_LB + 1


class Steps:

    def __init__(self, engine, sem):
        self.engine, self.sem, self.n, self.turn = engine, sem, 0, None

    def did(self, ins):
        ins.then_inc(self.sem, 1)
        self.n += 1
        return self.value()

    def value(self):
        return self.n if self.turn is None else self.turn + self.n

    def wait(self, value=None):
        self.engine.wait_ge(self.sem, self.value() if value is None else value)

    def then(self, ins):
        self.did(ins)
        self.wait()

    def enter(self, i, first, per):
        self.turn, self.start, self.per = (i - first) * per, self.n, per

    def leave(self, turns):
        assert self.n - self.start == self.per, (self.n - self.start, self.per)
        self.n, self.turn = self.start + turns * self.per, None


def build(nc, hidden, w_in, b_in, conv_w, conv_b, a_log, d_param, dt_bias, norm_w, w_out, b_out,
          mup, gate_w, expert_w, expert_b, out):
    ctx = ExitStack()
    with ctx:
        def sb(name, shape, dt=F32):
            return ctx.enter_context(nc.sbuf_tensor(name, shape, dt))

        def sem(name):
            return ctx.enter_context(nc.semaphore(name))

        x_rows = hidden.rearrange("b l d -> (b l) d").rearrange("(t p) d -> p t d", p=P)
        out_rows = out.rearrange("b l d -> (b l) d").rearrange("(t p) d -> p t d", p=P)
        xn_rows = nc.dram_tensor("xn_rows", [TOKENS, D], F32)
        slots_out = nc.dram_tensor("slots_out", [MAX_SLOT_TILES * P, D], F32)
        w_in_rows = w_in.rearrange("(k p) n -> p k n", p=P)
        w_out_rows = w_out.rearrange("(g c p) n -> g p c n", c=CT, p=P)

        banks = [ctx.enter_context(nc.psum_tensor(f"bank{i}", [P, 512], F32)) for i in range(8)]
        xres = sb("xres", [P, NT, D])
        ident = sb("ident", [P, P])
        ones = sb("ones", [P, P])
        le = sb("le", [P, P])
        le_half = sb("le_half", [P, P])
        minus_half = sb("minus_half", [P, NT])
        gw_T = sb("gw_T", [P, KD, NE])
        iota_e = sb("iota_e", [P, NE])
        tile_start = sb("tile_start", [P, MAX_SLOT_TILES])
        par = sb("par", [P, NPAR, NG * CT])
        parb = sb("parb", [P, NPARB, NG])
        iota_p = sb("iota_p", [P, P])
        token_id = sb("token_id", [P, NT])
        stats = sb("stats", [P, QT, 6])
        mean_var = sb("mean_var", [P, QT, 2])
        mean = sb("mean", [P, NT])
        tile_stats = sb("tile_stats", [P, NT, 6])
        tile_mean_var = sb("tile_mean_var", [P, NT, 2])
        var_eps = sb("var_eps", [P, NT])
        rstd = sb("rstd", [P, NT])

        HI, LO = range(2)
        THREE = ((HI, HI), (HI, LO), (LO, HI))

        s_dve, s_pool, a_exp = sem("dve_step"), sem("pool_step"), sem("a_exp")
        waited = sem("waited")
        s_added = sem("first_choice_added")
        s_mix, s_last = sem("dve_mixer_step"), sem("dve_last_step")
        x_in = [sem(f"x_in{q}") for q in range(NQ)]
        gate_in, bias_in = sem("gate_in"), sem("bias_in")
        rows_in, dtw_in = sem("rows_in"), sem("dtw_in")
        masks_made = sem("masks_made")
        d_wide, params_T, params_made, gate_T, gate_ready = (
            sem("d_wide"), sem("params_T"), sem("params_made"), sem("gate_T"), sem("gate_ready"))

        class Norm:

            def __init__(self, n):
                self.var_ready = sem(f"{n}_var_ready")
                self.rstd_ready = sem(f"{n}_rstd_ready")
                self.xn_ready = sem(f"{n}_xn_ready")
                self.turned = sem(f"{n}_xn_turned")
                self.xt_ready = sem(f"{n}_xt_ready")
                self.xt_used = sem(f"{n}_xt_used")
                if n != "mid":
                    self.stored = [sem(f"{n}_xn_stored{h}") for h in range(2)]

        both_w_in = [sem(f"w_in{e}") for e in range(NE)]
        both_xg_in = [sem(f"xg_in{u}") for u in range(U)]
        both_y_out = [sem(f"y_out{u}") for u in range(U)]
        both_y_in = [sem(f"y_in{i}") for i in range(QT)]

        class Mix:

            def __init__(self, n, turn):
                self.w_in, self.xg_in, self.y_out, self.y_in = both_w_in, both_xg_in, both_y_out, both_y_in
                self.w_before = turn * 16
                self.xg_before = turn * 16 * SLOT_LOOPS
                self.y_out_before = turn * 16 * (SLOT_LOOPS + 1)
                self.y_in_before = turn * 32 * NQ
                self.name, self.norm = n, Norm(n)
                self.gate_taken = sem(f"{n}_gate_taken")
                self.logits_done = sem(f"{n}_logits_done")
                self.best_ready = sem(f"{n}_best_ready")
                self.gate_exp = sem(f"{n}_gate_exp")
                self.sent_ready = sem(f"{n}_sent_ready")
                self.ranks_done = sem(f"{n}_ranks_done")
                self.map_ready = sem(f"{n}_map_ready")
                self.parts_ready = sem(f"{n}_parts_ready")
                self.tile_ready = sem(f"{n}_tile_ready")
                self.low_ready = sem(f"{n}_low_ready")
                self.high_ready = sem(f"{n}_high_ready")
                self.w_hi_made = sem(f"{n}_w_hi_made")
                self.w_lo_made = sem(f"{n}_w_lo_made")
                self.xg_hi = sem(f"{n}_xg_hi")
                self.table_done = sem(f"{n}_table_done")
                self.table_ready = sem(f"{n}_table_ready")
                self.turned = sem(f"{n}_turned")
                self.xg_ready = sem(f"{n}_xg_ready")
                self.product_done = sem(f"{n}_product_done")
                self.y_ready = sem(f"{n}_y_ready")
                self.picked = sem(f"{n}_picked")
                self.stored = sem(f"{n}_stored")

            def allocate(self, stack):
                def sb(name, shape, dt=F32, stack=stack):
                    return stack.enter_context(nc.sbuf_tensor(f"{self.name}_{name}", shape, dt))

                with ExitStack() as early:
                    self.w_raw = sb("w_raw", [P, NE * KD * D], F32, early)
                w_lo = sb("w_lo", [P, NE * KD * D], F32R)
                self.w = [sb("w_hi", [P, NE * KD * D], F32R), w_lo]
                self.eb = sb("eb", [P, NE * D])
                self.logits_T = [self.eb[0:NE, (NQ + q) * BLK:(NQ + q + 1) * BLK] for q in range(NQ)]
                self.slot_part_i = sb("slot_part_i", [P, 2, 2, NT], U32)
                self.slot_part = sb("slot_part", [P, 2, 2, NT])
                self.table = sb("table", [P, MAX_SLOT_TILES], U32)
                self.zeros = sb("zeros", [P, NT])
                self.lt = sb("lt", [P, P])
                self.total = sb("total", [P, 4, NE])
                self.total_i = sb("total_i", [P, 2, NE], I32)
                self.bounds = sb("bounds", [P, 1 + NE])
                self.slot_f = sb("slot_f", [P, 2, NT])
                self.slot_i = sb("slot_i", [P, 2, NT], U32)
                self.emap = sb("emap", [P, MAX_SLOT_TILES])
                self.emap_i = sb("emap_i", [P, MAX_SLOT_TILES], I32)
                self.gates = sb("gates", [P, 2, NT])
                self.gate_e = sb("gate_e", [P, 3, NT])
                with ExitStack() as early:
                    self.xn = sb("xn", [P, 2, QT, D], F32, early)
                    self.norm.slots = [self.xn[:, n // QT, n % QT, :] for n in range(2 * QT)]
                    self.xt = sb("xt", [P, 2, KD, PAIR * P], F32, early)
                with ExitStack() as early:
                    self.hot_low = sb("hot_low", [P, 2 * NT, P], F16, early)
                    self.hot_tile = sb("hot_tile", [P, 2 * NT, MAX_SLOT_TILES], F32, early)
                    self.hot_high = sb("hot_high", [P, 2 * NT, MAX_SLOT_TILES], F16, early)
                    hot_words = NT * P + 3 * NT * MAX_SLOT_TILES
                    sb("to_xt", [P, 2 * QT * D - hot_words], F32, early)
                    self.logits = sb("logits", [P, NT, NE], F32, early)
                    self.best = sb("best", [P, NT, 8], F32, early)
                    self.best_at = sb("best_at", [P, NT, 8], U32, early)
                    self.pick = sb("pick", [P, 2, NT], F32, early)
                    self.one_hot = sb("one_hot", [P, 2, NT, NE], F32, early)
                    self.sent = sb("sent", [P, NT, NE], F32, early)
                    self.rank = sb("rank", [P, NT, NE], F32, early)
                    self.counts = sb("counts", [P, NE, NT], F32, early)
                    self.offsets = sb("offsets", [P, NE, NT], F32, early)
                with ExitStack() as early:
                    self.xg = sb("xg", [P, U, D], F32, early)
                    self.xg_T = [sb(f"xg_T_{p}", [P, U, KD, P], F32R, early) for p in ("hi", "lo")]
                    self.y_sb = sb("y_sb", [P, U, D], F32, early)
                self.y_pick = sb("y_pick", [P, QT, 2, D])

        mixes = [Mix("mix1", 0), Mix("mix2", 1)]
        mid = Norm("mid")
        dt_done, dt_taken, dt_turned, w_dt_cleared, soft_in, soft_exp, soft_ln, dt_ready = (
            sem("dt_done"), sem("dt_taken"), sem("dt_turned"), sem("w_dt_cleared"),
            sem("soft_in"), sem("soft_exp"), sem("soft_ln"), sem("dt_ready"))

        w_loaded = [sem(f"w_loaded{i}") for i in range(IN_TILES)]
        w_hi_made, w_split = sem("w_hi_made"), sem("w_split")
        wo_loaded, wo_hi_made, wo_split = sem("wo_loaded"), sem("wo_hi_made"), sem("wo_split")
        w_dt_hi, w_dt_split, b_out_added = sem("w_dt_hi"), sem("w_dt_split"), sem("b_out_added")
        last_kept, bank4_cleared = sem("last_kept"), sem("bank4_cleared")
        y_hi_made, y_split, sq_added = sem("y_hi_made"), sem("y_split"), sem("sq_added")
        dt_blk_made, dec_ready, pool_step = sem("dt_blk_made"), sem("dec_ready"), sem("pool_mixer_step")
        in_done, in_taken = sem("in_done"), sem("in_taken")
        conv_done, tanh_done, silu_done = sem("conv_done"), sem("tanh_done"), sem("silu_done")
        c_rep_made = sem("c_rep_made")
        r_made, da_rep_made = sem("r_made"), sem("da_rep_made")
        seg_done, turn_done, g_done = sem("seg_done"), sem("turn_done"), sem("g_done")
        decay_ready, tok_ready = sem("decay_ready"), sem("tok_ready")
        weights_ready = sem("weights_ready")
        chunk_done, state_ready = sem("chunk_done"), sem("state_ready")
        z_done, y_ready, sq_ready = sem("z_done"), sem("y_ready"), sem("sq_ready")
        v_ready, rs_ready = sem("v_ready"), sem("rs_ready")
        out_done, out_added = sem("out_done"), sem("out_added")

        def norm_stats(dve, st, nm, q):
            for i in range(QT):
                st.did(nc.vector.bn_stats(stats[:, i, :], xres[:, q * QT + i, :]))
            st.wait()
            for i in range(QT):
                st.did(nc.vector.bn_aggr(mean_var[:, i, :], stats[:, i, :]))
            st.wait()
            block = slice(q * QT, (q + 1) * QT)
            st.did(nc.vector.tensor_copy(mean[:, block], mean_var[:, :, 0]))
            nc.vector.tensor_scalar(var_eps[:, block], mean_var[:, :, 1], EPS, None, ALU.add).then_inc(nm.var_ready, 1)

        def norm_apply(dve, nm, q):
            dve.wait_ge(nm.rstd_ready, q + 1)
            for i in range(QT):
                t = q * QT + i
                if t >= 2 * QT:
                    dve.wait_ge(nm.turned, t - 2 * QT + 1)
                    if nm is not mid:
                        dve.wait_ge(nm.stored[q % 2], 16)
                nc.vector.tensor_scalar(nm.slots[t % (2 * QT)], xres[:, t, :], mean[:, t:t + 1], rstd[:, t:t + 1],
                                        ALU.subtract, ALU.mult).then_inc(nm.xn_ready, 1)

        def norm_rstd(pool, nm, q):
            pool.wait_ge(nm.var_ready, q + 1)
            nc.gpsimd.tensor_tensor(rstd[:, q * QT:(q + 1) * QT], var_eps[:, q * QT:(q + 1) * QT], minus_half[:, 0:QT], ALU.pow
                                    ).then_inc(nm.rstd_ready, 1)

        def norm_turn(pe, nm, t):
            pe.wait_ge(nm.xn_ready, t + 1)
            if t >= QT:
                if nm is mid:
                    pe.wait_ge(nm.xt_used, t - QT + 1)
                else:
                    pe.wait_ge(nm.xt_ready, t - QT + 1)
            for k in range(KD):
                last = nc.tensor.transpose(banks[t % QT][:, k * P:(k + 1) * P], nm.slots[t % (2 * QT)][:, k * P:(k + 1) * P], ident[:])
            last.then_inc(nm.turned, 1)

        turn_banks, out_banks = [banks[0], banks[1], banks[7]], [banks[4], banks[5], banks[6]]

        def load_expert(sp, m, e):
            sp.dma_start(m.w_raw[:, e * KD * D:(e + 1) * KD * D].rearrange("p (k o) -> p k o", k=KD),
                         expert_w[e].rearrange("(k p) o -> p k o", p=P)).then_inc(m.w_in[e], 16)

        def mix_sync(sp, m, last):
            nm = m.norm
            for q in range(NQ):
                for e in {0: (0,), 2: (1, 2, 3)}.get(q, ()):
                    load_expert(sp, m, e)
                sp.wait_ge(nm.xn_ready, (q + 1) * QT)
                sp.dma_start(xn_rows[q * BLK:(q + 1) * BLK, :].rearrange("(t p) d -> p t d", p=P), m.xn[:, q % 2, :, :]
                             ).then_inc(nm.stored[q % 2], 16)

            def store(i, u):
                sp.wait_ge(m.y_ready, U + i * U + u + 1)
                sp.dma_start(slots_out[ds((i * U + u) * P, P), :], m.y_sb[:, u, :]).then_inc(m.y_out[u], 16)

            for e in range(4, NE):
                load_expert(sp, m, e)
            sp.wait_ge(m.logits_done, 1)
            if m is mixes[0]:
                sp.wait_ge(params_T, 1)
            sp.dma_start(m.eb[:], expert_b.rearrange("e d -> (e d)").partition_broadcast(P)).then_inc(bias_in, 16)
            with sp.Fori(0, SLOT_LOOPS) as i:
                for u in range(U):
                    store(i, u)
            if last:
                ends = [QT, 2 * QT, 3 * QT] + list(range(3 * QT + 1, NT + 1))
                for a, e in zip([0] + ends, ends):
                    sp.wait_ge(m.picked, e)
                    sp.dma_start(out_rows[:, a:e, :], xres[:, a:e, :]).then_inc(m.stored, 16)
                sp.wait_ge(m.stored, 16 * len(ends))

        def mix_tensor(pe, m, after_logits=None):
            nm = m.norm

            def gate(h):
                pe.wait_ge(nm.xt_ready, (h + 1) * PAIR)
                if h >= 2:
                    pe.wait_ge(m.gate_taken, h - 1)
                for k in range(KD):
                    last = nc.tensor.matmul(banks[4 + h % 2][0:NE, 0:PAIR * P], gw_T[:, k, :], m.xt[:, h % 2, k, :],
                                            start=(k == 0), stop=(k == KD - 1))
                last.then_inc(nm.xt_used, 1)

            def gate_turn(h):
                pe.wait_ge(m.gate_taken, h + 1)
                for t in range(h * PAIR, (h + 1) * PAIR):
                    last = nc.tensor.transpose(banks[6][:, t * NE:(t + 1) * NE], m.logits_T[t // QT][:, (t % QT) * P:(t % QT + 1) * P],
                                               ident[0:NE, 0:NE])
                return last

            pe.wait_ge(masks_made, 1)
            pe.wait_ge(gate_ready, 1)
            for h in range(NT // PAIR):
                for t in range(h * PAIR, (h + 1) * PAIR):
                    norm_turn(pe, nm, t)
                if h:
                    gate(h - 1)
                if h >= 2:
                    gate_turn(h - 2)
            gate_turn(NT // PAIR - 2)
            gate(NT // PAIR - 1)
            gate_turn(NT // PAIR - 1).then_inc(m.logits_done, 1)
            if after_logits:
                after_logits()
            pe.wait_ge(m.sent_ready, 1)
            flat = m.sent[:, :, :].rearrange("p t e -> p (t e)")
            nc.tensor.matmul(banks[3][:, 0:P], m.lt[:], flat, start=True, stop=True)
            nc.tensor.matmul(banks[3][:, P:2 * P], ones[:], flat, start=True, stop=True).then_inc(m.ranks_done, 1)
            for n in range(2 * NT):
                pe.wait_ge(m.low_ready, n // HOT + 1)
                pe.wait_ge(m.high_ready, n // NT + 1)
                last = nc.tensor.matmul(banks[2][:, 0:MAX_SLOT_TILES], m.hot_low[:, n, :], m.hot_high[:, n, :],
                                        start=(n == 0), stop=(n == 2 * NT - 1))
            last.then_inc(m.table_done, 1)


            def turn_slots(i, u):
                pe.wait_ge(m.xg_in[u], i * 16 + (m.xg_before + 16))
                pe.wait_ge(m.xg_ready, i * U + u + 1)
                for k in range(KD):
                    last = nc.tensor.transpose(turn_banks[u][:, k * P:(k + 1) * P], m.xg[:, u, k * P:(k + 1) * P], ident[:])
                last.then_inc(m.turned, 1)

            def expert(i, u):
                pe.wait_ge(m.xg_ready, U + i * U + u + 1)
                pe.wait_ge(m.y_ready, i * U + u + 1)
                e = pe.value_load(m.emap_i[0:1, ds(i * U + u, 1)], min_val=0, max_val=(NE - 1) * D)
                for k in range(KD):
                    for n, (px, pw) in enumerate(THREE):
                        last = nc.tensor.matmul(out_banks[u][:], m.xg_T[px][:, u, k, :], m.w[pw][:, ds(e * KD + k * D, D)],
                                                start=(k == 0 and n == 0), stop=(k == KD - 1 and n == 2))
                last.then_inc(m.product_done, 1)

            pe.sem_inc(m.turned, U)
            pe.sem_inc(m.product_done, U)
            turn_slots(0, 0)
            pe.wait_ge(m.map_ready, 1)
            if m is mixes[0]:
                pe.wait_ge(params_made, 1)
            pe.wait_ge(m.w_lo_made, NE)
            with pe.Fori(0, SLOT_LOOPS - 1) as i:
                for u in range(U):
                    turn_slots(i + (u + 1) // U, (u + 1) % U)
                    expert(i, u)
            n = SLOT_LOOPS - 1
            for u in range(U):
                if u < U - 1:
                    turn_slots(n, u + 1)
                expert(n, u)

        def mix_scalar(act, m):
            nm = m.norm
            def take_gate(h):
                act.wait_ge(nm.xt_used, h + 1)
                nc.scalar.copy(m.logits_T[h * PAIR // QT][:, h * PAIR % QT * P:(h * PAIR % QT + PAIR) * P],
                               banks[4 + h % 2][0:NE, 0:PAIR * P]).then_inc(m.gate_taken, 1)

            def w_hi(e, pieces=range(KD)):
                act.wait_ge(m.w_in[e], m.w_before + 16)
                where = slice((e * KD + pieces[0]) * D, (e * KD + pieces[-1] + 1) * D)
                nc.scalar.copy(m.w[HI][:, where], m.w_raw[:, where]).then_inc(m.w_hi_made, len(pieces))

            for h in range(NT // PAIR):
                for t in range(h * PAIR, (h + 1) * PAIR):
                    act.wait_ge(nm.turned, t + 1)
                    if h >= 2:
                        act.wait_ge(nm.xt_used, h - 1)
                    nc.scalar.copy(m.xt[:, h % 2, :, t % PAIR * P:(t % PAIR + 1) * P],
                                   banks[t % QT][:].rearrange("p (k t) -> p k t", k=KD)).then_inc(nm.xt_ready, 1)
                    if t >= 2 * QT:
                        w_hi(t // QT - 2, [t % QT])
                if h:
                    take_gate(h - 1)
            take_gate(NT // PAIR - 1)
            for e in (2, 3):
                w_hi(e)
            act.wait_ge(m.best_ready, 1)
            nc.scalar.activation(m.gate_e[:, 1, :], m.gate_e[:, 0, :], ACT.Exp).then_inc(m.gate_exp, 1)
            for e in range(4, NE):
                w_hi(e)
            with act.Fori(0, SLOT_LOOPS) as i:
                for u in range(U):
                    act.wait_ge(m.turned, U + i * U + u + 1)
                    act.wait_ge(m.product_done, i * U + u + 1)
                    nc.scalar.copy(m.xg_T[HI][:, u, :, :].rearrange("p k t -> p (k t)"), turn_banks[u][:]).then_inc(m.xg_hi, 1)

        def w_low(engine, m, e):
            where = slice(e * KD * D, (e + 1) * KD * D)
            return engine.tensor_tensor(m.w[LO][:, where], m.w_raw[:, where], m.w[HI][:, where].bitcast(F32), ALU.subtract)

        def mix_pool(pool, m):
            def pool_low(e):
                pool.wait_ge(m.w_hi_made, KD * (e + 1))
                w_low(nc.gpsimd, m, e).then_inc(m.w_lo_made, 1)

            for q in range(NQ):
                norm_rstd(pool, m.norm, q)
            pool_low(2)
            pool_low(3)
            for j in range(2):
                hot = m.hot_high[:, j * NT:(j + 1) * NT, :]
                pool.wait_ge(m.tile_ready, 1)
                nc.gpsimd.tensor_tensor(hot, m.hot_tile[:, j * NT:(j + 1) * NT, :],
                                        token_id[:, :, None].to_broadcast([P, NT, MAX_SLOT_TILES]), ALU.mult
                                        ).then_inc(m.high_ready, 1)
            pool_low(4)
            for h in range(2):
                pool.wait_ge(m.norm.stored[h], 16 * NQ // 2)
            pool.wait_ge(m.table_ready, 1)
            for n in range(MAX_SLOT_TILES):
                pool.wait_ge(m.turned, n + 1)
                nc.gpsimd.indirect_dma_start(m.xg[:, n % U, :], None, xn_rows[:, :],
                                             bass.IndirectOffsetOnAxis(m.table[:, n:n + 1], 0)).then_inc(m.xg_in[n % U], 16)

        def mix_vector(dve, st, m, block_ready, after_norm=None, after_table=None):
            nm = m.norm
            dve.wait_ge(masks_made, 1)
            st.did(nc.vector.tensor_tensor(m.lt[:], le[:], ident[:], ALU.subtract))
            st.did(nc.vector.memset(m.zeros[:], 0.0))
            block_ready(0)
            norm_stats(dve, st, nm, 0)
            for q in range(NQ):
                if q < NQ - 1:
                    block_ready(q + 1)
                    norm_stats(dve, st, nm, q + 1)
                norm_apply(dve, nm, q)
            if after_norm:
                after_norm()
            for e in (0, 1):
                dve.wait_ge(m.w_hi_made, KD * (e + 1))
                w_low(nc.vector, m, e).then_inc(m.w_lo_made, 1)
            dve.wait_ge(m.logits_done, 1)
            st.then(nc.vector.tensor_copy(m.logits[:, :, :].rearrange("p t e -> p (t e)"), banks[6][:, 0:NT * NE]))
            for t in range(NT):
                st.did(nc.vector.max(m.best[:, t, :], m.logits[:, t, :]))
            st.wait()
            for t in range(NT):
                st.did(nc.vector.max_index(m.best_at[:, t, :], m.best[:, t, :], m.logits[:, t, :]))
            nc.vector.tensor_tensor(m.gate_e[:, 0, :], m.best[:, :, 1], m.best[:, :, 0], ALU.subtract).then_inc(m.best_ready, 1)
            st.wait()
            st.then(nc.vector.tensor_copy(m.pick[:, :, :].rearrange("p j t -> p t j"), m.best_at[:, :, 0:2]))
            for j in range(2):
                st.did(nc.vector.tensor_tensor(m.one_hot[:, j, :, :], iota_e[:, None, :].to_broadcast([P, NT, NE]),
                                               m.pick[:, j, :, None].to_broadcast([P, NT, NE]), ALU.is_equal))
            st.wait()
            nc.vector.tensor_tensor(m.sent[:], m.one_hot[:, 0, :, :], m.one_hot[:, 1, :, :], ALU.add).then_inc(m.sent_ready, 1)
            dve.wait_ge(m.gate_exp, 1)
            st.then(nc.vector.tensor_scalar(m.gate_e[:, 2, :], m.gate_e[:, 1, :], 1.0, None, ALU.add))
            st.then(nc.vector.reciprocal(m.gate_e[:, 0, :], m.gate_e[:, 2, :]))
            st.did(nc.vector.tensor_scalar(m.gates[:, 0, :], m.gate_e[:, 0, :], 0.5, None, ALU.mult))
            st.did(nc.vector.scalar_tensor_tensor(m.gates[:, 1, :], m.gate_e[:, 0, :], 0.5, m.gate_e[:, 1, :], ALU.mult, ALU.mult))
            dve.wait_ge(m.ranks_done, 1)
            st.did(nc.vector.tensor_copy(m.rank[:, :, :].rearrange("p t e -> p (t e)"), banks[3][:, 0:P]))
            st.then(nc.vector.tensor_copy(m.counts[:], banks[3][:, P:2 * P].rearrange("p (t e) -> p e t", e=NE)))
            st.then(nc.vector.tensor_reduce(m.total[:, 0, :], m.counts[:], AX_X, ALU.add))
            st.then(nc.vector.tensor_scalar(m.total_i[:, 0, :], m.total[:, 0, :], float(P - 1), None, ALU.add))
            st.then(nc.vector.tensor_scalar(m.total_i[:, 1, :], m.total_i[:, 0, :], 7, 7, ALU.logical_shift_right, ALU.logical_shift_left))
            st.then(nc.vector.tensor_copy(m.total[:, 1, :], m.total_i[:, 1, :]))
            st.did(nc.vector.memset(m.bounds[:, 0:1], 0.0))
            st.then(nc.vector.memset(m.total[:, 2, :], 0.0))
            st.then(nc.vector.tensor_tensor_scan(m.bounds[:, 1:1 + NE], m.total[:, 1, :], m.total[:, 2, :], 0.0, ALU.add, ALU.add))
            for e in range(NE):
                st.did(nc.vector.tensor_tensor_scan(m.offsets[:, e, :], m.counts[:, e, :], m.zeros[:, 0:NT], m.bounds[:, e:e + 1],
                                                    ALU.add, ALU.add))
            st.wait()
            st.then(nc.vector.tensor_tensor(m.offsets[:], m.offsets[:], m.counts[:], ALU.subtract))
            st.then(nc.vector.tensor_tensor(m.rank[:], m.rank[:], m.offsets[:, :, :].rearrange("p e t -> p t e"), ALU.add))
            for j in range(2):
                st.did(nc.vector.tensor_tensor(m.one_hot[:, j, :, :], m.one_hot[:, j, :, :], m.rank[:], ALU.mult))
            st.wait()
            for j in range(2):
                st.did(nc.vector.tensor_reduce(m.slot_f[:, j, :], m.one_hot[:, j, :, :], AX_X, ALU.add))
            st.wait()
            st.then(nc.vector.tensor_copy(m.slot_i[:], m.slot_f[:]))
            st.did(nc.vector.tensor_scalar(m.slot_part_i[:, 0, :, :], m.slot_i[:], P - 1, None, ALU.bitwise_and))
            st.did(nc.vector.tensor_scalar(m.slot_part_i[:, 1, :, :], m.slot_i[:], 7, None, ALU.logical_shift_right))
            st.wait()
            for h in range(2):
                dve.wait_ge(nm.stored[h], 16 * NQ // 2)
            nc.vector.tensor_copy(m.slot_part[:], m.slot_part_i[:]).then_inc(m.parts_ready, 1)
            dve.wait_ge(m.parts_ready, 1)
            tile = m.slot_part[:, 1, :, :].rearrange("p j t -> p (j t)")
            nc.vector.tensor_tensor(m.hot_tile[:], iota_p[:, None, 0:MAX_SLOT_TILES].to_broadcast([P, 2 * NT, MAX_SLOT_TILES]),
                                    tile[:, :, None].to_broadcast([P, 2 * NT, MAX_SLOT_TILES]), ALU.is_equal).then_inc(m.tile_ready, 1)
            low = m.slot_part[:, 0, :, :].rearrange("p j t -> p (j t)")
            for n in range(0, 2 * NT, HOT):
                nc.vector.tensor_tensor(m.hot_low[:, n:n + HOT, :], iota_p[:, None, :].to_broadcast([P, HOT, P]),
                                        low[:, n:n + HOT, None].to_broadcast([P, HOT, P]), ALU.is_equal).then_inc(m.low_ready, 1)
            st.then(nc.vector.tensor_scalar(m.emap[:], tile_start[:], m.bounds[:, 1:2], None, ALU.is_ge))
            for e in range(1, NE):
                st.then(nc.vector.scalar_tensor_tensor(m.emap[:], tile_start[:], m.bounds[:, 1 + e:2 + e], m.emap[:], ALU.is_ge, ALU.add))
            nc.vector.tensor_scalar(m.emap_i[:], m.emap[:], float(NE - 1), float(D), ALU.min, ALU.mult).then_inc(m.map_ready, 1)
            dve.wait_ge(m.table_done, 1)
            nc.vector.tensor_copy(m.table[:], banks[2][:, 0:MAX_SLOT_TILES]).then_inc(m.table_ready, 1)
            if after_table:
                after_table()
            for e in (5, 6, 7):
                dve.wait_ge(m.w_hi_made, KD * (e + 1))
                w_low(nc.vector, m, e).then_inc(m.w_lo_made, 1)
            dve.sem_inc(m.y_ready, U)
            for u in range(U):
                dve.sem_inc(m.y_out[u], 16)
            dve.wait_ge(m.map_ready, 1)
            dve.wait_ge(bias_in, 16 if m is mixes[0] else 32)
            dve.sem_inc(m.xg_ready, U)

            def low(i, u):
                dve.wait_ge(m.xg_hi, i * U + u + 1)
                dve.wait_ge(m.product_done, i * U + u + 1)
                nc.vector.tensor_tensor(m.xg_T[LO][:, u, :, :].rearrange("p k t -> p (k t)"), turn_banks[u][:],
                                        m.xg_T[HI][:, u, :, :].rearrange("p k t -> p (k t)").bitcast(F32), ALU.subtract
                                        ).then_inc(m.xg_ready, 1)

            def result(i, u):
                dve.wait_ge(m.product_done, U + i * U + u + 1)
                dve.wait_ge(m.y_out[u], i * 16 + (m.y_out_before + 16))
                e = dve.value_load(m.emap_i[0:1, ds(i * U + u, 1)], min_val=0, max_val=(NE - 1) * D)
                nc.vector.tensor_tensor(m.y_sb[:, u, :], out_banks[u][:], m.eb[:, ds(e, D)], ALU.add).then_inc(m.y_ready, 1)

            low(0, 0)
            with dve.Fori(0, SLOT_LOOPS - 1) as i:
                for u in range(U):
                    low(i + (u + 1) // U, (u + 1) % U)
                    result(i, u)
            n = SLOT_LOOPS - 1
            for u in range(U):
                if u < U - 1:
                    low(n, u + 1)
                result(n, u)

        def pick_pool(pool, m, t):
            i, q = t % QT, t // QT
            if t == 0:
                for u in range(U):
                    pool.wait_ge(m.y_out[u], m.y_out_before + 16 * SLOT_LOOPS + 16)
            if q:
                pool.wait_ge(m.picked, t - QT + 1)
            for j in range(2):
                nc.gpsimd.indirect_dma_start(m.y_pick[:, i, j, :], None, slots_out[:, :],
                                             bass.IndirectOffsetOnAxis(m.slot_i[:, j, t:t + 1], 0)).then_inc(m.y_in[i], 16)

        def pick_add(dve, t, j):
            m = mixes[0]
            return nc.vector.scalar_tensor_tensor(xres[:, t, :], m.y_pick[:, t % QT, j, :], m.gates[:, j, t:t + 1], xres[:, t, :],
                                                  ALU.mult, ALU.add)

        def pick_vector(dve, st, m, q, i):
            row = xres[:, ds(q * QT + i, 1), :].rearrange("p a d -> p (a d)")
            dve.wait_ge(m.y_in[i], q * 32 + (m.y_in_before + 32))
            st.then(nc.vector.scalar_tensor_tensor(row, m.y_pick[:, i, 0, :], m.gates[:, 0, ds(q * QT + i, 1)], row, ALU.mult, ALU.add))
            nc.vector.scalar_tensor_tensor(row, m.y_pick[:, i, 1, :], m.gates[:, 1, ds(q * QT + i, 1)], row, ALU.mult, ALU.add
                                           ).then_inc(m.picked, 1)

        phase = ExitStack()
        m = mixes[0]
        m.allocate(phase)
        ROW_W = P
        ROW_BC = ROW_W + P * TAPS
        ROW_BCW = ROW_BC + 3 * P
        ROW_D = ROW_BCW + P * TAPS
        rows_a = m.eb[:, 0:P]
        rows_w = m.eb[:, ROW_W:ROW_W + P * TAPS]
        rows_bc = m.eb[:, ROW_BC:ROW_BC + 3 * P].rearrange("p (v n) -> p v n", v=3)
        rows_bcw = m.eb[:, ROW_BCW:ROW_BCW + P * TAPS]
        d_rows = m.eb[:, ROW_D:ROW_D + 2]
        rows_gate = m.eb[:, 2 * NQ * BLK - D:2 * NQ * BLK]
        block1 = nc.Block()
        block1.__enter__()

        @block1.sync
        def _(sp):
            for q in range(NQ):
                sp.dma_start(xres[:, q * QT:(q + 1) * QT, :], x_rows[:, q * QT:(q + 1) * QT, :]).then_inc(x_in[q], 16)
                if q == 0:
                    sp.dma_start(rows_gate[0:NE, :], gate_w).then_inc(gate_in, 16)
            mix_sync(sp, mixes[0], False)

        @block1.scalar
        def _(act):
            def rows(dst, src):
                act.dma_start(dst, src).then_inc(rows_in, 16)

            r = NG * CT
            for n, v in enumerate((b_in[X0:B0], b_in[0:X0], mup[X0:B0], mup[0:X0], conv_b[0:D_SSM], norm_w)):
                rows(rows_a[n * r:(n + 1) * r, :], v.rearrange("(r p) -> r p", p=P))
            rows(d_rows[96:96 + r, :], d_param.rearrange("(r h) -> r h", h=2))
            rows(rows_w[0:r, :], conv_w[0:D_SSM, :].rearrange("(r p) k -> r (p k)", p=P))
            for n, (v, o) in enumerate(((b_in, B0), (mup, B0), (conv_b, D_SSM))):
                rows(rows_bc[0:NG, n, 0:2 * NS].rearrange("g (s n) -> g s n", s=2),
                     v[o:o + 2 * NG * NS].rearrange("(s g n) -> g s n", s=2, g=NG))
                for c in (2, 3):
                    rows(rows_bc[0:NG, n, c * NS:(c + 1) * NS], v[o + NG * NS:o + 2 * NG * NS].rearrange("(g n) -> g n", g=NG))
            taps = conv_w[D_SSM:D_SSM + 2 * NG * NS, :]
            rows(rows_bcw[0:NG, 0:2 * NS * TAPS].rearrange("g (s n) -> g s n", s=2), taps.rearrange("(s g n) k -> g s (n k)", s=2, g=NG))
            for c in (2, 3):
                rows(rows_bcw[0:NG, c * NS * TAPS:(c + 1) * NS * TAPS], taps[NG * NS:, :].rearrange("(g n) k -> g (n k)", g=NG))

            mix_scalar(act, mixes[0])

        @block1.gpsimd
        def _(pool):
            nc.gpsimd.memset(ones[:], 1.0).then_inc(s_pool, 1)
            nc.gpsimd.memset(le_half[:], 0.5).then_inc(s_pool, 1)
            pool.wait_ge(s_pool, 2)

            def mask(dst, src, op, row, col):
                nc.gpsimd.affine_select(out=dst[:], in_=src[:], pattern=[[col, P]], compare_op=op, fill=0.0, base=0,
                                        channel_multiplier=row).then_inc(s_pool, 1)

            mask(ident, ones, ALU.is_equal, 1, -1)
            mask(le, ones, ALU.is_ge, -1, 1)
            mask(le_half, le_half, ALU.is_ge, -1, 1)
            nc.gpsimd.iota(iota_e[:], pattern=[[1, NE]], base=0, channel_multiplier=0, allow_small_or_imprecise_dtypes=True
                           ).then_inc(s_pool, 1)
            nc.gpsimd.iota(tile_start[:], pattern=[[P, MAX_SLOT_TILES]], base=0, channel_multiplier=0,
                           allow_small_or_imprecise_dtypes=True).then_inc(s_pool, 1)
            nc.gpsimd.memset(minus_half[:], -0.5).then_inc(s_pool, 1)
            nc.gpsimd.iota(iota_p[:], pattern=[[1, P]], base=0, channel_multiplier=0, allow_small_or_imprecise_dtypes=True
                           ).then_inc(s_pool, 1)
            nc.gpsimd.iota(token_id[:], pattern=[[P, NT]], base=0, channel_multiplier=1, allow_small_or_imprecise_dtypes=True
                           ).then_inc(s_pool, 1)
            pool.wait_ge(s_pool, 10)
            pool.sem_inc(masks_made, 1)
            mix_pool(pool, mixes[0])
            for t in range(NT):
                pick_pool(pool, mixes[0], t)

        @block1.vector
        def _(dve):
            st = Steps(dve, s_dve)
            dve.wait_ge(gate_T, 1)
            nc.vector.tensor_copy(gw_T[:], banks[0][:, 0:KD * NE].rearrange("p (k e) -> p k e", k=KD)).then_inc(gate_ready, 1)

            def widen_d():
                dve.wait_ge(rows_in, 16 * 20)
                nc.vector.tensor_copy(rows_a[96:96 + NG * CT, :].rearrange("r (h c) -> r h c", h=2),
                                      d_rows[96:96 + NG * CT, :, None].to_broadcast([NG * CT, 2, HD])).then_inc(d_wide, 1)

            def parameters():
                dve.wait_ge(params_T, 1)
                r = NG * CT

                def col(n):
                    return banks[5][:, n * r:(n + 1) * r]

                st.did(nc.vector.tensor_copy(par[:, P_MX, :], col(2)))
                st.did(nc.vector.tensor_copy(par[:, P_MZ, :], col(3)))
                st.did(nc.vector.tensor_copy(par[:, P_CB, :], col(4)))
                st.did(nc.vector.tensor_scalar(par[:, P_NW, :], col(5), 0.5, None, ALU.mult))
                st.did(nc.vector.tensor_scalar(par[:, P_D, :], col(6), 0.5, None, ALU.mult))
                st.did(nc.vector.tensor_scalar(par[:, P_HMZ, :], col(3), 0.5, None, ALU.mult))
                for k in range(TAPS):
                    st.did(nc.vector.tensor_copy(par[:, P_TAP + k, :], col(7 + k)))
                o = 11 * r
                st.did(nc.vector.tensor_copy(parb[:, 0:Q_LM, :].rearrange("p v g -> p (v g)"), banks[5][:, o:o + Q_LM * NG]))
                st.wait()
                st.did(nc.vector.tensor_tensor(par[:, P_BX, :], col(0), par[:, P_MX, :], ALU.mult))
                st.did(nc.vector.tensor_tensor(par[:, P_BZ, :], col(1), par[:, P_MZ, :], ALU.mult))
                st.did(nc.vector.tensor_tensor(parb[:, Q_B, :], parb[:, Q_B, :], parb[:, Q_M, :], ALU.mult))
                last = TAPS - 1
                st.did(nc.vector.tensor_tensor(par[:, P_LM, :], par[:, P_TAP + last, :], par[:, P_MX, :], ALU.mult))
                st.did(nc.vector.tensor_tensor(parb[:, Q_LM, :], parb[:, Q_TAP + last, :], parb[:, Q_M, :], ALU.mult))
                st.wait()
                st.did(nc.vector.tensor_tensor(par[:, P_LB, :], par[:, P_TAP + last, :], par[:, P_BX, :], ALU.mult))
                st.then(nc.vector.tensor_tensor(parb[:, Q_LB, :], parb[:, Q_TAP + last, :], parb[:, Q_B, :], ALU.mult))
                st.did(nc.vector.tensor_tensor(par[:, P_LB, :], par[:, P_LB, :], par[:, P_CB, :], ALU.add))
                st.did(nc.vector.tensor_tensor(parb[:, Q_LB, :], parb[:, Q_LB, :], parb[:, Q_CB, :], ALU.add))
                st.wait()
                nc.vector.tensor_scalar(par[:, P_HBZ, :], par[:, P_BZ, :], 0.5, None, ALU.mult).then_inc(params_made, 1)

            mix_vector(dve, st, mixes[0], lambda q: dve.wait_ge(x_in[q], 16), widen_d, parameters)

            for t in range(NT):
                dve.wait_ge(m.y_in[t % QT], t // QT * 32 + m.y_in_before + 32)
                pick_add(dve, t, 0).then_inc(s_added, 1)
                if t:
                    dve.wait_ge(m.picked, t)
                    st.did(nc.vector.bn_stats(tile_stats[:, t - 1, :], xres[:, t - 1, :]))
                dve.wait_ge(s_added, t + 1)
                pick_add(dve, t, 1).then_inc(m.picked, 1)
            dve.wait_ge(m.picked, NT)
            st.then(nc.vector.bn_stats(tile_stats[:, NT - 1, :], xres[:, NT - 1, :]))
            for t in range(NT):
                st.did(nc.vector.bn_aggr(tile_mean_var[:, t, :], tile_stats[:, t, :]))
            st.wait()
            st.did(nc.vector.tensor_copy(mean[:], tile_mean_var[:, :, 0]))
            st.did(nc.vector.tensor_scalar(var_eps[:], tile_mean_var[:, :, 1], EPS, None, ALU.add))
            st.wait()

        @block1.tensor
        def _(pe):
            pe.wait_ge(masks_made, 1)
            pe.wait_ge(gate_in, 16)
            for k in range(KD):
                last = nc.tensor.transpose(banks[0][:, k * NE:(k + 1) * NE], rows_gate[0:NE, k * P:(k + 1) * P], ident[0:NE, 0:NE])
            last.then_inc(gate_T, 1)
            def parameters():
                pe.wait_ge(d_wide, 1)
                r = NG * CT
                nc.tensor.transpose(banks[5][:, 0:7 * r], rows_a[0:7 * r, :], ident[0:7 * r, 0:7 * r])
                for k in range(TAPS):
                    nc.tensor.transpose(banks[5][:, (7 + k) * r:(8 + k) * r],
                                        rows_w[0:r, :].rearrange("r (p k) -> r p k", k=TAPS)[:, :, k], ident[0:r, 0:r])
                o = 11 * r
                for n in range(3):
                    nc.tensor.transpose(banks[5][:, o + n * NG:o + (n + 1) * NG], rows_bc[0:NG, n, :], ident[0:NG, 0:NG])
                o += 3 * NG
                for k in range(TAPS):
                    last = nc.tensor.transpose(banks[5][:, o + k * NG:o + (k + 1) * NG],
                                               rows_bcw[0:NG, :].rearrange("g (n k) -> g n k", k=TAPS)[:, :, k], ident[0:NG, 0:NG])
                last.then_inc(params_T, 1)

            mix_tensor(pe, mixes[0], parameters)

        block1.__exit__(None, None, None)
        phase.close()

        phase = ExitStack()

        def sb(name, shape, dt=F32):
            return phase.enter_context(nc.sbuf_tensor(name, shape, dt))

        xn = [sb(f"xn_{p}", [P, KD, TOKENS], F32R) for p in ("hi", "lo")]
        w_raw = sb("w_raw", [P, 2, KD, P])
        w_grp = [sb(f"w_{p}", [P, IN_TILES, KD, P], F32R) for p in ("hi", "lo")]
        wo_raw = w_raw[:, :, :, :].rearrange("p a k n -> p (a k n)").rearrange("p (c d) -> p c d", c=CT)
        wo = [sb(f"wo_{p}", [P, CT, D], F32R) for p in ("hi", "lo")]
        y_part = [sb(f"y_{p}", [P, CT, BLK], F32R) for p in ("hi", "lo")]
        gt_r = sb("gt_r", [P, P], F32R)
        le_r = sb("le_r", [P, P], F32R)
        dt_all = sb("dt_all", [P, NG * NT * GH])
        da = sb("da", [P, 2, NG * NT * GH], F32R)
        da_rep = sb("da_rep", [P, 2, 2, GH, NS], F32R)
        r_seg = sb("r_seg", [P, 2, 2, GH, P], F32R)
        x_raw = sb("x_raw", [P, CT, PAD + BLK])
        bc_raw = sb("bc_raw", [P, PAD + BLK])
        no_steps = sb("no_steps", [P, PAD])
        x_c = sb("x_c", [P, 2, CT, BLK])
        bc_c = sb("bc_c", [P, 2, BLK])
        th_x = sb("th_x", [P, BLK])
        th_z = sb("th_z", [P, CT, BLK])
        z_c = sb("z_c", [P, 2, CT, BLK])
        c_rep = sb("c_rep", [P, 2, BLK])
        decay = sb("decay", [P, GH, P])
        wts = sb("wts", [P, GH, P])
        g_m = sb("g_m", [P, P])
        x_tok = sb("x_tok", [P, GC + NS])
        e_cum = sb("e_cum", [P, 2, P])
        c_dec = sb("c_dec", [P, P])
        w_dec = sb("w_dec", [P, GH])
        b_dec = sb("b_dec", [P, GH, NS])
        state = sb("state", [P, GC])
        dt_blk = sb("dt_blk", [P, 2, QT * GH])
        v_grp = sb("v_grp", [P, QT])
        rs_grp = sb("rs_grp", [P, QT])
        mid.slots = [buf[:, n // CT, n % CT, :] for buf in (z_c, x_c) for n in range(2 * CT)]
        b_out_all = th_x
        w_dt_raw = wts[:, :, 0:NH]
        w_dt = [w[:, ZB, :, :] for w in w_grp]
        dt_T = [th_z[0:NH, 0, :], th_z[0:NH, 1, :], x_raw[0:NH, 0, 0:BLK], x_raw[0:NH, 1, 0:BLK]]
        dt_vec = decay[:, :, 0:NH]
        sp_a, sp_d = z_c[:, 0, 0, :], z_c[:, 0, 1, :]
        sp_b, sp_c = th_z[:, 0, :], th_z[:, 1, :]

        class At:
            def __init__(self, g, k):
                self.g, self.k = g, k
                self.grp = g + k // NQ
                self.tb = k % NQ
                self.half = self.tb % HALVES
                self.par = self.tb % 2
                self.n = g * NQ + k if isinstance(g, int) else None
                self.first, self.last = self.n == 0, self.n == BLOCKS - 1

            def before(self, n):
                return self.n is not None and self.n < n

            def plus(self, d):
                return At(self.g, self.k + d)

            def count(self, per, extra=0):
                assert isinstance(self.g, int) or self.k * per + extra > 0, "a wait for zero at the first group"
                return self.g * (per * NQ) + (self.k * per + extra)

            def in_group(self, per, extra):
                assert isinstance(self.g, int) or self.k // NQ * per + extra > 0, "a wait for zero at the first group"
                return self.g * per + (self.k // NQ * per + extra)

        def in_slot(c):
            return [(BC, XA), (XB,), (ZA,), (ZB,)][c]

        def split_slot(b, c):
            if b.n is not None and b.n // NQ == NG - 1:
                return ()
            if b.tb == NQ - 2:
                return [(), (BC, XA), (XB,), (ZA,)][c]
            return (ZB,) if b.tb == NQ - 1 and c == 0 else ()

        def in_tile(pe, b, i):
            if b.tb == 0:
                pe.wait_ge(w_split, b.in_group(IN_TILES, i + 1))
            if not (b.first and i < 2):
                pe.wait_ge(in_taken, b.count(IN_TILES, i - 1))
            dst = banks[(b.k * IN_TILES + i) % 2]
            for k in range(KD):
                for n, (pw, px) in enumerate(THREE):
                    last = nc.tensor.matmul(dst[:], w_grp[pw][:, i, k, :], xn[px][:, k, b.tb * BLK:(b.tb + 1) * BLK],
                                            start=(k == 0 and n == 0), stop=(k == KD - 1 and n == 2))
            last.then_inc(in_done, 1)

        def chunk_start(pe, b, c):
            if c == 0:
                pe.wait_ge(silu_done, b.count(3, 3))
                pe.wait_ge(c_rep_made, b.count(1, 1))
            t = slice(c * P, (c + 1) * P)
            pe.wait_ge(r_made, b.count(QT, c + 1))
            if not (b.first and c == 0):
                pe.wait_ge(decay_ready, b.count(QT, c))
            for p in (HI, LO):
                last = nc.tensor.matmul(banks[2][:], gt_r[:], r_seg[:, c % 2, p, :, :].rearrange("p h t -> p (h t)"),
                                        start=(p == HI), stop=(p == LO))
            last.then_inc(seg_done, 1)
            if not (b.first and c == 0):
                pe.wait_ge(tok_ready, b.count(QT, c))
            pe.wait_ge(da_rep_made, b.count(QT, c + 1))
            for p in (HI, LO):
                nc.tensor.matmul(banks[3][:, 0:P], da_rep[:, c % 2, p, :, :].rearrange("p h n -> p (h n)"),
                                 le_r[:], start=(p == HI), stop=(p == LO))
            for j in range(CT):
                nc.tensor.transpose(banks[3][:, P + j * P:P + (j + 1) * P], x_c[:, b.par, j, t], ident[:])
            nc.tensor.transpose(banks[3][:, P + GC:P + GC + NS], bc_c[0:NS, b.par, t], ident[0:NS, 0:NS]).then_inc(turn_done, 1)
            if not (b.first and c == 0):
                pe.wait_ge(state_ready, b.count(QT, c))
            nc.tensor.matmul(banks[4][:, 0:P], bc_c[0:NS, b.par, t], c_rep[0:NS, b.par, t],
                             start=True, stop=True).then_inc(g_done, 1)

        def chunk_end(pe, b, c):
            t = slice(c * P, (c + 1) * P)
            fresh = b.half == 0 and c == 0
            if c == 0 and not b.first:
                pe.wait_ge(y_ready, b.count(1))
            pe.wait_ge(dec_ready, b.count(QT, c + 1))
            pe.wait_ge(weights_ready, b.count(QT, c + 1))
            for j in range(CT):
                if not fresh:
                    nc.tensor.matmul(banks[5 + j][:, t], state[:, j * P:(j + 1) * P], c_dec[:], start=True, stop=True,
                                     skip_group_check=True)
                for h in range(2):
                    hh = 2 * j + h
                    nc.tensor.matmul(banks[5 + j][h * HD:(h + 1) * HD, t], x_tok[:, hh * HD:(hh + 1) * HD], wts[:, hh, :],
                                     start=fresh, stop=True, skip_group_check=True)
            for h in range(GH):
                last = nc.tensor.matmul(banks[4][h * NS:(h + 1) * NS, P + h * HD:P + (h + 1) * HD], b_dec[:, h, :],
                                        x_tok[:, h * HD:(h + 1) * HD], start=True, stop=True, skip_group_check=True)
            if c == 0 and not b.first:
                last = sum_squares(pe, b.plus(-1))
            last.then_inc(chunk_done, 1)

        def sum_squares(pe, b):
            pe.wait_ge(sq_added, b.count(1, 1))
            for i in range(QT):
                last = nc.tensor.matmul(banks[4][:, P + GC + i:P + GC + i + 1], z_c[:, b.par, 0, i * P:(i + 1) * P], ones[:, 0:1],
                                        start=True, stop=True)
            return last

        def out_tile(pe, b, i):
            if i == 0:
                if b.tb == 0:
                    pe.wait_ge(wo_split, b.in_group(1, 1))
                pe.wait_ge(y_split, b.count(1, 1))
            pe.wait_ge(out_added, b.count(QT, 1 + i))
            for j in range(CT):
                for n, (py, pw) in enumerate(THREE):
                    last = nc.tensor.matmul(banks[7][:], y_part[py][:, j, i * P:(i + 1) * P], wo[pw][:, j, :],
                                            start=(j == 0 and n == 0), stop=(j == CT - 1 and n == 2))
            last.then_inc(out_done, 1)

        def tensor_block(pe, b):
            for c in range(QT):
                chunk_start(pe, b, c)
                if not b.last:
                    for i in in_slot(c):
                        in_tile(pe, b.plus(1), i)
                chunk_end(pe, b, c)
                if not b.first:
                    out_tile(pe, b.plus(-1), c)

        def column(v, n, b, j=0):
            return v[:, n, ds(b.grp * CT + j, 1)] if v is par else v[:, n, ds(b.grp, 1)]

        def parts_of(v, i):
            if i != BC:
                return [(slice(0, P), v[:, i % 2, :, :])]
            return [(slice(0, 2 * NS), v[:, 0, :, 0:2 * NS]), (slice(2 * NS, 3 * NS), v[:, 0, :, NS:2 * NS]),
                    (slice(3 * NS, P), v[:, 0, :, NS:2 * NS])]

        def split_w_hi(act, b, i):
            per = 32 if i == BC else 16
            act.wait_ge(w_loaded[i], b.in_group(per, per))
            if not b.first:
                act.wait_ge(in_done, At(b.g, b.k // NQ * NQ).count(IN_TILES, i + 1 - IN_TILES))
            for where, src in parts_of(w_raw, i):
                last = nc.scalar.copy(w_grp[HI][:, i, :, where], src)
            last.then_inc(w_hi_made, 1)

        def take_in(act, b, i):
            act.wait_ge(in_done, b.count(IN_TILES, i + 1))
            src = banks[(b.k * IN_TILES + i) % 2]
            if i in (ZA, ZB):
                j = i - ZA
                if not b.first:
                    act.wait_ge(z_done, b.count(1))
                if not b.before(2):
                    act.wait_ge(v_ready, b.plus(-1).count(1))
                act.sem_inc(waited, 1)
                nc.scalar.activation(th_z[:, j, :], src[:], ACT.Tanh, bias=column(par, P_HBZ, b, j), scale=column(par, P_HMZ, b, j))
                nc.scalar.activation(z_c[:, b.par, j, :], src[:], ACT.Identity, bias=column(par, P_BZ, b, j),
                                     scale=column(par, P_MZ, b, j)).then_inc(in_taken, 1)
                return
            if i == BC:
                s, o = column(parb, Q_M, b), column(parb, Q_B, b)
                sl, ol = column(parb, Q_LM, b), column(parb, Q_LB, b)
                raw, conv = bc_raw, bc_c[:, b.par, :]
            else:
                s, o = column(par, P_MX, b, i - XA), column(par, P_BX, b, i - XA)
                sl, ol = column(par, P_LM, b, i - XA), column(par, P_LB, b, i - XA)
                raw, conv = x_raw[:, i - XA, :], x_c[:, b.par, i - XA, :]
            if not b.before(2):
                act.wait_ge(y_ready if i == BC else y_split, b.plus(-1).count(1))
            if not b.first:
                act.wait_ge(conv_done, b.plus(-1).count(3, i + 1))
                act.wait_ge(in_taken, b.plus(-1).count(IN_TILES, i + 1))
            act.sem_inc(waited, 1)
            nc.scalar.copy(raw[:, 0:PAD], raw[:, BLK:BLK + PAD] if b.half else no_steps[:]).then_inc(last_kept, 1)
            nc.scalar.activation(conv, src[:], ACT.Identity, bias=ol, scale=sl)
            act.wait_ge(last_kept, b.count(3, i + 1))
            act.sem_inc(waited, 1)
            nc.scalar.activation(raw[:, PAD:], src[:], ACT.Identity, bias=o, scale=s).then_inc(in_taken, 1)

        def tanh_conv(act, b, i):
            act.wait_ge(conv_done, b.count(3, i + 1))
            if not (b.first and i == 0):
                act.wait_ge(silu_done, b.count(3, i))
            src = bc_c[:, b.par, :] if i == BC else x_c[:, b.par, i - XA, :]
            nc.scalar.activation(th_x[:], src, ACT.Tanh, scale=0.5).then_inc(tanh_done, 1)

        def repeat_c(act, b):
            act.wait_ge(silu_done, b.count(3, 1))
            for h in range(2):
                last = nc.scalar.mul(c_rep[h * 2 * NS:(h + 1) * 2 * NS, b.par, :], bc_c[2 * NS:4 * NS, b.par, :], 0.5)
            last.then_inc(c_rep_made, 1)

        def repeat_da(act, b, c):
            if not (b.first and c < 2):
                act.wait_ge(turn_done, b.count(QT, c - 1))
            act.sem_inc(waited, 1)
            where = ds(b.grp * (NT * GH) + (b.tb * QT + c) * GH, GH)
            nc.scalar.copy(da_rep[:, c % 2, :, :, :], da[:, :, where].bitcast(F32)[:, :, :, None].to_broadcast([P, 2, GH, NS])
                           ).then_inc(da_rep_made, 1)

        def chunk_scalar(act, b, c):
            act.wait_ge(seg_done, b.count(QT, c + 1))
            if not (b.first and c == 0):
                act.wait_ge(weights_ready, b.count(QT, c))
                act.wait_ge(dec_ready, b.count(QT, c))
            nc.scalar.activation(decay[:, :, :].rearrange("p h t -> p (h t)"), banks[2][:], ACT.Exp).then_inc(decay_ready, 1)
            act.wait_ge(turn_done, b.count(QT, c + 1))
            if c >= 2 or not b.first:
                act.wait_ge(state_ready, b.count(QT, c - 1))
            nc.scalar.activation(e_cum[:, c % 2, :], banks[3][:, 0:P], ACT.Exp)
            nc.scalar.mul(x_tok[:], banks[3][:, P:P + GC + NS], 0.5).then_inc(tok_ready, 1)
            if not (b.last and c >= 2):
                repeat_da(act, b.plus((c + 2) // QT), (c + 2) % QT)

        def take_y(act, b):
            act.wait_ge(y_ready, b.count(1, 1))
            if not b.first:
                act.wait_ge(out_done, b.count(QT, 1))
            nc.scalar.copy(y_part[HI][:], x_c[:, b.par, :, :]).then_inc(y_hi_made, 1)
            nc.scalar.activation(z_c[:, b.par, :, :], x_c[:, b.par, :, :], ACT.Square).then_inc(sq_ready, 1)

        def split_wo_hi(act, b):
            act.wait_ge(wo_loaded, b.in_group(16, 16))
            if not b.first:
                act.wait_ge(out_done, b.count(QT, 1))
            act.sem_inc(waited, 1)
            for j in range(CT):
                last = nc.scalar.activation(wo[HI][:, j, :], wo_raw[:, j, :], ACT.Identity, scale=column(par, P_NW, b, j))
            last.then_inc(wo_hi_made, 1)

        def scalar_block(act, b):
            nx = b.plus(1)
            for c in range(QT):
                chunk_scalar(act, b, c)
                if c == 0 and not b.first:
                    take_y(act, b.plus(-1))
                if not b.last:
                    if c == 0:
                        take_in(act, nx, BC)
                        take_in(act, nx, XA)
                    elif c == 1:
                        tanh_conv(act, nx, BC)
                        take_in(act, nx, XB)
                    elif c == 2:
                        tanh_conv(act, nx, XA)
                        take_in(act, nx, ZA)
                        repeat_c(act, nx)
                    else:
                        tanh_conv(act, nx, XB)
                        take_in(act, nx, ZB)
                for i in split_slot(b, c):
                    split_w_hi(act, At(b.g, b.k // NQ * NQ + NQ), i)
            if b.tb == 0:
                split_wo_hi(act, b)

        def split_w_lo(dve, b, i):
            dve.wait_ge(w_hi_made, b.in_group(IN_TILES, i + 1))
            for where, src in parts_of(w_raw, i):
                last = nc.vector.tensor_tensor(w_grp[LO][:, i, :, where], src, w_grp[HI][:, i, :, where].bitcast(F32), ALU.subtract)
            last.then_inc(w_split, 1)

        def split_wo_lo(dve, b):
            dve.wait_ge(wo_hi_made, b.in_group(1, 1))
            dve.sem_inc(waited, 1)
            for j in range(CT):
                last = nc.vector.scalar_tensor_tensor(wo[LO][:, j, :], wo_raw[:, j, :], column(par, P_NW, b, j),
                                                      wo[HI][:, j, :].bitcast(F32), ALU.mult, ALU.subtract)
            last.then_inc(wo_split, 1)

        def split_y_lo(dve, b):
            dve.wait_ge(y_hi_made, b.count(1, 1))
            nc.vector.tensor_tensor(y_part[LO][:], x_c[:, b.par, :, :], y_part[HI][:].bitcast(F32), ALU.subtract).then_inc(y_split, 1)

        def convolve(dve, st, b, i):
            dve.wait_ge(in_taken, b.count(IN_TILES, i + 1))
            if i == BC:
                src, dst = bc_raw, bc_c[:, b.par, :]
                w = [column(parb, Q_TAP + k, b) for k in range(PAD)]
            else:
                j = i - XA
                src, dst = x_raw[:, j, :], x_c[:, b.par, j, :]
                w = [column(par, P_TAP + k, b, j) for k in range(PAD)]
            for k in range(PAD):
                ins = nc.vector.scalar_tensor_tensor(dst, src[:, k:k + BLK], w[k], dst, ALU.mult, ALU.add)
                if k < PAD - 1:
                    st.then(ins)
            ins.then_inc(conv_done, 1)

        def silu(dve, b, i):
            dve.wait_ge(tanh_done, b.count(3, i + 1))
            v = bc_c[:, b.par, :] if i == BC else x_c[:, b.par, i - XA, :]
            nc.vector.scalar_tensor_tensor(v, th_x[:], 1.0, v, ALU.add, ALU.mult).then_inc(silu_done, 1)

        def gate_z(dve, b):
            dve.wait_ge(in_taken, b.count(IN_TILES, IN_TILES))
            nc.vector.scalar_tensor_tensor(z_c[:, b.par, :, :], th_z[:], 1.0, z_c[:, b.par, :, :], ALU.add, ALU.mult).then_inc(z_done, 1)

        def chunk_weights(dve, st, b, c):
            dt_c = dt_blk[:, b.par, c * GH:(c + 1) * GH]
            dve.wait_ge(g_done, b.count(QT, c + 1))
            st.then(nc.vector.tensor_tensor(g_m[:], banks[4][:, 0:P], le_half[:], ALU.mult))
            if c == 0:
                dve.wait_ge(dt_blk_made, b.count(1, 1))
            dve.wait_ge(decay_ready, b.count(QT, c + 1))
            for h in range(GH):
                last = nc.vector.scalar_tensor_tensor(wts[:, h, :], decay[:, h, :], dt_c[:, h:h + 1], g_m[:], ALU.mult, ALU.mult)
            last.then_inc(weights_ready, 1)

        def mean_square(dve):
            nc.vector.tensor_scalar(v_grp[:], banks[4][:, P + GC:P + GC + QT], 0.25 / GC, EPS, ALU.mult, ALU.add).then_inc(v_ready, 1)

        def chunk_state(dve, st, b, c):
            fresh = b.half == 0 and c == 0
            dve.wait_ge(chunk_done, b.count(QT, c + 1))
            if c == 0 and not b.first:
                mean_square(dve)
            if fresh:
                ins = nc.vector.tensor_copy(state[:], banks[4][:, P:P + GC])
            else:
                ins = nc.vector.scalar_tensor_tensor(state[:], state[:], e_cum[:, c % 2, P - 1:P], banks[4][:, P:P + GC],
                                                     ALU.mult, ALU.add)
            ins.then_inc(state_ready, 1)

        def add_out(dve, b, i):
            dve.wait_ge(out_done, b.count(QT, 1 + i + 1))
            if i == 0:
                dve.wait_ge(rs_ready, b.count(1, 1))
            row = xres[:, b.tb * QT + i, :]
            nc.vector.scalar_tensor_tensor(row, banks[7][:], rs_grp[:, i:i + 1], row, ALU.mult, ALU.add).then_inc(out_added, 1)

        def finish_y(dve, st, b):
            for j in range(CT):
                st.did(nc.vector.scalar_tensor_tensor(x_c[:, b.par, j, :], x_c[:, b.par, j, :], column(par, P_D, b, j), banks[5 + j][:],
                                                      ALU.mult, ALU.add))
            st.wait()
            dve.wait_ge(z_done, b.count(1, 1))
            nc.vector.tensor_tensor(x_c[:, b.par, :, :], x_c[:, b.par, :, :], z_c[:, b.par, :, :], ALU.mult).then_inc(y_ready, 1)

        def vector_block(dve, st, b):
            nx = b.plus(1)
            for c in range(QT):
                chunk_weights(dve, st, b, c)
                if c == 0:
                    if not b.first:
                        split_y_lo(dve, b.plus(-1))
                    gate_z(dve, b)
                if c in (1, 2) and not b.last:
                    convolve(dve, st, nx, (XA, XB)[c - 1])
                if c == QT - 1 and not b.last:
                    silu(dve, nx, XB)
                chunk_state(dve, st, b, c)
                if c in (1, 2) and not b.last:
                    silu(dve, nx, (BC, XA)[c - 1])
                if c == 0 and not b.last:
                    convolve(dve, st, nx, BC)
                if not b.first:
                    add_out(dve, b.plus(-1), c)
                for i in split_slot(b, c):
                    split_w_lo(dve, At(b.g, b.k // NQ * NQ + NQ), i)
            finish_y(dve, st, b)
            if b.tb == 0:
                split_wo_lo(dve, b)

        def pool_dt(pool, b):
            if not b.before(2):
                pool.wait_ge(weights_ready, b.plus(-1).count(QT))
            pool.sem_inc(waited, 1)
            nc.gpsimd.tensor_copy(dt_blk[:, b.par, :], dt_all[:, ds(b.grp * (NT * GH) + b.tb * QT * GH, QT * GH)]
                                  ).then_inc(dt_blk_made, 1)

        def pool_segments(pool, b, c):
            if not (b.first and c < 2):
                pool.wait_ge(seg_done, b.count(QT, c - 1))
            pool.sem_inc(waited, 1)
            where = ds(b.grp * (NT * GH) + (b.tb * QT + c) * GH, GH)
            nc.gpsimd.tensor_tensor(r_seg[:, c % 2, :, :, :], da[:, :, where].bitcast(F32)[:, :, :, None].to_broadcast([P, 2, GH, P]),
                                    le[:, None, None, :].to_broadcast([P, 2, GH, P]), ALU.mult).then_inc(r_made, 1)

        def pool_decays(pool, st, b, c):
            if c == 0:
                pool.wait_ge(dt_blk_made, b.count(1, 1))
                pool.wait_ge(c_rep_made, b.count(1, 1))
            pool.wait_ge(decay_ready, b.count(QT, c + 1))
            st.did(nc.gpsimd.tensor_tensor(w_dec[:], decay[:, :, P - 1], dt_blk[:, b.par, c * GH:(c + 1) * GH], ALU.mult))
            if not (b.first and c == 0):
                pool.wait_ge(chunk_done, b.count(QT, c))
            pool.wait_ge(tok_ready, b.count(QT, c + 1))
            st.wait()
            last = nc.gpsimd.tensor_tensor(b_dec[:], x_tok[:, None, GC:GC + NS].to_broadcast([P, GH, NS]),
                                           w_dec[:, :, None].to_broadcast([P, GH, NS]), ALU.mult)
            if not (b.half == 0 and c == 0):
                last = nc.gpsimd.tensor_tensor(c_dec[:], c_rep[:, b.par, c * P:(c + 1) * P], e_cum[:, c % 2, :], ALU.mult)
            last.then_inc(dec_ready, 1)

        def add_squares(pool, b):
            assert CT == 2
            pool.wait_ge(sq_ready, b.count(1, 1))
            nc.gpsimd.tensor_tensor(z_c[:, b.par, 0, :], z_c[:, b.par, 0, :], z_c[:, b.par, 1, :], ALU.add).then_inc(sq_added, 1)

        def pool_block(pool, st, b):
            for c in range(QT):
                pool_decays(pool, st, b, c)
                if c == 0 and not b.first:
                    add_squares(pool, b.plus(-1))
                nx = b.plus((c + 2) // QT)
                if not (b.last and c >= 2):
                    pool_segments(pool, nx, (c + 2) % QT)
                if c == 0 and not b.first:
                    pool.wait_ge(v_ready, b.count(1))
                    nc.gpsimd.tensor_tensor(rs_grp[:], v_grp[:], minus_half[:, 0:QT], ALU.pow).then_inc(rs_ready, 1)
                if c == 2 and not b.last:
                    pool_dt(pool, nx)

        def load_group(sp, g):
            for i in range(IN_TILES):
                if i >= 2:
                    sp.wait_ge(w_split, g * IN_TILES + (i - 1))
                elif not isinstance(g, int):
                    sp.wait_ge(wo_split, g)
                if not isinstance(g, int):
                    sp.sem_inc(waited, 1)
                if i == BC:
                    sp.dma_start(w_raw[:, 0, :, 0:NS], w_in_rows[:, :, ds(g * NS + B0, NS)]).then_inc(w_loaded[i], 16)
                    sp.dma_start(w_raw[:, 0, :, NS:2 * NS], w_in_rows[:, :, ds(g * NS + C0, NS)]).then_inc(w_loaded[i], 16)
                else:
                    base = X0 + (i - XA) * P if i in (XA, XB) else (i - ZA) * P
                    sp.dma_start(w_raw[:, i % 2, :, :], w_in_rows[:, :, ds(g * GC + base, P)]).then_inc(w_loaded[i], 16)
            sp.wait_ge(w_split, g * IN_TILES + IN_TILES)
            if not isinstance(g, int):
                sp.sem_inc(waited, 1)
            sp.dma_start(wo_raw, w_out_rows[ds(g, 1), :, :, :].rearrange("a p c n -> p (a c) n")).then_inc(wo_loaded, 16)

        block2 = nc.Block()
        block2.__enter__()

        @block2.sync
        def _(sp):
            sp.dma_start(w_dt_raw, w_in_rows[:, :, DT0:DT0 + NH]).then_inc(dtw_in, 16)
            sp.dma_start(b_out_all[:], b_out.partition_broadcast(P)).then_inc(dtw_in, 16)
            for n, v in enumerate((b_in[DT0:DT0 + NH], mup[DT0:DT0 + NH], dt_bias, a_log)):
                sp.dma_start(dt_vec[:, n, :], v.partition_broadcast(P)).then_inc(dtw_in, 16)
            load_group(sp, 0)
            with sp.Fori(1, NG) as g:
                load_group(sp, g)

        @block2.scalar
        def _(act):
            b = At(0, 0)

            def take_dt(q):
                act.wait_ge(dt_done, q + 1)
                nc.scalar.copy(dt_T[q], banks[4 + q][0:NH, :]).then_inc(dt_taken, 1)

            for t in range(NT):
                act.wait_ge(mid.turned, t + 1)
                nc.scalar.copy(xn[HI][:, :, t * P:(t + 1) * P], banks[t % QT][:].rearrange("p (k t) -> p k t", k=KD)
                               ).then_inc(mid.xt_ready, 1)
                if t == QT - 1:
                    act.wait_ge(dtw_in, 16 * 6)
                    act.wait_ge(w_dt_cleared, 2)
                    nc.scalar.copy(w_dt[HI][:, :, 0:NH], w_dt_raw).then_inc(w_dt_hi, 1)
                    for i in (BC, XA):
                        split_w_hi(act, b, i)
                elif t % QT == QT - 1:
                    take_dt(t // QT - 1)
                if t == 3 * QT - 1:
                    for i in (XB, ZA):
                        split_w_hi(act, b, i)
            take_dt(NQ - 1)
            split_w_hi(act, b, ZB)
            take_in(act, b, BC)
            act.wait_ge(soft_in, 1)
            nc.scalar.activation(dt_vec[:, 0, :], dt_vec[:, 3, :], ACT.Exp).then_inc(a_exp, 1)
            nc.scalar.activation(sp_c, sp_b, ACT.Exp, scale=-1.0).then_inc(soft_exp, 1)
            act.wait_ge(soft_exp, 1)
            nc.scalar.activation(sp_b, sp_c, ACT.Ln, bias=1.0).then_inc(soft_ln, 1)
            take_in(act, b, XA)
            act.wait_ge(b_out_added, NT)
            tanh_conv(act, b, BC)
            take_in(act, b, XB)
            repeat_c(act, b)
            tanh_conv(act, b, XA)
            act.wait_ge(dt_ready, 1)
            take_in(act, b, ZA)
            tanh_conv(act, b, XB)
            take_in(act, b, ZB)
            repeat_da(act, b, 0)
            repeat_da(act, b, 1)
            scalar_block(act, b)
            with act.Fori(0, NG - 1) as g:
                for k in range(1, NQ + 1):
                    scalar_block(act, At(g, k))
            for k in range(1, NQ):
                scalar_block(act, At(NG - 1, k))
            take_y(act, At(NG - 1, NQ - 1))

        @block2.vector
        def _(dve):
            st = Steps(dve, s_mix)
            dve.sem_inc(out_added, 1)
            st.did(nc.vector.memset(no_steps[:], 0.0))
            st.did(nc.vector.tensor_scalar(gt_r[:], le[:], -1.0, 1.0, ALU.mult, ALU.add))
            st.did(nc.vector.tensor_copy(le_r[:], le[:]))

            def norm_lo(q):
                for t in range(q * QT, (q + 1) * QT):
                    dve.wait_ge(mid.xt_ready, t + 1)
                    where = slice(t * P, (t + 1) * P)
                    nc.vector.tensor_tensor(xn[LO][:, :, where], banks[t % QT][:].rearrange("p (k t) -> p k t", k=KD),
                                            xn[HI][:, :, where].bitcast(F32), ALU.subtract).then_inc(mid.xt_used, 1)

            b = At(0, 0)
            for q in range(NQ):
                norm_apply(dve, mid, q)
                if q:
                    norm_lo(q - 1)
                    if q == 1:
                        dve.wait_ge(w_dt_hi, 1)
                        nc.vector.tensor_tensor(w_dt[LO][:, :, 0:NH], w_dt_raw, w_dt[HI][:, :, 0:NH].bitcast(F32), ALU.subtract
                                                ).then_inc(w_dt_split, 1)
                        for i in (BC, XA):
                            split_w_lo(dve, b, i)
            norm_lo(NQ - 1)
            for i in (XB, ZA):
                split_w_lo(dve, b, i)

            def by_head(v):
                return v.rearrange("p (g h) -> p g h", g=NG)[:, :, None, :].to_broadcast([P, NG, NT, GH])

            def wide(v):
                return v.rearrange("p (g t h) -> p g t h", g=NG, h=GH)

            dve.wait_ge(dtw_in, 16 * 6)
            dve.wait_ge(dt_turned, 1)
            st.then(nc.vector.tensor_tensor(wide(sp_a), banks[4][:].rearrange("p (t g h) -> p g t h", t=NT, g=NG),
                                            by_head(dt_vec[:, 0, :]), ALU.add))
            nc.vector.memset(banks[4][:, P:P + GC], 0.0).then_inc(bank4_cleared, 1)
            st.then(nc.vector.tensor_tensor(wide(sp_a), wide(sp_a), by_head(dt_vec[:, 1, :]), ALU.mult))
            st.then(nc.vector.tensor_tensor(wide(sp_a), wide(sp_a), by_head(dt_vec[:, 2, :]), ALU.add))
            nc.vector.scalar_tensor_tensor(sp_b, sp_a, -1.0, sp_a, ALU.mult, ALU.max).then_inc(soft_in, 1)
            split_w_lo(dve, b, ZB)
            dve.wait_ge(soft_exp, 1)
            st.then(nc.vector.tensor_scalar(sp_d, sp_c, -0.25, 1.0 / 3.0, ALU.mult, ALU.add))
            st.then(nc.vector.tensor_tensor(sp_d, sp_d, sp_c, ALU.mult))
            st.then(nc.vector.scalar_tensor_tensor(sp_d, sp_d, -0.5, sp_c, ALU.add, ALU.mult))
            st.then(nc.vector.scalar_tensor_tensor(sp_d, sp_d, 1.0, sp_c, ALU.add, ALU.mult))
            dve.wait_ge(soft_ln, 1)
            st.then(nc.vector.tensor_tensor(sp_d, sp_d, sp_b, ALU.subtract))
            st.then(nc.vector.scalar_tensor_tensor(sp_d, sp_c, 2.0 ** -5, sp_d, ALU.is_lt, ALU.mult))
            st.then(nc.vector.tensor_tensor(sp_d, sp_d, sp_b, ALU.add))
            st.then(nc.vector.scalar_tensor_tensor(dt_all[:], sp_a, 0.0, sp_d, ALU.max, ALU.add))
            dve.wait_ge(a_exp, 1)
            st.then(nc.vector.tensor_tensor(wide(sp_b), wide(dt_all[:, :]), by_head(dt_vec[:, 0, :]), ALU.mult))
            st.then(nc.vector.tensor_scalar(sp_b, sp_b, -1.0, None, ALU.mult))
            st.then(nc.vector.tensor_copy(da[:, HI, :], sp_b))
            nc.vector.tensor_tensor(da[:, LO, :], sp_b, da[:, HI, :].bitcast(F32), ALU.subtract).then_inc(dt_ready, 1)
            for i in (BC, XA, XB):
                convolve(dve, st, b, i)
                silu(dve, b, i)
            vector_block(dve, st, b)
            with dve.Fori(0, NG - 1) as g:
                st.enter(g, 0, STEPS_PER_GROUP)
                for k in range(1, NQ + 1):
                    vector_block(dve, st, At(g, k))
                st.leave(NG - 1)
            for k in range(1, NQ):
                vector_block(dve, st, At(NG - 1, k))
            b = At(NG - 1, NQ - 1)
            split_y_lo(dve, b)
            dve.wait_ge(chunk_done, BLOCKS * QT + 1)
            mean_square(dve)
            for i in range(QT):
                add_out(dve, b, i)

        @block2.gpsimd
        def _(pool):
            for q in range(NQ):
                block = slice(q * QT, (q + 1) * QT)
                nc.gpsimd.tensor_tensor(rstd[:, block], var_eps[:, block], minus_half[:, 0:QT], ALU.pow).then_inc(mid.rstd_ready, 1)
            for p in (HI, LO):
                nc.gpsimd.memset(w_grp[p][:, ZB, :, :].bitcast(F32), 0.0).then_inc(w_dt_cleared, 1)
            pool.wait_ge(dtw_in, 16 * 6)
            for t in range(NT):
                pool.wait_ge(mid.xn_ready, t + 1)
                nc.gpsimd.tensor_tensor(xres[:, t, :], xres[:, t, :], b_out_all[:], ALU.add).then_inc(b_out_added, 1)
            st = Steps(pool, pool_step)
            pool.wait_ge(dt_ready, 1)
            b = At(0, 0)
            pool_dt(pool, b)
            pool_segments(pool, b, 0)
            pool_segments(pool, b, 1)
            pool_block(pool, st, b)
            with pool.Fori(0, NG - 1) as g:
                st.enter(g, 0, POOL_STEPS_PER_GROUP)
                for k in range(1, NQ + 1):
                    pool_block(pool, st, At(g, k))
                st.leave(NG - 1)
            for k in range(1, NQ):
                pool_block(pool, st, At(NG - 1, k))
            add_squares(pool, At(NG - 1, NQ - 1))
            pool.wait_ge(v_ready, BLOCKS)
            nc.gpsimd.tensor_tensor(rs_grp[:], v_grp[:], minus_half[:, 0:QT], ALU.pow).then_inc(rs_ready, 1)

        @block2.tensor
        def _(pe):
            pe.sem_inc(out_done, 1)

            def dt_products(q):
                pe.wait_ge(w_dt_split, 1)
                pe.wait_ge(mid.xt_used, (q + 1) * QT)
                for k in range(KD):
                    for n, (pw, px) in enumerate(THREE):
                        last = nc.tensor.matmul(banks[4 + q][:], w_dt[pw][:, k, :], xn[px][:, k, q * BLK:(q + 1) * BLK],
                                                start=(k == 0 and n == 0), stop=(k == KD - 1 and n == 2))
                last.then_inc(dt_done, 1)

            for q in range(NQ):
                for t in range(q * QT, (q + 1) * QT):
                    norm_turn(pe, mid, t)
                if q:
                    dt_products(q - 1)
            dt_products(NQ - 1)
            for t in range(NT):
                pe.wait_ge(dt_taken, t // QT + 1)
                last = nc.tensor.transpose(banks[4][:, t * NH:(t + 1) * NH], dt_T[t // QT][:, (t % QT) * P:(t % QT + 1) * P],
                                           ident[0:NH, 0:NH])
            last.then_inc(dt_turned, 1)
            b = At(0, 0)
            for i in range(IN_TILES):
                in_tile(pe, b, i)
            pe.wait_ge(bank4_cleared, 1)
            tensor_block(pe, b)
            with pe.Fori(0, NG - 1) as g:
                for k in range(1, NQ + 1):
                    tensor_block(pe, At(g, k))
            for k in range(1, NQ):
                tensor_block(pe, At(NG - 1, k))
            b = At(NG - 1, NQ - 1)
            pe.wait_ge(state_ready, BLOCKS * QT)
            sum_squares(pe, b).then_inc(chunk_done, 1)
            for i in range(QT):
                out_tile(pe, b, i)

        block2.__exit__(None, None, None)
        phase.close()

        phase = ExitStack()
        mixes[1].allocate(phase)
        block3 = nc.Block()
        block3.__enter__()

        @block3.sync
        def _(sp):
            mix_sync(sp, mixes[1], True)

        @block3.scalar
        def _(act):
            mix_scalar(act, mixes[1])

        @block3.gpsimd
        def _(pool):
            mix_pool(pool, mixes[1])
            for t in range(NT):
                pick_pool(pool, mixes[1], t)

        @block3.vector
        def _(dve):
            st = Steps(dve, s_last)
            mix_vector(dve, st, mixes[1], lambda q: None)
            with dve.Fori(0, NQ) as q:
                st.enter(q, 0, QT)
                for i in range(QT):
                    pick_vector(dve, st, mixes[1], q, i)
                st.leave(NQ)

        @block3.tensor
        def _(pe):
            mix_tensor(pe, mixes[1])

        block3.__exit__(None, None, None)
        phase.close()


_INS = ["L0_attn_hidden_states", "L0_attn_W_in", "L0_attn_b_in", "L0_attn_conv_w", "L0_attn_conv_b", "L0_attn_A_log",
        "L0_attn_D_param", "L0_attn_dt_bias", "L0_attn_norm_w", "L0_attn_W_out", "L0_attn_b_out", "L0_attn_mup_vector",
        "L0_ffn_gate_w", "L0_ffn_expert_w", "L0_ffn_expert_b"]


def kernel(**inputs):
    import numpy as _np
    import concourse.bacc as _bacc
    from concourse import mybir as _mybir
    from concourse.bass_utils import run_bass_kernel_spmd as _run

    nc = _bacc.Bacc("TRN2", target_bir_lowering=False, num_devices=1)
    arrays, args = {}, []
    for name in _INS:
        a = _np.ascontiguousarray(inputs[name])
        arrays[f"in_{name}_dram"] = a
        args.append(nc.dram_tensor(f"in_{name}_dram", a.shape, _mybir.dt.from_np(a.dtype), kind="ExternalInput").ap())
    out = nc.dram_tensor("out_0_dram", inputs["L0_attn_hidden_states"].shape, _mybir.dt.float32, kind="ExternalOutput").ap()
    build(nc, *args, out)
    r = _run(nc, [arrays], core_ids=[0])
    return r.results[0]["out_0_dram"]
```
